# Optimizing a Trainium2 kernel written in Bass

```python
import numpy as np
import jax
import jax.numpy as jnp

def _softmax(x, axis=-1):
    return jax.nn.softmax(x, axis=axis)

def _gelu(x):
    return jax.nn.gelu(x, approximate=True)

def _silu(x):
    return jax.nn.silu(x)

def _sigmoid(x):
    return jax.nn.sigmoid(x)

def _layernorm(x, axis=-1, eps=1e-05):
    m = jnp.mean(x, axis=axis, keepdims=True)
    v = jnp.var(x, axis=axis, keepdims=True)
    return (x - m) / jnp.sqrt(v + eps)

def _scatter_add(tgt, idx, src, axis=0):
    return tgt.at[idx].add(src)

def _segment_sum(src, seg, n):
    return jax.ops.segment_sum(src, seg, n)
kernel_name = 'mk_sandwich_d1_jaxref_r4_c56d38'

def setup_inputs(seed: int=0):
    np.random.seed(seed)
    _w = jnp.asarray

    def _L0_attn_setup():
        import jax, jax.numpy as jnp
        import numpy as np
        import math
        EPS = 1e-05
        K = 4
        N = 16

        def _causal_depthwise_conv(x, w, b):
            c = x.shape[-1]
            y = jax.lax.conv_general_dilated(x, w, window_strides=(1,), padding=[(K - 1, 0)], dimension_numbers=('NWC', 'WIO', 'NWC'), feature_group_count=c)
            return y + b
        key = jax.random.key(seed)
        b, l, d = (1, 512, 256)
        di = 2 * d
        dt_rank = math.ceil(d / 16)
        ks = jax.random.split(key, 8)
        s = 0.02
        return {'x': jax.random.normal(ks[0], (b, l, d), jnp.float32), 'norm_scale': jnp.ones((d,), jnp.float32), 'w_in': jax.random.normal(ks[1], (d, 4 * d), jnp.float32) * s, 'conv_w': jax.random.normal(ks[2], (K, 1, di), jnp.float32) * 0.2, 'conv_b': jnp.zeros((di,), jnp.float32), 'A_log': jax.random.normal(ks[3], (di, N), jnp.float32) * 0.5, 'D': jax.random.normal(ks[4], (di,), jnp.float32) * 0.1, 'w_xproj': jax.random.normal(ks[5], (di, dt_rank + 2 * N), jnp.float32) * s, 'w_dt': jax.random.normal(ks[6], (dt_rank, di), jnp.float32) * s, 'b_dt': jnp.zeros((di,), jnp.float32), 'w_out': jax.random.normal(ks[7], (di, d), jnp.float32) * s}
    _L0_attn_in = _L0_attn_setup()

    def _L0_ffn_setup():
        import jax, jax.numpy as jnp
        import numpy as np
        B, T, D, R, KEXP = (4, 1024, 256, 64, 8)
        RH = max(D, 32)
        SCALE = 0.02

        def _fused_branch(Q_side, K_side, V, W, U, b, router_w1, router_b1, router_w2, router_b2, expert_bias):
            xV = jnp.einsum('btd,kdr->btkr', Q_side, V)
            yW = jnp.einsum('btd,kdr->btkr', K_side, W)
            cum_yW = jnp.cumsum(yW, axis=1)
            prod = xV * cum_yW
            h = jax.nn.gelu(Q_side @ router_w1.T + router_b1, approximate=False)
            logits = h @ router_w2.T + router_b2 + expert_bias
            weights = jax.nn.softmax(logits, axis=-1)
            out = jnp.einsum('btkr,kdr->btd', prod * weights[..., None], U)
            out = out + weights @ b
            n_valid = jnp.arange(1, Q_side.shape[1] + 1, dtype=Q_side.dtype)
            return out / n_valid[None, :, None]
        key = jax.random.key(seed)
        ks = jax.random.split(key, 20)
        x = jax.random.normal(ks[0], (B, T, D), dtype=jnp.float32)
        W_Q = jax.random.normal(ks[1], (D, D), dtype=jnp.float32) * (1.0 / np.sqrt(D))
        W_K = jax.random.normal(ks[2], (D, D), dtype=jnp.float32) * (1.0 / np.sqrt(D))
        W_O = jax.random.normal(ks[3], (D, D), dtype=jnp.float32) * (1.0 / np.sqrt(D))
        W_inv = jnp.eye(D, dtype=jnp.float32) + 0.01 * jax.random.normal(ks[4], (D, D), dtype=jnp.float32)
        V_fwd = jax.random.normal(ks[5], (KEXP, D, R), dtype=jnp.float32) * SCALE
        W_fwd = jax.random.normal(ks[6], (KEXP, D, R), dtype=jnp.float32) * SCALE
        U_fwd = jax.random.normal(ks[7], (KEXP, D, R), dtype=jnp.float32) * SCALE
        b_fwd = jnp.zeros((KEXP, D), dtype=jnp.float32)
        V_inv = jax.random.normal(ks[8], (KEXP, D, R), dtype=jnp.float32) * SCALE
        W_inv_exp = jax.random.normal(ks[9], (KEXP, D, R), dtype=jnp.float32) * SCALE
        U_inv = jax.random.normal(ks[10], (KEXP, D, R), dtype=jnp.float32) * SCALE
        b_inv = jnp.zeros((KEXP, D), dtype=jnp.float32)
        router_w1 = jax.random.normal(ks[11], (RH, D), dtype=jnp.float32) * (1.0 / np.sqrt(D))
        router_b1 = jnp.zeros((RH,), dtype=jnp.float32)
        router_w2 = jax.random.normal(ks[12], (KEXP, RH), dtype=jnp.float32) * (1.0 / np.sqrt(RH))
        router_b2 = jnp.zeros((KEXP,), dtype=jnp.float32)
        alpha_bi = jnp.asarray(0.5, dtype=jnp.float32)
        expert_bias = jnp.zeros((KEXP,), dtype=jnp.float32)
        return dict(x=x, W_Q=W_Q, W_K=W_K, W_O=W_O, W_inv=W_inv, V_fwd=V_fwd, W_fwd=W_fwd, U_fwd=U_fwd, b_fwd=b_fwd, V_inv=V_inv, W_inv_exp=W_inv_exp, U_inv=U_inv, b_inv=b_inv, router_w1=router_w1, router_b1=router_b1, router_w2=router_w2, router_b2=router_b2, alpha_bi=alpha_bi, expert_bias=expert_bias)
    _L0_ffn_in = _L0_ffn_setup()
    _d = {'L0_attn_x': _L0_attn_in['x'], 'L0_attn_norm_scale': _L0_attn_in['norm_scale'], 'L0_attn_w_in': _L0_attn_in['w_in'], 'L0_attn_conv_w': _L0_attn_in['conv_w'], 'L0_attn_conv_b': _L0_attn_in['conv_b'], 'L0_attn_A_log': _L0_attn_in['A_log'], 'L0_attn_D': _L0_attn_in['D'], 'L0_attn_w_xproj': _L0_attn_in['w_xproj'], 'L0_attn_w_dt': _L0_attn_in['w_dt'], 'L0_attn_b_dt': _L0_attn_in['b_dt'], 'L0_attn_w_out': _L0_attn_in['w_out'], 'L0_ffn_W_Q': _L0_ffn_in['W_Q'], 'L0_ffn_W_K': _L0_ffn_in['W_K'], 'L0_ffn_W_O': _L0_ffn_in['W_O'], 'L0_ffn_W_inv': _L0_ffn_in['W_inv'], 'L0_ffn_V_fwd': _L0_ffn_in['V_fwd'], 'L0_ffn_W_fwd': _L0_ffn_in['W_fwd'], 'L0_ffn_U_fwd': _L0_ffn_in['U_fwd'], 'L0_ffn_b_fwd': _L0_ffn_in['b_fwd'], 'L0_ffn_V_inv': _L0_ffn_in['V_inv'], 'L0_ffn_W_inv_exp': _L0_ffn_in['W_inv_exp'], 'L0_ffn_U_inv': _L0_ffn_in['U_inv'], 'L0_ffn_b_inv': _L0_ffn_in['b_inv'], 'L0_ffn_router_w1': _L0_ffn_in['router_w1'], 'L0_ffn_router_b1': _L0_ffn_in['router_b1'], 'L0_ffn_router_w2': _L0_ffn_in['router_w2'], 'L0_ffn_router_b2': _L0_ffn_in['router_b2'], 'L0_ffn_alpha_bi': _L0_ffn_in['alpha_bi'], 'L0_ffn_expert_bias': _L0_ffn_in['expert_bias']}
    _x0 = _d['L0_attn_x']
    _d['L0_attn_x'] = jax.random.normal(jax.random.fold_in(jax.random.key(seed), 1), (16, 512, 256), dtype=_x0.dtype)
    del _x0
    return _d

def reference(L0_attn_x, L0_attn_norm_scale, L0_attn_w_in, L0_attn_conv_w, L0_attn_conv_b, L0_attn_A_log, L0_attn_D, L0_attn_w_xproj, L0_attn_w_dt, L0_attn_b_dt, L0_attn_w_out, L0_ffn_W_Q, L0_ffn_W_K, L0_ffn_W_O, L0_ffn_W_inv, L0_ffn_V_fwd, L0_ffn_W_fwd, L0_ffn_U_fwd, L0_ffn_b_fwd, L0_ffn_V_inv, L0_ffn_W_inv_exp, L0_ffn_U_inv, L0_ffn_b_inv, L0_ffn_router_w1, L0_ffn_router_b1, L0_ffn_router_w2, L0_ffn_router_b2, L0_ffn_alpha_bi, L0_ffn_expert_bias):

    def _L0_attn_ref(x, norm_scale, w_in, conv_w, conv_b, A_log, D, w_xproj, w_dt, b_dt, w_out):
        import jax, jax.numpy as jnp
        import numpy as np
        import math
        EPS = 1e-05
        K = 4
        N = 16

        def _causal_depthwise_conv(x, w, b):
            c = x.shape[-1]
            y = jax.lax.conv_general_dilated(x, w, window_strides=(1,), padding=[(K - 1, 0)], dimension_numbers=('NWC', 'WIO', 'NWC'), feature_group_count=c)
            return y + b
        dt_rank = w_dt.shape[0]
        h = x * jax.lax.rsqrt(jnp.mean(x * x, axis=-1, keepdims=True) + EPS) * norm_scale
        h = h @ w_in
        xs, res = jnp.split(h, 2, axis=-1)
        res = jax.nn.silu(res)
        xs = jax.nn.silu(_causal_depthwise_conv(xs, conv_w, conv_b))
        proj = xs @ w_xproj
        delta, B, C = jnp.split(proj, [dt_rank, dt_rank + N], axis=-1)
        delta = jax.nn.softplus(delta @ w_dt + b_dt)
        A = -jnp.exp(A_log)
        deltaA = jnp.exp(delta[..., None] * A)
        deltaBx = (delta * xs)[..., None] * B[:, :, None, :]

        def combine(e_i, e_j):
            a_i, b_i = e_i
            a_j, b_j = e_j
            return (a_i * a_j, a_j * b_i + b_j)
        _, ys = jax.lax.associative_scan(combine, (deltaA, deltaBx), axis=1)
        y = jnp.einsum('blcn,bln->blc', ys, C)
        out = (y + xs * D) * res
        return x + out @ w_out

    def _L0_ffn_ref(x, W_Q, W_K, W_O, W_inv, V_fwd, W_fwd, U_fwd, b_fwd, V_inv, W_inv_exp, U_inv, b_inv, router_w1, router_b1, router_w2, router_b2, alpha_bi, expert_bias):
        import jax, jax.numpy as jnp
        import numpy as np
        B, T, D, R, KEXP = (4, 1024, 256, 64, 8)
        RH = max(D, 32)
        SCALE = 0.02

        def _fused_branch(Q_side, K_side, V, W, U, b, router_w1, router_b1, router_w2, router_b2, expert_bias):
            xV = jnp.einsum('btd,kdr->btkr', Q_side, V)
            yW = jnp.einsum('btd,kdr->btkr', K_side, W)
            cum_yW = jnp.cumsum(yW, axis=1)
            prod = xV * cum_yW
            h = jax.nn.gelu(Q_side @ router_w1.T + router_b1, approximate=False)
            logits = h @ router_w2.T + router_b2 + expert_bias
            weights = jax.nn.softmax(logits, axis=-1)
            out = jnp.einsum('btkr,kdr->btd', prod * weights[..., None], U)
            out = out + weights @ b
            n_valid = jnp.arange(1, Q_side.shape[1] + 1, dtype=Q_side.dtype)
            return out / n_valid[None, :, None]
        Q = x @ W_Q.T
        K = x @ W_K.T
        invQ = Q @ W_inv.T
        invK = K @ W_inv.T
        fwd = _fused_branch(Q, K, V_fwd, W_fwd, U_fwd, b_fwd, router_w1, router_b1, router_w2, router_b2, expert_bias)
        inv = _fused_branch(invQ, invK, W_inv_exp, V_inv, U_inv, b_inv, router_w1, router_b1, router_w2, router_b2, expert_bias)
        out = fwd + alpha_bi * inv
        return out @ W_O.T
    x = L0_attn_x
    x = x + _layernorm(_L0_attn_ref(_layernorm(x, axis=-1), L0_attn_norm_scale, L0_attn_w_in, L0_attn_conv_w, L0_attn_conv_b, L0_attn_A_log, L0_attn_D, L0_attn_w_xproj, L0_attn_w_dt, L0_attn_b_dt, L0_attn_w_out), axis=-1)
    x = x + _layernorm(_L0_ffn_ref(_layernorm(x, axis=-1), L0_ffn_W_Q, L0_ffn_W_K, L0_ffn_W_O, L0_ffn_W_inv, L0_ffn_V_fwd, L0_ffn_W_fwd, L0_ffn_U_fwd, L0_ffn_b_fwd, L0_ffn_V_inv, L0_ffn_W_inv_exp, L0_ffn_U_inv, L0_ffn_b_inv, L0_ffn_router_w1, L0_ffn_router_b1, L0_ffn_router_w2, L0_ffn_router_b2, L0_ffn_alpha_bi, L0_ffn_expert_bias), axis=-1)
    return x

_drawn_inputs = setup_inputs


def setup_inputs(seed=0):
    import zlib

    import numpy as np

    out = dict(_drawn_inputs(seed))
    spreads = {'L0_attn_norm_scale': (1.0, 0.6),
     'L0_attn_conv_b': (0.0, 0.8),
     'L0_attn_b_dt': (0.0, 2.0),
     'L0_ffn_b_fwd': (0.0, 0.1),
     'L0_ffn_b_inv': (0.0, 0.1),
     'L0_ffn_router_b1': (0.0, 0.8),
     'L0_ffn_router_b2': (0.0, 0.8),
     'L0_ffn_expert_bias': (0.0, 0.755)}
    factors = {'L0_attn_w_in': 8.0,
     'L0_attn_conv_w': 8.0,
     'L0_attn_A_log': 8.0,
     'L0_attn_D': 64.0,
     'L0_attn_w_xproj': 8.0,
     'L0_attn_w_dt': 8.0,
     'L0_attn_w_out': 8.0}
    for name, (base, spread) in spreads.items():
        noise = np.random.default_rng([zlib.crc32(name.encode()), seed]).standard_normal(out[name].shape)
        drawn = base * np.exp(spread * noise) if base else spread * noise
        out[name] = jnp.asarray(drawn.astype(out[name].dtype))
    for name, factor in factors.items():
        out[name] = (out[name] * factor).astype(out[name].dtype)
    return out
```

```python
import concourse.bass as bass
from concourse import mybir
from contextlib import ExitStack

FP32 = mybir.dt.float32
ALU = mybir.AluOpType
ACT = mybir.ActivationFunctionType
AX = mybir.AxisListType

P = 128
NB, T, D = 16, 512, 256
DI, NS, RANK = 512, 16, 16
TAPS = 4
KE, RK = 8, 64
KR = KE * RK
TB, CT, DT = T // P, DI // P, D // P
NPROJ = RANK + 2 * NS
EPS = 1e-5
SLOTS = NS
BB_RING = 4
EXP_SET = "natural_log_exp_and_others"


class Batch:

    def __init__(self, const, turn=None):
        self.const, self.turn = const, turn
        self.parity = const % 2

    def shift(self, k):
        return Batch(self.const + k, self.turn)

    @property
    def exists(self):
        return self.turn is not None or 0 <= self.const < NB

    def count(self, per_batch, more):
        if self.turn is None:
            return self.const * per_batch + more
        return self.turn * (2 * per_batch) + (self.const * per_batch + more)

    def half_count(self, per_pair, more):
        if self.turn is None:
            return self.const // 2 * per_pair + more
        return self.turn * per_pair + (self.const // 2 * per_pair + more)

    def dram(self, ap):
        if self.turn is None:
            return ap[self.const]
        return ap[bass.ds(self.turn * 2 + self.const, 1)].rearrange("o p j d -> (o p) j d")


class Steps:

    def __init__(self, sem, names):
        self.sem, self.names = sem, names
        self.index = {n: i for i, n in enumerate(names)}
        self.next = 0

    def done(self, batch, name):
        return batch.count(len(self.names), self.index[name] + 1)

    def step(self, name):
        assert self.names[self.next] == name, (self.names[self.next], name)
        self.next = (self.next + 1) % len(self.names)
        return self.sem


SCHEDULE = {
    (0, 0): [("F", "stats", 0), ("L", "pt", 3)],
    (0, 1): [("L", "mm", 4)],
    (0, 2): [("L", "out", 1)],
    (0, 3): [("B", "y", 0), ("B", "y", 1), ("B", "y", 2), ("B", "y", 3)],
    (1, 0): [("F", "h", 0), ("L", "pt", 4)],
    (1, 1): [("L", "mm", 5)],
    (2, 0): [("L", "pt", 5)],
    (2, 1): [("L", "mm", 6), ("F", "hT", 0)],
    (2, 2): [("F", "hT", 1)],
    (2, 3): [("L", "out", 2)],
    (3, 0): [("L", "pt", 6)],
    (3, 1): [("L", "mm", 7)],
    (3, 2): [("B", "wo", 0)],
    (4, 0): [("L", "pt", 7)],
    (4, 1): [("B", "wo", 1)],
    (4, 2): [("F", "xs", 0)],
    (4, 3): [("L", "out", 3)],
    (5, 0): [("B", "ln2", 0)],
    (5, 1): [("F", "xs", 1)],
    (5, 3): [("F", "xs", 2)],
    (6, 0): [("B", "x1", 0)],
    (6, 1): [("F", "xs", 3)],
    (6, 2): [("L", "fin1", 0)],
    (6, 3): [("F", "res", 0)],
    (7, 0): [("F", "res", 1)],
    (7, 2): [("F", "res", 2), ("L", "fin2", 0)],
    (8, 0): [("B", "xn", 0)],
    (8, 1): [("F", "res", 3)],
    (8, 2): [("B", "xnT", 0)],
    (8, 3): [("B", "xnT", 1)],
    (9, 0): [("F", "silu", 0)],
    (9, 1): [("B", "rt", 0)],
    (9, 3): [("B", "rt", 1)],
    (10, 0): [("F", "proj", 0)],
    (10, 2): [("B", "rt", 2)],
    (10, 3): [("B", "rt", 3)],
    (11, 0): [("B", "gelu", 0)],
    (11, 1): [("B", "logit", 0)],
    (11, 2): [("F", "dt", 0)],
    (12, 0): [("B", "soft", 0)],
    (12, 1): [("F", "dt", 1)],
    (12, 2): [("L", "mm", 0)],
    (13, 0): [("L", "pt", 0), ("F", "dt", 2)],
    (13, 1): [("L", "mm", 1)],
    (13, 3): [("F", "dt", 3)],
    (14, 0): [("L", "pt", 1)],
    (14, 1): [("L", "mm", 2)],
    (14, 3): [("L", "out", 0)],
    (15, 0): [("L", "pt", 2)],
    (15, 1): [("L", "mm", 3)],
}
TAIL_SLOT = 12


def numbered(*names, count=4):
    return [f"{n}{i}" for n in names for i in range(count)]


def program(nc, x, norm_scale, w_in, conv_w, conv_b, A_log, D_skip, w_xproj, w_dt, b_dt, w_out,
            W_Q, W_K, W_O, W_inv, V_fwd, W_fwd, U_fwd, b_fwd, V_inv, W_inv_exp, U_inv, b_inv,
            router_w1, router_b1, router_w2, router_b2, alpha_bi, expert_bias, out):
    ctx = ExitStack()
    with ctx:
        ctx.enter_context(nc.allow_non_contiguous_dma(reason="small weights, loaded once"))

        def sb(name, *shape):
            return ctx.enter_context(nc.sbuf_tensor(name, list(shape), FP32))

        def psum(name):
            return ctx.enter_context(nc.psum_tensor(name, [P, T], FP32))

        def sem(name):
            return ctx.enter_context(nc.semaphore(name))

        w_in_sb = sb("w_in_sb", P, DT, 2 * DI)
        w_out_sb = sb("w_out_sb", P, CT, D)
        w_xproj_sb = sb("w_xproj_sb", P, CT, NPROJ)
        w_dt_sb = sb("w_dt_sb", RANK, DI)
        decay_rate = sb("decay_rate", P, CT, NS)
        conv_w_sb = sb("conv_w_sb", P, CT, TAPS)
        conv_b_sb = sb("conv_b_sb", P, CT)
        skip_sb = sb("skip_sb", P, CT)
        b_dt_sb = sb("b_dt_sb", P, CT)
        norm_sb = sb("norm_sb", P, DT)
        b1_sb = sb("b1_sb", P, DT)
        q_to_expert = [sb(f"q_to_expert{br}", P, DT, KR) for br in range(2)]
        k_to_expert = [sb(f"k_to_expert{br}", P, DT, KR) for br in range(2)]
        q_to_router = [sb(f"q_to_router{br}", P, DT, D) for br in range(2)]
        expert_to_out = sb("expert_to_out", P, 8, D)
        w2T = sb("w2T", P, DT, KE)
        bias_to_out = sb("bias_to_out", 2 * KE, D)
        logit_bias = sb("logit_bias", P, TB, 2, KE)
        n_valid = sb("n_valid", P, TB, 2)
        alpha_sb = sb("alpha_sb", P, 1)
        minus_half = sb("minus_half", P, TB)
        one = sb("one", P, 1)
        ident = sb("ident", P, P)

        x_front = sb("x_front", P, TB, D)
        x_back = [sb(f"x_back{i}", P, TB, D) for i in range(2)]
        hT = sb("hT", P, DT, T)
        xs = [sb(f"xs{i}", P, CT, T) for i in range(2)]
        res = [sb(f"res{i}", P, CT, T) for i in range(2)]
        delta = [sb(f"delta{i}", P, CT, T) for i in range(2)]
        dx = [sb(f"dx{i}", P, CT, T) for i in range(2)]
        scratch = sb("scratch", P, 4, T)
        B_rows = sb("B_rows", P, BB_RING, T)
        bx = [sb(f"bx{i}", P, CT // 2, T) for i in range(2)]
        h = [sb(f"h{i}", P, CT, T) for i in range(2)]
        yT = sb("yT", P, TB, DI)
        rows = sb("rows", P, TB, D)
        xnT = sb("xnT", P, DT, T)
        cumT = sb("cumT", P, DT, T)
        cum_sb = [sb(f"cum_sb{i}", P, KR) for i in range(2)]
        prod = [sb(f"prod{i}", P, KR) for i in range(2)]
        prodT = sb("prodT", P, 8, P)
        o_rows = sb("o_rows", P, TB, D)
        projT = sb("projT", NPROJ, T)
        C_tok = [sb(f"C_tok{i}", P, TB, NS) for i in range(2)]
        st_f, st_b, st_1, st_o = (sb(f"st_{n}", P, TB, 6) for n in "fb1o")
        mv_f, mv_b, mv_1, mv_o = (sb(f"mv_{n}", P, TB, 2) for n in "fb1o")
        ve_f, ms_f, rs_f, r2_f = (sb(n, P, TB) for n in ("ve_f", "ms_f", "rs_f", "r2_f"))
        r_x0 = [sb(f"r_x0{i}", P, TB) for i in range(2)]
        r_keep = sb("r_keep", P, TB)
        ve_b, rs_b, ve_1, rs_1, ve_o, rs_o = (sb(n, P, TB) for n in ("ve_b", "rs_b", "ve_1", "rs_1", "ve_o", "rs_o"))
        logits = sb("logits", P, TB, 2, KE)
        top = sb("top", P, TB * 2)
        total = sb("total", P, TB * 2)
        gate = sb("gate", P, TB, 2 * KE)
        gateT = sb("gateT", 2 * KE, T)

        B_dram = nc.dram_tensor("B_scratch", [2, NS, T], FP32).ap()

        decay = [psum(f"decay{i}") for i in range(2)]
        stateT = [psum(f"stateT{i}") for i in range(2)]
        bank = [psum(f"bank{i}") for i in range(4)]

        f_pe = Steps(sem("f_pe"), numbered("hT", count=2) + numbered("xs") + numbered("res") + ["proj", "Ct"] + numbered("dt"))
        f_act = Steps(sem("f_act"), numbered("hT", count=2) + numbered("cv") + numbered("res") + ["silux", "silur", "proj", "Ct"]
                      + [f"{n}{c}" for c in range(CT) for n in ("ab", "rl", "ex", "ln")])
        f_dve = Steps(sem("f_dve"), numbered("st", "ag", "h") + [f"{n}{c}" for c in range(CT) for n in ("cvA", "cvB", "cvC")]
                      + [f"{n}{c}" for c in range(CT) for n in ("d1", "d2", "dx")])
        f_pool = Steps(sem("f_pool"), ["ve", "r1", "ms", "mr", "me", "r2", "rs"] + [f"{n}{c}" for c in range(CT) for n in ("v", "w")])
        s_exp = Steps(sem("s_exp"), [f"{n},{c}" for n in range(NS) for c in range(CT)])
        s_bx = Steps(sem("s_bx"), [f"{n},{c}" for n in range(NS) for c in range(2)])
        s_scan = Steps(sem("s_scan"), [f"{n},{c}" for n in range(NS) for c in range(CT)])
        s_tr = Steps(sem("s_tr"), [f"{n},{c}" for n in range(NS) for c in range(TB)])
        s_acc = Steps(sem("s_acc"), [f"{n},{c}" for n in range(NS) for c in range(TB)])
        b_pe = Steps(sem("b_pe"), numbered("y") + ["wo0", "wo1", "xnT0", "xnT1"] + numbered("rt") + ["lg", "gT"])
        b_act = Steps(sem("b_act"), ["xnT0", "xnT1"] + numbered("rt") + ["gelu", "ex", "gT"])
        b_dve = Steps(sem("b_dve"), ["keep"] + [f"{n}{c}" for c in range(CT) for n in ("u", "o")] + numbered("r", "st", "ag", "t", "x", "s1", "a1", "xn")
                      + ["cum0", "cum1", "lb", "mx", "sub", "sm", "sn", "rc", "wr", "wa"])
        b_pool = Steps(sem("b_pool"), ["ve", "rb", "ve1", "rb1"])
        l_pe = Steps(sem("l_pe"), ["cum0", "xv0", "pt0", "cum1", "xv1", "pt1", "cum2", "xv2", "out0", "pt2", "cum3", "xv3",
                                   "pt3", "cum4", "xv4", "out1", "pt4", "cum5", "xv5", "pt5", "cum6", "xv6", "out2",
                                   "pt6", "cum7", "xv7", "pt7", "out3"])
        l_act = Steps(sem("l_act"), [n for n in l_pe.names if not n.startswith("xv")])
        l_dve = Steps(sem("l_dve"), [f"{n}{u}" for u in range(8) for n in ("pr", "pw")] + numbered("st", "ag", "t", "x"))
        l_pool = Steps(sem("l_pool"), ["ve", "rs"])
        xf_in = sem("xf_in")
        xb_in = [sem(f"xb_in{i}") for i in range(2)]
        stored = [sem(f"stored{i}") for i in range(2)]
        B_out = sem("B_out")
        B_in = [sem(f"B_in{i}") for i in range(BB_RING)]
        w_ld = sem("w_ld")
        w_pe = sem("w_pe")
        w_act = sem("w_act")
        w_dve = sem("w_dve")
        w_pool = sem("w_pool")
        passed = {name: sem(f"passed_{name}") for name in ("sp", "pool", "pe", "act", "dve")}

        def bank_uses(stage, task, k):
            if stage == "F":
                return {"hT": [(f_act, f"hT{k}")], "xs": [(f_dve, f"cvC{k}")], "res": [(f_act, f"res{k}")],
                        "proj": [(f_act, "proj"), (f_act, "Ct")], "dt": [(f_act, f"rl{k}")]}.get(task, [])
            if stage == "B":
                return {"y": [(b_dve, f"u{k}")], "wo": [(b_dve, f"r{2 * k + 1}")], "xnT": [(b_dve, f"cum{k}")],
                        "rt": [(b_act, f"rt{k}")], "logit": [(b_dve, "lb")], "soft": [(b_act, "gT")]}.get(task, [])
            return {"mm": [(l_act, f"cum{k}"), (l_dve, f"pr{k}")], "pt": [(l_act, f"pt{k}")], "out": [(l_act, f"out{k}")]}.get(task, [])

        class Use:

            def __init__(self, tensor, sem, free_at):
                self.bank, self.sem, self.free_at = tensor, sem, free_at

        def walk(engine, prologue, tasks, scan_part, scans_here=True):
            held = [None] * 4
            at = [0]

            def run(stage, task, k, batch):
                uses = []
                for steps, name in bank_uses(stage, task, k):
                    before = held[at[0] % 4]
                    uses.append(Use(bank[at[0] % 4], before[0].sem, before[0].done(before[1], before[2]))
                                if before else Use(bank[at[0] % 4], w_act, 1))
                    held[at[0] % 4] = (steps, batch, name)
                    at[0] += 1
                if (stage, task) in tasks:
                    tasks[stage, task](batch, k, uses)

            def iteration(q):
                for slot in range(SLOTS):
                    for quarter in range(4):
                        scan_part(q, slot, quarter)
                        for stage, task, k in SCHEDULE.get((slot, quarter), []):
                            batch = q.shift(1 if stage == "F" else -1 if stage == "B" or slot >= TAIL_SLOT else -2)
                            if batch.exists:
                                run(stage, task, k, batch)

            prologue()
            for slot in range(SLOTS):
                for quarter in range(4):
                    for stage, task, k in SCHEDULE.get((slot, quarter), []):
                        if stage == "F":
                            run(stage, task, k, Batch(0))
            iteration(Batch(0))
            iteration(Batch(1))
            turns = (NB - 4) // 2
            with engine.Fori(0, turns) as turn:
                start = [(s, Batch(b.const, turn), n) for s, b, n in held]
                held[:] = start
                first_at = at[0]
                iteration(Batch(2, turn))
                iteration(Batch(3, turn))
                assert (at[0] - first_at) % 4 == 0
                for (s, b, n), (s2, b2, n2) in zip(start, held):
                    assert s is s2 and n == n2 and b2.const == b.const + 2
            held[:] = [(s, Batch(b.const + 2 * (turns - 1)), n) for s, b, n in held]
            for q in range(NB - 2, NB + 2):
                iteration(Batch(q))

        stage_V = [h[0][:, 0:2, :], h[0][:, 2:4, :]]
        stage_W = [h[1][:, 0:2, :], h[1][:, 2:4, :]]
        stage_U = [bx[0][:, :, :], bx[1][:, :, :]]
        raw = yT[:, :, :].rearrange("p a (b c) -> p (a b) c", b=2)
        wq_raw, wk_raw, winv_raw, wo_raw = (raw[:, 2 * i:2 * i + 2, :] for i in range(4))
        r1_raw = o_rows[:, 0:2, :]
        r2_raw = o_rows[0:KE, 2, :]
        b_raw = o_rows[0:2 * KE, 3, :]
        tr = scratch[:, :, :].rearrange("p a (b c) -> p (a b) c", b=2)
        winvT, r1T, woT, wqiT = (tr[:, 2 * i:2 * i + 2, :] for i in range(4))
        wkiT = cumT[:, 0, :].rearrange("p (a b) -> p a b", a=2)
        bT = cumT[:, 1, 0:2 * 2 * KE].rearrange("p (a b) -> p a b", a=2)
        bias_raw = logits
        block = ctx.enter_context(nc.Block())

        N_WEIGHTS = [0]

        @block.sync
        def _(sp):
            def load(dst, src):
                sp.dma_start(dst, src).then_inc(w_ld, 16)
                N_WEIGHTS[0] += 1

            def rows_of(ap):
                return ap.rearrange("b (j p) d -> b p j d", p=P)

            x_rows, out_rows = rows_of(x), rows_of(out)

            def prologue():
                sp.dma_start(x_front[:, :, :], x_rows[0]).then_inc(xf_in, 16)
                square = "(t p) n -> p t n"
                load(wq_raw, W_Q.rearrange(square, p=P))
                load(wk_raw, W_K.rearrange(square, p=P))
                load(winv_raw, W_inv.rearrange(square, p=P))
                load(wo_raw, W_O.rearrange(square, p=P))
                load(r1_raw, router_w1.rearrange(square, p=P))
                load(r2_raw, router_w2)
                load(o_rows[0:KE, 3, :], b_fwd)
                load(o_rows[KE:2 * KE, 3, :], b_inv)
                for staged, weights in ((stage_V, (V_fwd, W_inv_exp)), (stage_W, (W_fwd, V_inv)), (stage_U, (U_fwd, U_inv))):
                    for br in range(2):
                        for t in range(DT):
                            load(staged[br][:, t, :].rearrange("p (k r) -> p k r", k=KE),
                                 weights[br][:, t * P:(t + 1) * P, :].rearrange("k p r -> p k r"))
                load(w_in_sb[:, :, :], w_in.rearrange(square, p=P))
                load(w_out_sb[:, :, :], w_out.rearrange(square, p=P))
                load(w_xproj_sb[:, :, :], w_xproj.rearrange(square, p=P))
                load(w_dt_sb[:, :], w_dt)
                load(decay_rate[:, :, :], A_log.rearrange(square, p=P))
                for c in range(CT):
                    load(conv_w_sb[:, c, :], conv_w[:, 0, c * P:(c + 1) * P].rearrange("k p -> p k"))
                for dst, src in ((conv_b_sb, conv_b), (skip_sb, D_skip), (b_dt_sb, b_dt), (norm_sb, norm_scale), (b1_sb, router_b1)):
                    load(dst[:, :], src.rearrange("(t p) -> p t", p=P))
                load(alpha_sb[:, :], alpha_bi.partition_broadcast(P))
                load(bias_raw[:, 0, 0, :], router_b2.rearrange("(o k) -> o k", o=1).partition_broadcast(P).rearrange("p o k -> p (o k)"))
                load(bias_raw[:, 0, 1, :], expert_bias.rearrange("(o k) -> o k", o=1).partition_broadcast(P).rearrange("p o k -> p (o k)"))

            def row_of_B(batch, n):
                back = n - BB_RING
                free = batch if back >= 0 else batch.shift(-1)
                if free.exists:
                    sp.wait_ge(s_bx.sem, s_bx.done(free, f"{back % NS},1"))
                if n == 0:
                    sp.sem_inc(passed["sp"], 1)
                    sp.wait_ge(B_out, batch.count(16, 16))
                sp.dma_start(B_rows[:, n % BB_RING, :],
                             B_dram[batch.parity, n:n + 1, :].partition_broadcast(P).rearrange("p o t -> p (o t)")
                             ).then_inc(B_in[n % BB_RING], 16)

            def load_x_front(batch, k, uses):
                nxt = batch.shift(1)
                if nxt.turn is None and nxt.const >= NB:
                    return
                sp.wait_ge(f_pe.sem, f_pe.done(batch, "hT1"))
                sp.sem_inc(passed["sp"], 1)
                sp.dma_start(x_front[:, :, :], nxt.dram(x_rows)).then_inc(xf_in, 16)

            def write_B(batch, k, uses):
                sp.wait_ge(f_act.sem, f_act.done(batch, "proj"))
                sp.dma_start(B_dram[batch.parity], projT[RANK:RANK + NS, :]).then_inc(B_out, 16)

            def first_rows(batch, k, uses):
                if k == 3:
                    for n in range(BB_RING - 1):
                        row_of_B(batch, n)

            def load_x_back(batch):
                if batch.turn is not None or batch.const >= 2:
                    sp.wait_ge(stored[batch.parity], batch.half_count(16, 0))
                    sp.sem_inc(passed["sp"], 1)
                sp.dma_start(x_back[batch.parity][:, :, :], batch.dram(x_rows)).then_inc(xb_in[batch.parity], 16)

            def store(batch, k, uses):
                sp.wait_ge(l_dve.sem, l_dve.done(batch, "x3"))
                sp.sem_inc(passed["sp"], 1)
                sp.dma_start(batch.dram(out_rows), x_back[batch.parity][:, :, :]).then_inc(stored[batch.parity], 16)

            def scan_part(q, slot, quarter):
                if quarter == 0 and q.exists:
                    if slot + BB_RING - 1 < NS:
                        row_of_B(q, slot + BB_RING - 1)
                    if slot == 8:
                        load_x_back(q)

            walk(sp, prologue, {("F", "hT"): lambda b, k, u: load_x_front(b, k, u) if k == 1 else None,
                                ("F", "proj"): write_B, ("F", "dt"): first_rows, ("L", "fin2"): store}, scan_part)
            for i in range(2):
                sp.wait_ge(stored[i], NB // 2 * 16)

        @block.gpsimd
        def _(pool):
            def prologue():
                chain = [0]

                def link(ins):
                    chain[0] += 1
                    ins.then_inc(w_pool, 1)
                    pool.wait_ge(w_pool, chain[0])

                link(pool.memset(ident[:, :], 0.0))
                link(pool.affine_select(out=ident[:, :], in_=ident[:, :], compare_op=ALU.not_equal, fill=1.0,
                                        base=0, pattern=[[-1, P]], channel_multiplier=1))
                link(pool.memset(minus_half[:, :], -0.5))
                link(pool.memset(one[:, :], 1.0))
                link(pool.iota(n_valid[:, :, :], pattern=[[P, TB], [0, 2]], base=1, channel_multiplier=1,
                               allow_small_or_imprecise_dtypes=True))

            def rstd(steps, batch, var, ve, rs, names):
                pool.tensor_scalar(ve[:, :], var, EPS, None, ALU.add).then_inc(steps.step(names[0]), 1)
                pool.wait_ge(steps.sem, steps.done(batch, names[0]))
                pool.tensor_tensor(rs[:, :], ve[:, :], minus_half[:, :], ALU.pow).then_inc(steps.step(names[1]), 1)

            def front_rstd(b, k, uses):
                pool.wait_ge(f_dve.sem, f_dve.done(b, "ag3"))
                pool.sem_inc(passed["pool"], 1)
                r = r_x0[b.parity]
                rstd(f_pool, b, mv_f[:, :, 1], ve_f, r, ("ve", "r1"))
                pool.wait_ge(f_pool.sem, f_pool.done(b, "r1"))
                pool.tensor_tensor(ms_f[:, :], mv_f[:, :, 1], r[:, :], ALU.mult).then_inc(f_pool.step("ms"), 1)
                pool.wait_ge(f_pool.sem, f_pool.done(b, "ms"))
                pool.tensor_tensor(ms_f[:, :], ms_f[:, :], r[:, :], ALU.mult).then_inc(f_pool.step("mr"), 1)
                pool.wait_ge(f_pool.sem, f_pool.done(b, "mr"))
                pool.sem_inc(passed["pool"], 1)
                pool.tensor_scalar(ms_f[:, :], ms_f[:, :], EPS, None, ALU.add).then_inc(f_pool.step("me"), 1)
                pool.wait_ge(f_pool.sem, f_pool.done(b, "me"))
                pool.tensor_tensor(r2_f[:, :], ms_f[:, :], minus_half[:, :], ALU.pow).then_inc(f_pool.step("r2"), 1)
                pool.wait_ge(f_pool.sem, f_pool.done(b, "r2"))
                pool.tensor_tensor(rs_f[:, :], r2_f[:, :], r[:, :], ALU.mult).then_inc(f_pool.step("rs"), 1)

            def softplus_rest(b, c, uses):
                e, v = scratch[:, c % 2, :], scratch[:, 2 + c % 2, :]
                if c >= 2:
                    pool.wait_ge(f_dve.sem, f_dve.done(b, f"d1{c - 2}"))
                pool.wait_ge(f_act.sem, f_act.done(b, f"ex{c}"))
                pool.sem_inc(passed["pool"], 1)
                pool.tensor_scalar(v, e, 1.0, -1.0, ALU.add, ALU.add).then_inc(f_pool.step(f"v{c}"), 1)
                pool.wait_ge(f_pool.sem, f_pool.done(b, f"v{c}"))
                pool.tensor_tensor(v, e, v, ALU.subtract).then_inc(f_pool.step(f"w{c}"), 1)

            def back_rstd(b, k, uses):
                pool.wait_ge(b_dve.sem, b_dve.done(b, "ag3"))
                pool.sem_inc(passed["pool"], 1)
                rstd(b_pool, b, mv_b[:, :, 1], ve_b, rs_b, ("ve", "rb"))

            def x1_rstd(b, k, uses):
                pool.wait_ge(b_dve.sem, b_dve.done(b, "a13"))
                pool.sem_inc(passed["pool"], 1)
                rstd(b_pool, b, mv_1[:, :, 1], ve_1, rs_1, ("ve1", "rb1"))

            def out_rstd(b, k, uses):
                pool.wait_ge(l_dve.sem, l_dve.done(b, "ag3"))
                pool.sem_inc(passed["pool"], 1)
                rstd(l_pool, b, mv_o[:, :, 1], ve_o, rs_o, ("ve", "rs"))

            def scan_part(q, n, quarter):
                if not q.exists or quarter % 2:
                    return
                half = quarter // 2
                if n == 0 and half == 0:
                    pool.wait_ge(f_dve.sem, f_dve.done(q, "dx3"))
                if half == 0:
                    pool.wait_ge(B_in[n % BB_RING], q.count(16 * NS // BB_RING, 16 * (n // BB_RING + 1)))
                free = q if n else q.shift(-1)
                if free.exists:
                    pool.wait_ge(s_scan.sem, s_scan.done(free, f"{(n - 1) % NS},{2 * half + 1}"))
                row = B_rows[:, n % BB_RING, :].rearrange("p (o t) -> p o t", o=1).broadcast_to([P, CT // 2, T])
                pool.tensor_tensor(bx[half][:, :, :], dx[q.parity][:, 2 * half:2 * half + 2, :], row, ALU.mult).then_inc(s_bx.step(f"{n},{half}"), 1)

            walk(pool, prologue, {("F", "stats"): front_rstd, ("F", "dt"): softplus_rest, ("B", "ln2"): back_rstd,
                                  ("B", "x1"): x1_rstd, ("L", "fin1"): out_rstd}, scan_part)

        def square_T(raw_w):
            return [(a * D + f * P, a * D + (f + 1) * P, raw_w[:, f, a * P:(a + 1) * P], None) for a in range(DT) for f in range(DT)]

        def product(lhs, rhs):
            return [(m * D, (m + 1) * D, lhs[:, t, m * P:(m + 1) * P], rhs[:, t, :], t == 0, t == DT - 1)
                    for m in range(DT) for t in range(DT)]

        jobs = []

        def job(mms, dst, width, depends, scaled=None, parts=P):
            jobs.append((mms, dst, width, depends, scaled, parts))
            return len(jobs) - 1

        flat = lambda ap: ap.rearrange("p a b -> p (a b)")
        j_winvT = job(square_T(winv_raw), flat(winvT), 2 * D, -1)
        j_r1T = job(square_T(r1_raw), flat(r1T), 2 * D, -1)
        j_woT = job(square_T(wo_raw), flat(woT), 2 * D, -1)
        job([(t * KE, (t + 1) * KE, r2_raw[:, t * P:(t + 1) * P], None) for t in range(DT)], flat(w2T), 2 * KE, -1)
        j_bT = job([(t * 2 * KE, (t + 1) * 2 * KE, b_raw[:, t * P:(t + 1) * P], None) for t in range(DT)], bT, 4 * KE, -1, "b")
        j_wqiT = job(product(winvT, wq_raw), flat(wqiT), 2 * D, j_winvT)
        j_wkiT = job(product(winvT, wk_raw), flat(wkiT), 2 * D, j_winvT)
        for br in range(2):
            for lhs, rhs, dst, dep in ((wq_raw if br == 0 else wqiT, stage_V[br], q_to_expert[br], j_wqiT),
                                       (wk_raw if br == 0 else wkiT, stage_W[br], k_to_expert[br], j_wkiT)):
                for m in range(DT):
                    job([(0, KR, lhs[:, t, m * P:(m + 1) * P], rhs[:, t, :], t == 0, t == DT - 1) for t in range(DT)],
                        dst[:, m, :], KR, dep)
            job(product(wq_raw if br == 0 else wqiT, r1T), flat(q_to_router[br]), 2 * D, j_wkiT)
        for br in range(2):
            for pair in range(2):
                mms = []
                for i in range(2):
                    kt = 2 * pair + i
                    mms += [(i * D, (i + 1) * D, stage_U[br][:, t, kt * P:(kt + 1) * P], woT[:, t, :], t == 0, t == DT - 1) for t in range(DT)]
                k0 = 4 * br + 2 * pair
                job(mms, flat(expert_to_out[:, k0:k0 + 2, :]), 2 * D, j_woT, "all" if br else None)
        job([(0, D, bT[:, t, :], woT[:, t, :], t == 0, t == DT - 1) for t in range(DT)], bias_to_out[:, :], D, j_bT, None, 2 * KE)
        N_ACT = [0]

        @block.tensor
        def _(pe):
            def prologue():
                pe.wait_ge(w_ld, 16 * N_WEIGHTS[0])
                pe.wait_ge(w_pool, 2)
                for i, (mms, dst, width, depends, scaled, parts) in enumerate(jobs):
                    if max(i - 3, depends + 1) > 0:
                        pe.wait_ge(w_act, max(i - 3, depends + 1))
                    for mm in mms:
                        if mm[3] is None:
                            src = mm[2]
                            k = src.shape[0]
                            last = pe.transpose(bank[i % 4][:, mm[0]:mm[1]], src, ident[0:k, 0:k])
                        else:
                            last = pe.matmul(bank[i % 4][0:parts, mm[0]:mm[1]], mm[2], mm[3], start=mm[4], stop=mm[5])
                    last.then_inc(w_pe, 1)
                pe.wait_ge(w_act, len(jobs))

            def matmuls(out_ap, pairs):
                for i, (lhsT, rhs) in enumerate(pairs):
                    last = pe.matmul(out_ap, lhsT, rhs, start=(i == 0), stop=(i == len(pairs) - 1))
                return last

            def rows_T(b, t, uses, src, steps, name):
                pe.wait_ge(uses[0].sem, uses[0].free_at)
                for j in range(TB):
                    last = pe.transpose(uses[0].bank[:, j * P:(j + 1) * P], src[:, j, t * P:(t + 1) * P], ident[:, :])
                last.then_inc(steps.step(name), 1)

            def hT_task(b, t, uses):
                pe.wait_ge(f_dve.sem, f_dve.done(b, "h3"))
                rows_T(b, t, uses, x_front, f_pe, f"hT{t}")

            def xs_task(b, c, uses):
                if c == 0:
                    pe.wait_ge(f_act.sem, f_act.done(b, "hT1"))
                pe.wait_ge(uses[0].sem, uses[0].free_at)
                matmuls(uses[0].bank[:, :], [(w_in_sb[:, t, c * P:(c + 1) * P], hT[:, t, :]) for t in range(DT)]).then_inc(f_pe.step(f"xs{c}"), 1)

            def res_task(b, c, uses):
                pe.wait_ge(uses[0].sem, uses[0].free_at)
                matmuls(uses[0].bank[:, :], [(w_in_sb[:, t, DI + c * P:DI + (c + 1) * P], hT[:, t, :]) for t in range(DT)]).then_inc(f_pe.step(f"res{c}"), 1)

            def proj_task(b, k, uses):
                pe.wait_ge(f_act.sem, f_act.done(b, "silux"))
                pe.wait_ge(uses[0].sem, uses[0].free_at)
                matmuls(uses[0].bank[0:NPROJ, :], [(w_xproj_sb[:, c, :], xs[b.parity][:, c, :]) for c in range(CT)]).then_inc(f_pe.step("proj"), 1)
                pe.wait_ge(uses[1].sem, uses[1].free_at)
                pe.wait_ge(f_act.sem, f_act.done(b, "proj"))
                pe.sem_inc(passed["pe"], 1)
                for j in range(TB):
                    last = pe.transpose(uses[1].bank[:, j * NPROJ:(j + 1) * NPROJ], projT[:, j * P:(j + 1) * P], ident[0:NPROJ, 0:NPROJ])
                last.then_inc(f_pe.step("Ct"), 1)

            def dt_task(b, c, uses):
                pe.wait_ge(uses[0].sem, uses[0].free_at)
                matmuls(uses[0].bank[:, :], [(w_dt_sb[:, c * P:(c + 1) * P], projT[0:RANK, :])]).then_inc(f_pe.step(f"dt{c}"), 1)

            def y_task(b, c, uses):
                if c == 0:
                    pe.wait_ge(s_acc.sem, s_acc.done(b, f"{NS - 1},{TB - 1}"))
                pe.wait_ge(uses[0].sem, uses[0].free_at)
                for j in range(TB):
                    last = pe.transpose(uses[0].bank[:, j * P:(j + 1) * P], yT[:, j, c * P:(c + 1) * P], ident[:, :])
                last.then_inc(b_pe.step(f"y{c}"), 1)

            def wo_task(b, k, uses):
                if k == 0:
                    pe.wait_ge(b_dve.sem, b_dve.done(b, "o3"))
                pe.wait_ge(uses[0].sem, uses[0].free_at)
                for i in range(2):
                    j = 2 * k + i
                    last = matmuls(uses[0].bank[:, i * D:(i + 1) * D],
                                   [(res[b.parity][:, c, j * P:(j + 1) * P], w_out_sb[:, c, :]) for c in range(CT)])
                last.then_inc(b_pe.step(f"wo{k}"), 1)

            def xnT_task(b, t, uses):
                pe.wait_ge(b_dve.sem, b_dve.done(b, "xn3"))
                rows_T(b, t, uses, rows, b_pe, f"xnT{t}")

            def rt_task(b, k, uses):
                br, m = k // 2, k % 2
                if k == 0:
                    pe.wait_ge(b_act.sem, b_act.done(b, "xnT1"))
                pe.wait_ge(uses[0].sem, uses[0].free_at)
                matmuls(uses[0].bank[:, :], [(q_to_router[br][:, t, m * P:(m + 1) * P], xnT[:, t, :]) for t in range(DT)]).then_inc(b_pe.step(f"rt{k}"), 1)

            def logit_task(b, k, uses):
                pe.wait_ge(b_act.sem, b_act.done(b, "gelu"))
                pe.wait_ge(uses[0].sem, uses[0].free_at)
                for j in range(TB):
                    for br in range(2):
                        at = (j * 2 + br) * KE
                        last = matmuls(uses[0].bank[:, at:at + KE],
                                       [(scratch[:, 2 * br + m, j * P:(j + 1) * P], w2T[:, m, :]) for m in range(DT)])
                last.then_inc(b_pe.step("lg"), 1)

            def gateT_task(b, k, uses):
                pe.wait_ge(b_dve.sem, b_dve.done(b, "wa"))
                pe.wait_ge(uses[0].sem, uses[0].free_at)
                for j in range(TB):
                    last = pe.transpose(uses[0].bank[0:2 * KE, j * P:(j + 1) * P], gate[:, j, :], ident[:, :])
                last.then_inc(b_pe.step("gT"), 1)

            def mm_task(b, u, uses):
                j, br = u // 2, u % 2
                if u == 0:
                    pe.wait_ge(b_dve.sem, b_dve.done(b, "cum1"))
                pe.wait_ge(uses[0].sem, uses[0].free_at)
                matmuls(uses[0].bank[:, :], [(cumT[:, t, j * P:(j + 1) * P], k_to_expert[br][:, t, :]) for t in range(DT)]).then_inc(l_pe.step(f"cum{u}"), 1)
                pe.wait_ge(uses[1].sem, uses[1].free_at)
                matmuls(uses[1].bank[:, :], [(xnT[:, t, j * P:(j + 1) * P], q_to_expert[br][:, t, :]) for t in range(DT)]).then_inc(l_pe.step(f"xv{u}"), 1)

            def pt_task(b, u, uses):
                pe.wait_ge(l_dve.sem, l_dve.done(b, f"pw{u}"))
                pe.wait_ge(uses[0].sem, uses[0].free_at)
                for i in range(KR // P):
                    last = pe.transpose(uses[0].bank[:, i * P:(i + 1) * P], prod[u % 2][:, i * P:(i + 1) * P], ident[:, :])
                last.then_inc(l_pe.step(f"pt{u}"), 1)

            def out_task(b, j, uses):
                pe.wait_ge(l_act.sem, l_act.done(b, f"pt{2 * j + 1}"))
                if j == 0:
                    pe.wait_ge(b_act.sem, b_act.done(b, "gT"))
                pe.wait_ge(uses[0].sem, uses[0].free_at)
                matmuls(uses[0].bank[:, 0:D], [(prodT[:, i, :], expert_to_out[:, i, :]) for i in range(8)]
                                  + [(gateT[:, j * P:(j + 1) * P], bias_to_out[:, :])]).then_inc(l_pe.step(f"out{j}"), 1)

            def scan_part(q, slot, j):
                batch, n = (q, slot - 1) if slot else (q.shift(-1), NS - 1)
                if not batch.exists:
                    return
                if j == 0:
                    pe.wait_ge(s_scan.sem, s_scan.done(batch, f"{n},{CT - 1}"))
                back = n * TB + j - 2
                free = batch if back >= 0 else batch.shift(-1)
                if free.exists:
                    pe.wait_ge(s_acc.sem, s_acc.done(free, f"{back % (NS * TB) // TB},{back % TB}"))
                for c in range(CT):
                    last = pe.transpose(stateT[j % 2][:, c * P:(c + 1) * P], h[n % 2][:, c, j * P:(j + 1) * P], ident[:, :])
                last.then_inc(s_tr.step(f"{n},{j}"), 1)

            walk(pe, prologue, {("F", "hT"): hT_task, ("F", "xs"): xs_task, ("F", "res"): res_task, ("F", "proj"): proj_task,
                                ("F", "dt"): dt_task, ("B", "y"): y_task, ("B", "wo"): wo_task, ("B", "xnT"): xnT_task,
                                ("B", "rt"): rt_task, ("B", "logit"): logit_task, ("B", "soft"): gateT_task,
                                ("L", "mm"): mm_task, ("L", "pt"): pt_task, ("L", "out"): out_task}, scan_part)

        @block.scalar
        def _(act):
            def prologue():
                act.preload_act_table_set(EXP_SET)
                act.wait_ge(w_ld, 16 * N_WEIGHTS[0])
                for i, (mms, dst, width, depends, scaled, parts) in enumerate(jobs):
                    act.wait_ge(w_pe, i + 1)
                    src = bank[i % 4][0:parts, 0:width]
                    if scaled == "b":
                        both = src.rearrange("p (a b) -> p a b", a=2)
                        act.activation(dst[:, :, 0:KE], both[:, :, 0:KE], ACT.Copy)
                        act.activation(dst[:, :, KE:2 * KE], both[:, :, KE:2 * KE], ACT.Copy, scale=alpha_sb[:, 0:1]).then_inc(w_act, 1)
                    elif scaled == "all":
                        act.activation(dst, src, ACT.Copy, scale=alpha_sb[:, 0:1]).then_inc(w_act, 1)
                    else:
                        act.activation(dst, src, ACT.Copy).then_inc(w_act, 1)
                act.activation(decay_rate[:, :, :], decay_rate[:, :, :], ACT.Exp).then_inc(w_act, 1)
                act.wait_ge(w_dve, 2)

            def hT_task(b, t, uses):
                act.wait_ge(f_pe.sem, f_pe.done(b, f"hT{t}"))
                act.activation(hT[:, t, :], uses[0].bank[:, :], ACT.Copy, scale=norm_sb[:, t:t + 1]).then_inc(f_act.step(f"hT{t}"), 1)

            def xs_task(b, c, uses):
                if c == 0:
                    if b.shift(-2).exists:
                        act.wait_ge(b_dve.sem, b_dve.done(b.shift(-2), "o3"))
                act.wait_ge(f_pe.sem, f_pe.done(b, f"xs{c}"))
                act.activation(xs[b.parity][:, c, :], uses[0].bank[:, :], ACT.Identity,
                                          scale=conv_w_sb[:, c, TAPS - 1:TAPS], bias=conv_b_sb[:, c:c + 1]).then_inc(f_act.step(f"cv{c}"), 1)

            def res_task(b, c, uses):
                if c == 0:
                    if b.shift(-2).exists:
                        act.wait_ge(b_pe.sem, b_pe.done(b.shift(-2), "wo1"))
                act.wait_ge(f_pe.sem, f_pe.done(b, f"res{c}"))
                act.activation(res[b.parity][:, c, :], uses[0].bank[:, :], ACT.Copy).then_inc(f_act.step(f"res{c}"), 1)

            def silu_task(b, k, uses):
                act.wait_ge(f_dve.sem, f_dve.done(b, "cvC3"))
                act.sem_inc(passed["act"], 1)
                act.preload_act_table_set("silu_and_others")
                act.activation(xs[b.parity][:, :, :], xs[b.parity][:, :, :], ACT.Silu).then_inc(f_act.step("silux"), 1)
                act.wait_ge(f_act.sem, f_act.done(b, "res3"))
                act.activation(res[b.parity][:, :, :], res[b.parity][:, :, :], ACT.Silu).then_inc(f_act.step("silur"), 1)
                act.preload_act_table_set(EXP_SET)

            def proj_task(b, k, uses):
                act.wait_ge(f_pe.sem, f_pe.done(b, "proj"))
                if b.turn is not None or b.const > 0:
                    act.wait_ge(B_out, b.count(16, 0))
                act.activation(projT[:, :], uses[0].bank[0:NPROJ, :], ACT.Copy).then_inc(f_act.step("proj"), 1)
                act.wait_ge(f_pe.sem, f_pe.done(b, "Ct"))
                if b.shift(-2).exists:
                    act.wait_ge(s_acc.sem, s_acc.done(b.shift(-2), f"{NS - 1},{TB - 1}"))
                both = uses[1].bank[:, 0:TB * NPROJ].rearrange("p (j n) -> p j n", j=TB)
                act.activation(C_tok[b.parity][:, :, :], both[:, :, RANK + NS:NPROJ], ACT.Copy).then_inc(f_act.step("Ct"), 1)

            def dt_task(b, c, uses):
                e = scratch[:, c % 2, :]
                act.wait_ge(f_pe.sem, f_pe.done(b, f"dt{c}"))
                if c >= 2:
                    act.wait_ge(f_pool.sem, f_pool.done(b, f"w{c - 2}"))
                elif c == 0:
                    if b.shift(-2).exists:
                        act.wait_ge(b_pe.sem, b_pe.done(b.shift(-2), "lg"))
                    if b.shift(-2).exists:
                        act.wait_ge(s_bx.sem, s_bx.done(b.shift(-2), f"{NS - 1},1"))
                    if b.shift(-1).exists:
                        act.wait_ge(f_pool.sem, f_pool.done(b.shift(-1), "w3"))
                act.activation(e, uses[0].bank[:, :], ACT.Abs, bias=b_dt_sb[:, c:c + 1]).then_inc(f_act.step(f"ab{c}"), 1)
                act.activation(dx[b.parity][:, c, :], uses[0].bank[:, :], ACT.Relu, bias=b_dt_sb[:, c:c + 1]).then_inc(f_act.step(f"rl{c}"), 1)
                act.wait_ge(f_act.sem, f_act.done(b, f"ab{c}"))
                act.activation(e, e, ACT.Exp, scale=-1.0).then_inc(f_act.step(f"ex{c}"), 1)
                act.wait_ge(f_act.sem, f_act.done(b, f"ex{c}"))
                act.activation(delta[b.parity][:, c, :], e, ACT.Ln, bias=one[:, 0:1]).then_inc(f_act.step(f"ln{c}"), 1)

            def xnT_task(b, t, uses):
                act.wait_ge(b_pe.sem, b_pe.done(b, f"xnT{t}"))
                act.activation(xnT[:, t, :], uses[0].bank[:, :], ACT.Copy).then_inc(b_act.step(f"xnT{t}"), 1)

            def rt_task(b, k, uses):
                if k == 0:
                    if b.shift(1).exists:
                        act.wait_ge(f_dve.sem, f_dve.done(b.shift(1), "d13"))
                act.wait_ge(b_pe.sem, b_pe.done(b, f"rt{k}"))
                act.activation(scratch[:, k, :], uses[0].bank[:, :], ACT.Identity, bias=b1_sb[:, k % 2:k % 2 + 1]).then_inc(b_act.step(f"rt{k}"), 1)

            def gelu_task(b, k, uses):
                act.wait_ge(b_act.sem, b_act.done(b, "rt3"))
                act.sem_inc(passed["act"], 1)
                act.preload_act_table_set("gelu_and_others")
                act.activation(scratch[:, :, :], scratch[:, :, :], ACT.Gelu).then_inc(b_act.step("gelu"), 1)
                act.preload_act_table_set(EXP_SET)

            def soft_exp(b, k, uses):
                act.wait_ge(b_dve.sem, b_dve.done(b, "sub"))
                act.activation(logits[:, :, :, :], logits[:, :, :, :], ACT.Exp).then_inc(b_act.step("ex"), 1)

            def gateT_task(b, k, uses):
                act.wait_ge(b_pe.sem, b_pe.done(b, "gT"))
                act.activation(gateT[:, :], uses[0].bank[0:2 * KE, :], ACT.Copy).then_inc(b_act.step("gT"), 1)

            def mm_task(b, u, uses):
                act.wait_ge(l_pe.sem, l_pe.done(b, f"cum{u}"))
                if u >= 2:
                    act.wait_ge(l_dve.sem, l_dve.done(b, f"pr{u - 2}"))
                elif u == 0:
                    if b.shift(-1).exists:
                        act.wait_ge(l_dve.sem, l_dve.done(b.shift(-1), "pr7"))
                act.activation(cum_sb[u % 2][:, :], uses[0].bank[:, :], ACT.Copy).then_inc(l_act.step(f"cum{u}"), 1)

            def pt_task(b, u, uses):
                br, j = u % 2, u // 2
                if br == 0:
                    free = b if j else b.shift(-1)
                    if free.exists:
                        act.wait_ge(l_pe.sem, l_pe.done(free, f"out{(j - 1) % TB}"))
                act.wait_ge(l_pe.sem, l_pe.done(b, f"pt{u}"))
                act.activation(flat(prodT[:, 4 * br:4 * br + 4, :]), uses[0].bank[:, :], ACT.Copy).then_inc(l_act.step(f"pt{u}"), 1)

            def out_task(b, j, uses):
                if j == 0:
                    if b.shift(-1).exists:
                        act.wait_ge(l_dve.sem, l_dve.done(b.shift(-1), "x3"))
                act.wait_ge(l_pe.sem, l_pe.done(b, f"out{j}"))
                act.activation(o_rows[:, j, :], uses[0].bank[:, 0:D], ACT.Copy).then_inc(l_act.step(f"out{j}"), 1)

            def scan_part(q, n, c):
                if not q.exists:
                    return
                if n == 0:
                    act.wait_ge(f_dve.sem, f_dve.done(q, f"d2{c}"))
                back = n * CT + c - 2
                free = q if back >= 0 else q.shift(-1)
                if free.exists:
                    act.wait_ge(s_scan.sem, s_scan.done(free, f"{back % (NS * CT) // CT},{back % CT}"))
                act.activation(decay[c % 2][:, :], delta[q.parity][:, c, :], ACT.Exp, scale=decay_rate[:, c, n:n + 1]).then_inc(s_exp.step(f"{n},{c}"), 1)

            walk(act, prologue, {("F", "hT"): hT_task, ("F", "xs"): xs_task, ("F", "res"): res_task, ("F", "silu"): silu_task,
                                 ("F", "proj"): proj_task, ("F", "dt"): dt_task, ("B", "xnT"): xnT_task, ("B", "rt"): rt_task,
                                 ("B", "gelu"): gelu_task, ("B", "logit"): soft_exp, ("B", "soft"): gateT_task,
                                 ("L", "mm"): mm_task, ("L", "pt"): pt_task, ("L", "out"): out_task}, scan_part)

        @block.vector
        def _(dve):
            def prologue():
                dve.wait_ge(w_act, len(jobs) + 1)
                dve.tensor_scalar(decay_rate[:, :, :], decay_rate[:, :, :], -1.0, None, ALU.mult).then_inc(w_dve, 1)
                both = top[:, 0:KE]
                dve.tensor_tensor(both, bias_raw[:, 0, 0, :], bias_raw[:, 0, 1, :], ALU.add).then_inc(w_dve, 1)
                dve.wait_ge(w_dve, 2)
                dve.tensor_copy(logit_bias[:, :, :, :].rearrange("p a b k -> p (a b) k"),
                                both.rearrange("p (o k) -> p o k", o=1).broadcast_to([P, TB * 2, KE])).then_inc(w_dve, 1)
                dve.wait_ge(w_dve, 3)
                dve.wait_ge(w_pool, 5)

            def stats(steps, b, src, st, mv, s, a, ready):
                for j in range(TB):
                    if ready:
                        dve.wait_ge(steps.sem, steps.done(b, f"{ready}{j}"))
                    dve.bn_stats(st[:, j, :], src[:, j, :]).then_inc(steps.step(f"{s}{j}"), 1)
                dve.wait_ge(steps.sem, steps.done(b, f"{s}{TB - 1}"))
                dve.sem_inc(passed["dve"], 1)
                for j in range(TB):
                    dve.bn_aggr(mv[:, j, :], st[:, j, :]).then_inc(steps.step(f"{a}{j}"), 1)

            def centre(steps, dst, src, mv, rs, j, name):
                dve.tensor_scalar(dst[:, j, :], src[:, j, :], mv[:, j, 0:1], rs[:, j:j + 1], ALU.subtract, ALU.mult).then_inc(steps.step(name), 1)

            def front_stats(b, k, uses):
                dve.wait_ge(xf_in, b.count(16, 16))
                stats(f_dve, b, x_front, st_f, mv_f, "st", "ag", None)

            def h_task(b, k, uses):
                dve.wait_ge(f_pool.sem, f_pool.done(b, "rs"))
                for j in range(TB):
                    centre(f_dve, x_front, x_front, mv_f, rs_f, j, f"h{j}")

            def xs_task(b, c, uses):
                x_c = xs[b.parity][:, c, :]
                dve.wait_ge(f_act.sem, f_act.done(b, f"cv{c}"))
                for back, name in ((1, "cvA"), (2, "cvB"), (3, "cvC")):
                    dve.scalar_tensor_tensor(out=x_c[:, back:], in0=uses[0].bank[:, 0:T - back],
                                                        scalar=conv_w_sb[:, c, TAPS - 1 - back:TAPS - back],
                                                        in1=x_c[:, back:], op0=ALU.mult, op1=ALU.add).then_inc(f_dve.step(f"{name}{c}"), 1)
                    if back < 3:
                        dve.wait_ge(f_dve.sem, f_dve.done(b, f"{name}{c}"))

            def dt_task(b, c, uses):
                d, x_c = delta[b.parity][:, c, :], dx[b.parity][:, c, :]
                dve.wait_ge(f_pool.sem, f_pool.done(b, f"w{c}"))
                dve.wait_ge(f_act.sem, f_act.done(b, f"ln{c}"))
                dve.tensor_tensor(d, d, scratch[:, 2 + c % 2, :], ALU.add).then_inc(f_dve.step(f"d1{c}"), 1)
                dve.wait_ge(f_dve.sem, f_dve.done(b, f"d1{c}"))
                dve.tensor_tensor(d, d, x_c, ALU.add).then_inc(f_dve.step(f"d2{c}"), 1)
                dve.wait_ge(f_dve.sem, f_dve.done(b, f"d2{c}"))
                dve.tensor_tensor(x_c, d, xs[b.parity][:, c, :], ALU.mult).then_inc(f_dve.step(f"dx{c}"), 1)

            def y_task(b, c, uses):
                r = b.parity
                if c == 0:
                    dve.tensor_copy(r_keep[:, :], r_x0[r][:, :]).then_inc(b_dve.step("keep"), 1)
                dve.wait_ge(b_pe.sem, b_pe.done(b, f"y{c}"))
                dve.scalar_tensor_tensor(out=xs[r][:, c, :], in0=xs[r][:, c, :], scalar=skip_sb[:, c:c + 1],
                                                    in1=uses[0].bank[:, :], op0=ALU.mult, op1=ALU.add).then_inc(b_dve.step(f"u{c}"), 1)
                dve.wait_ge(b_dve.sem, b_dve.done(b, f"u{c}"))
                dve.tensor_tensor(res[r][:, c, :], xs[r][:, c, :], res[r][:, c, :], ALU.mult).then_inc(b_dve.step(f"o{c}"), 1)

            def wo_task(b, k, uses):
                if k == 0:
                    dve.wait_ge(xb_in[b.parity], b.half_count(16, 16))
                    if b.shift(-1).exists:
                        dve.wait_ge(b_pe.sem, b_pe.done(b.shift(-1), "xnT1"))
                dve.wait_ge(b_pe.sem, b_pe.done(b, f"wo{k}"))
                for i in range(2):
                    j = 2 * k + i
                    dve.scalar_tensor_tensor(out=rows[:, j, :], in0=x_back[b.parity][:, j, :], scalar=r_keep[:, j:j + 1],
                                                        in1=uses[0].bank[:, i * D:(i + 1) * D], op0=ALU.mult, op1=ALU.add).then_inc(b_dve.step(f"r{j}"), 1)

            def ln2_task(b, k, uses):
                stats(b_dve, b, rows, st_b, mv_b, "st", "ag", "r")

            def x1_task(b, k, uses):
                xb = x_back[b.parity]
                dve.wait_ge(b_pool.sem, b_pool.done(b, "rb"))
                for j in range(TB):
                    centre(b_dve, rows, rows, mv_b, rs_b, j, f"t{j}")
                for j in range(TB):
                    dve.wait_ge(b_dve.sem, b_dve.done(b, f"t{j}"))
                    dve.tensor_tensor(xb[:, j, :], xb[:, j, :], rows[:, j, :], ALU.add).then_inc(b_dve.step(f"x{j}"), 1)
                stats(b_dve, b, xb, st_1, mv_1, "s1", "a1", "x")

            def xn_task(b, k, uses):
                dve.wait_ge(b_pool.sem, b_pool.done(b, "rb1"))
                for j in range(TB):
                    centre(b_dve, rows, x_back[b.parity], mv_1, rs_1, j, f"xn{j}")

            def xnT_task(b, t, uses):
                dve.wait_ge(b_act.sem, b_act.done(b, f"xnT{t}"))
                dve.tensor_tensor_scan(cumT[:, t, :], one[:, 0:1].broadcast_to([P, T]), uses[0].bank[:, :], 0.0,
                                                  ALU.mult, ALU.add).then_inc(b_dve.step(f"cum{t}"), 1)

            def logit_task(b, k, uses):
                flat_l = logits[:, :, :, :].rearrange("p a b k -> p (a b) k")
                dve.wait_ge(b_pe.sem, b_pe.done(b, "lg"))
                dve.tensor_tensor(flat_l, uses[0].bank[:, 0:TB * 2 * KE].rearrange("p (a k) -> p a k", k=KE),
                                             logit_bias[:, :, :, :].rearrange("p a b k -> p (a b) k"), ALU.add).then_inc(b_dve.step("lb"), 1)
                dve.wait_ge(b_dve.sem, b_dve.done(b, "lb"))
                dve.tensor_reduce(top[:, :], flat_l, AX.X, ALU.max).then_inc(b_dve.step("mx"), 1)
                dve.wait_ge(b_dve.sem, b_dve.done(b, "mx"))
                dve.tensor_tensor(flat_l, flat_l, top[:, :].rearrange("p (a o) -> p a o", o=1).broadcast_to([P, TB * 2, KE]),
                                             ALU.subtract).then_inc(b_dve.step("sub"), 1)

            def soft_task(b, k, uses):
                flat_l = logits[:, :, :, :].rearrange("p a b k -> p (a b) k")
                dve.wait_ge(b_act.sem, b_act.done(b, "ex"))
                dve.tensor_reduce(total[:, :], flat_l, AX.X, ALU.add).then_inc(b_dve.step("sm"), 1)
                dve.wait_ge(b_dve.sem, b_dve.done(b, "sm"))
                dve.tensor_tensor(total[:, :], total[:, :], n_valid[:, :, :].rearrange("p a b -> p (a b)"), ALU.mult).then_inc(b_dve.step("sn"), 1)
                dve.wait_ge(b_dve.sem, b_dve.done(b, "sn"))
                dve.reciprocal(total[:, :], total[:, :]).then_inc(b_dve.step("rc"), 1)
                dve.wait_ge(b_dve.sem, b_dve.done(b, "rc"))
                dve.tensor_copy(top[:, :], total[:, :]).then_inc(b_dve.step("wr"), 1)
                dve.tensor_tensor(gate[:, :, :].rearrange("p a (b k) -> p (a b) k", k=KE), flat_l,
                                             total[:, :].rearrange("p (a o) -> p a o", o=1).broadcast_to([P, TB * 2, KE]), ALU.mult).then_inc(b_dve.step("wa"), 1)

            def mm_task(b, u, uses):
                j, br = u // 2, u % 2
                pr = prod[u % 2]
                dve.wait_ge(l_act.sem, l_act.done(b, f"cum{u}"))
                dve.wait_ge(l_pe.sem, l_pe.done(b, f"xv{u}"))
                free = b if u >= 2 else b.shift(-1)
                if free.exists:
                    dve.wait_ge(l_pe.sem, l_pe.done(free, f"pt{(u - 2) % 8}"))
                dve.tensor_tensor(pr[:, :], uses[1].bank[:, :], cum_sb[u % 2][:, :], ALU.mult).then_inc(l_dve.step(f"pr{u}"), 1)
                dve.wait_ge(l_dve.sem, l_dve.done(b, f"pr{u}"))
                if u == 0:
                    dve.wait_ge(b_dve.sem, b_dve.done(b, "wa"))
                g = gate[:, j, br * KE:(br + 1) * KE].rearrange("p (k o) -> p k o", o=1).broadcast_to([P, KE, RK])
                pr3 = pr[:, :].rearrange("p (k r) -> p k r", k=KE)
                dve.tensor_tensor(pr3, pr3, g, ALU.mult).then_inc(l_dve.step(f"pw{u}"), 1)

            def fin1_task(b, k, uses):
                dve.wait_ge(l_act.sem, l_act.done(b, "out3"))
                stats(l_dve, b, o_rows, st_o, mv_o, "st", "ag", None)

            def fin2_task(b, k, uses):
                xb = x_back[b.parity]
                dve.wait_ge(l_pool.sem, l_pool.done(b, "rs"))
                for j in range(TB):
                    centre(l_dve, o_rows, o_rows, mv_o, rs_o, j, f"t{j}")
                for j in range(TB):
                    dve.wait_ge(l_dve.sem, l_dve.done(b, f"t{j}"))
                    dve.tensor_tensor(xb[:, j, :], xb[:, j, :], o_rows[:, j, :], ALU.add).then_inc(l_dve.step(f"x{j}"), 1)

            def scan_part(q, slot, k):
                if q.exists:
                    n, c = slot, k
                    dve.wait_ge(s_exp.sem, s_exp.done(q, f"{n},{c}"))
                    if c % 2 == 0:
                        dve.wait_ge(s_bx.sem, s_bx.done(q, f"{n},{c // 2}"))
                    if c == 0:
                        free = q if n >= 2 else q.shift(-1)
                        if free.exists:
                            dve.wait_ge(s_tr.sem, s_tr.done(free, f"{(n - 2) % NS},{TB - 1}"))
                    dve.tensor_tensor_scan(h[n % 2][:, c, :], decay[c % 2][:, :], bx[c // 2][:, c % 2, :], 0.0,
                                                       ALU.mult, ALU.add).then_inc(s_scan.step(f"{n},{c}"), 1)
                batch, n = (q, slot - 1) if slot else (q.shift(-1), NS - 1)
                if not batch.exists:
                    return
                dve.wait_ge(s_tr.sem, s_tr.done(batch, f"{n},{k}"))
                if n == 0:
                    if k == 0:
                        dve.wait_ge(f_act.sem, f_act.done(batch, "Ct"))
                        if batch.shift(-1).exists:
                            dve.wait_ge(b_pe.sem, b_pe.done(batch.shift(-1), "y3"))
                    ins = dve.tensor_scalar(yT[:, k, :], stateT[k % 2][:, :], C_tok[batch.parity][:, k, n:n + 1], None, ALU.mult)
                else:
                    dve.wait_ge(s_acc.sem, s_acc.done(batch, f"{n - 1},{k}"))
                    ins = dve.scalar_tensor_tensor(out=yT[:, k, :], in0=stateT[k % 2][:, :], scalar=C_tok[batch.parity][:, k, n:n + 1],
                                                   in1=yT[:, k, :], op0=ALU.mult, op1=ALU.add)
                ins.then_inc(s_acc.step(f"{n},{k}"), 1)

            walk(dve, prologue, {("F", "stats"): front_stats, ("F", "h"): h_task, ("F", "xs"): xs_task, ("F", "dt"): dt_task,
                                 ("B", "y"): y_task, ("B", "wo"): wo_task, ("B", "ln2"): ln2_task, ("B", "x1"): x1_task,
                                 ("B", "xn"): xn_task, ("B", "xnT"): xnT_task, ("B", "logit"): logit_task, ("B", "soft"): soft_task,
                                 ("L", "mm"): mm_task, ("L", "fin1"): fin1_task, ("L", "fin2"): fin2_task}, scan_part)


INPUTS = ["L0_attn_x", "L0_attn_norm_scale", "L0_attn_w_in", "L0_attn_conv_w", "L0_attn_conv_b", "L0_attn_A_log", "L0_attn_D",
          "L0_attn_w_xproj", "L0_attn_w_dt", "L0_attn_b_dt", "L0_attn_w_out", "L0_ffn_W_Q", "L0_ffn_W_K", "L0_ffn_W_O",
          "L0_ffn_W_inv", "L0_ffn_V_fwd", "L0_ffn_W_fwd", "L0_ffn_U_fwd", "L0_ffn_b_fwd", "L0_ffn_V_inv", "L0_ffn_W_inv_exp",
          "L0_ffn_U_inv", "L0_ffn_b_inv", "L0_ffn_router_w1", "L0_ffn_router_b1", "L0_ffn_router_w2", "L0_ffn_router_b2",
          "L0_ffn_alpha_bi", "L0_ffn_expert_bias"]


def kernel(**inputs):
    import numpy as np
    import concourse.bacc as bacc
    from concourse.bass_utils import run_bass_kernel_spmd

    nc = bacc.Bacc("TRN2", target_bir_lowering=False, num_devices=1)
    arrays, args = {}, []
    for name in INPUTS:
        a = np.ascontiguousarray(inputs[name])
        if a.ndim == 0:
            a = a.reshape(1)
        arrays[f"in_{name}"] = a
        args.append(nc.dram_tensor(f"in_{name}", a.shape, mybir.dt.from_np(a.dtype), kind="ExternalInput").ap())
    args.append(nc.dram_tensor("out_0", (NB, T, D), FP32, kind="ExternalOutput").ap())
    program(nc, *args)
    result = run_bass_kernel_spmd(nc, [arrays], core_ids=[0])
    return result.results[0]["out_0"]
```

```python
import concourse.bass as bass
from concourse import mybir
from contextlib import ExitStack

FP32 = mybir.dt.float32
ALU = mybir.AluOpType
ACT = mybir.ActivationFunctionType
AX = mybir.AxisListType

P = 128
NB, T, D = 16, 512, 256
DI, NS, RANK = 512, 16, 16
TAPS = 4
KE, RK = 8, 64
KR = KE * RK
TB, CT, DT = T // P, DI // P, D // P
NPROJ = RANK + 2 * NS
EPS = 1e-5
SLOTS = NS
BB_RING = 4
EXP_SET = "natural_log_exp_and_others"


class Batch:

    def __init__(self, const, turn=None):
        self.const, self.turn = const, turn
        self.parity = const % 2

    def shift(self, k):
        return Batch(self.const + k, self.turn)

    @property
    def exists(self):
        return self.turn is not None or 0 <= self.const < NB

    def count(self, per_batch, more):
        if self.turn is None:
            return self.const * per_batch + more
        return self.turn * (2 * per_batch) + (self.const * per_batch + more)

    def half_count(self, per_pair, more):
        if self.turn is None:
            return self.const // 2 * per_pair + more
        return self.turn * per_pair + (self.const // 2 * per_pair + more)

    def dram(self, ap):
        if self.turn is None:
            return ap[self.const]
        return ap[bass.ds(self.turn * 2 + self.const, 1)].rearrange("o p j d -> (o p) j d")


class Steps:

    def __init__(self, sem, names):
        self.sem, self.names = sem, names
        self.index = {n: i for i, n in enumerate(names)}
        self.next = 0

    def done(self, batch, name):
        return batch.count(len(self.names), self.index[name] + 1)

    def step(self, name):
        assert self.names[self.next] == name, (self.names[self.next], name)
        self.next = (self.next + 1) % len(self.names)
        return self.sem


BEATS = 8 * SLOTS
TIMETABLE = {
    ("B", "keep", "dve"): (255,),
    ("F", "st", "dve"): (7,),
    ("F", "ag", "dve"): (9,),
    ("F", "rs", "pool"): (15,),
    ("F", "h", "act"): (19,),
    ("F", "hT", "pe"): (26, 30),
    ("F", "hT", "act"): (28, 30),
    ("F", "x", "sp"): (89,),
    ("F", "xs", "pe"): (33, 34, 38, 43),
    ("F", "xs", "act"): (35, 36, 40, 45),
    ("F", "cvA", "dve"): (36, 36, 40, 44),
    ("F", "cvB", "dve"): (36, 36, 41, 46),
    ("F", "cvC", "dve"): (36, 38, 43, 47),
    ("F", "res", "pe"): (36, 41, 46, 68),
    ("F", "res", "act"): (39, 46, 50, 73),
    ("F", "silu", "act"): (75,),
    ("F", "proj", "pe"): (79,),
    ("F", "proj", "act"): (85,),
    ("F", "B", "sp"): (92,),
    ("F", "Ct", "pe"): (89,),
    ("F", "Ct", "act"): (95,),
    ("F", "dt", "pe"): (93, 93, 95, 106),
    ("F", "dt", "act"): (95, 98, 105, 112),
    ("F", "ex", "act"): (97, 99, 105, 116),
    ("F", "v", "pool"): (101, 106, 113, 119),
    ("F", "w", "pool"): (101, 111, 117, 123),
    ("F", "w2", "pool"): (106, 113, 122, 123),
    ("F", "d1", "dve"): (104, 114, 122, 123),
    ("F", "dx", "dve"): (109, 119, 122, 123),
    ("F", "row", "sp"): (107, 111, 119),
    ("B", "y", "pe"): (264, 264, 264, 264),
    ("B", "u", "dve"): (263, 263, 263, 268),
    ("B", "o", "dve"): (263, 269, 270, 270),
    ("B", "wo", "pe"): (275, 279, 283, 287),
    ("B", "r", "dve"): (281, 286, 288, 288),
    ("B", "st", "dve"): (290,),
    ("B", "ag", "dve"): (295,),
    ("B", "rb", "pool"): (304,),
    ("B", "t", "act"): (307,),
    ("B", "x1", "dve"): (310,),
    ("B", "st1", "dve"): (311,),
    ("B", "ag1", "dve"): (312,),
    ("B", "rb1", "pool"): (316,),
    ("B", "xn", "act"): (318,),
    ("B", "xnT", "pe"): (320, 321),
    ("B", "xnT", "act"): (323, 327),
    ("B", "cum", "dve"): (327, 329),
    ("B", "rt", "pe"): (327, 330, 331, 341),
    ("B", "rt", "act"): (334, 340, 342, 344),
    ("B", "gelu", "act"): (349,),
    ("B", "logit", "pe"): (350,),
    ("B", "lb", "dve"): (350,),
    ("B", "mx", "dve"): (353,),
    ("B", "sub", "dve"): (353,),
    ("B", "ex", "act"): (359,),
    ("B", "sm", "dve"): (358,),
    ("B", "sn", "dve"): (358,),
    ("B", "rc", "dve"): (358,),
    ("B", "wa", "dve"): (360,),
    ("B", "gT", "pe"): (374,),
    ("B", "gT", "act"): (378,),
    ("L", "cum", "pe"): (357, 364, 370, 377, 389, 395, 396, 427),
    ("L", "xv", "pe"): (358, 366, 372, 381, 395, 418, 430, 436),
    ("L", "cum", "act"): (366, 370, 377, 381, 390, 398, 407, 430),
    ("L", "pr", "dve"): (366, 370, 377, 379, 398, 422, 433, 437),
    ("L", "pt", "pe"): (369, 378, 379, 386, 415, 433, 438, 440),
    ("L", "pt", "act"): (370, 382, 387, 388, 422, 436, 439, 443),
    ("L", "out", "pe"): (382, 382, 399, 399, 437, 438, 443, 446),
    ("L", "out", "act"): (389, 410, 449, 454),
    ("L", "st", "dve"): (459,),
    ("L", "ag", "dve"): (472,),
    ("L", "rs", "pool"): (477,),
    ("L", "t", "act"): (490,),
    ("L", "x", "dve"): (491,),
    ("L", "store", "sp"): (472,),
}

FILLED_BY = {("F", "hT"): "hT", ("F", "xs"): "xs", ("F", "cvA"): "xs", ("F", "cvB"): "xs", ("F", "cvC"): "xs", ("F", "res"): "res",
             ("F", "proj"): "proj", ("F", "Ct"): "Ct", ("F", "dt"): "dt", ("B", "u"): "y", ("B", "r"): "wo", ("B", "xnT"): "xnT",
             ("B", "cum"): "xnT", ("B", "rt"): "rt", ("B", "lb"): "logit", ("B", "gT"): "gT",
             ("L", "cum"): "cum", ("L", "pr"): "xv", ("L", "pt"): "pt", ("L", "out"): "out"}
SHARE_A_BANK = {"wo": 2, "out": 2}


def rows_of_plan(engine):
    return sorted((beat, i, stage, task, k) for i, ((stage, task, who), beats) in enumerate(TIMETABLE.items()) if who == engine
                  for k, beat in enumerate(beats))


def plan(engine):
    beats = [[] for _ in range(BEATS)]
    for beat, _, stage, task, k in rows_of_plan(engine):
        beats[beat % BEATS].append((beat // BEATS, stage, task, k))
    return beats


def bank_numbers():
    numbers, n = {}, 0
    for tasks in plan("pe"):
        for periods, stage, task, k in tasks:
            if k % SHARE_A_BANK.get(task, 1) == 0:
                numbers[stage, task, k] = (periods, n)
                n += 1
    return numbers, n


def steps_of(engine, stage, tasks):
    return [name.format(k) for _, _, of, task, k in rows_of_plan(engine) if of == stage for name in tasks.get(task, [])]


def numbered(*names):
    return [f"{n}{i}" for n in names for i in range(TB)]


def program(nc, x, norm_scale, w_in, conv_w, conv_b, A_log, D_skip, w_xproj, w_dt, b_dt, w_out,
            W_Q, W_K, W_O, W_inv, V_fwd, W_fwd, U_fwd, b_fwd, V_inv, W_inv_exp, U_inv, b_inv,
            router_w1, router_b1, router_w2, router_b2, alpha_bi, expert_bias, out):
    ctx = ExitStack()
    with ctx:
        ctx.enter_context(nc.allow_non_contiguous_dma(reason="small weights, loaded once"))

        def sb(name, *shape):
            return ctx.enter_context(nc.sbuf_tensor(name, list(shape), FP32))

        def psum(name):
            return ctx.enter_context(nc.psum_tensor(name, [P, T], FP32))

        def sem(name):
            return ctx.enter_context(nc.semaphore(name))

        w_in_sb = sb("w_in_sb", P, DT, 2 * DI)
        w_out_sb = sb("w_out_sb", P, CT, D)
        w_xproj_sb = sb("w_xproj_sb", P, CT, NPROJ)
        w_dt_sb = sb("w_dt_sb", RANK, DI)
        decay_rate = sb("decay_rate", P, CT, NS)
        conv_w_sb = sb("conv_w_sb", P, CT, TAPS)
        conv_b_sb = sb("conv_b_sb", P, CT)
        skip_sb = sb("skip_sb", P, CT)
        b_dt_sb = sb("b_dt_sb", P, CT)
        norm_sb = sb("norm_sb", P, DT)
        b1_sb = sb("b1_sb", P, DT)
        q_to_expert = [sb(f"q_to_expert{br}", P, DT, KR) for br in range(2)]
        k_to_expert = [sb(f"k_to_expert{br}", P, DT, KR) for br in range(2)]
        q_to_router = [sb(f"q_to_router{br}", P, DT, D) for br in range(2)]
        expert_to_out = sb("expert_to_out", P, 8, D)
        w2T = sb("w2T", P, DT, KE)
        bias_to_out = sb("bias_to_out", 2 * KE, D)
        logit_bias = sb("logit_bias", P, TB, 2, KE)
        n_valid = sb("n_valid", P, TB, 2)
        alpha_sb = sb("alpha_sb", P, 1)
        minus_half = sb("minus_half", P, TB)
        minus_one = sb("minus_one", P, TB)
        one = sb("one", P, 1)
        ident = sb("ident", P, P)

        x_front = sb("x_front", P, TB, D)
        x_back = [sb(f"x_back{i}", P, TB, D) for i in range(2)]
        hT = sb("hT", P, DT, T)
        xs = [sb(f"xs{i}", P, CT, T) for i in range(2)]
        res = [sb(f"res{i}", P, CT, T) for i in range(2)]
        delta = [sb(f"delta{i}", P, CT, T) for i in range(2)]
        dx = [sb(f"dx{i}", P, CT, T) for i in range(2)]
        scratch = sb("scratch", P, 4, T)
        B_rows = sb("B_rows", P, BB_RING, T)
        bx = [sb(f"bx{i}", P, CT // 2, T) for i in range(2)]
        h = [sb(f"h{i}", P, CT, T) for i in range(2)]
        yT = sb("yT", P, TB, DI)
        rows = sb("rows", P, TB, D)
        xnT = sb("xnT", P, DT, T)
        cumT = sb("cumT", P, DT, T)
        cum_sb = [sb(f"cum_sb{i}", P, KR) for i in range(2)]
        prod = [sb(f"prod{i}", P, KR) for i in range(2)]
        prodT = sb("prodT", P, 8, P)
        o_rows = sb("o_rows", P, TB, D)
        projT = sb("projT", NPROJ, T)
        C_tok = [sb(f"C_tok{i}", P, TB, NS) for i in range(2)]
        st_f, st_b, st_1, st_o = (sb(f"st_{n}", P, TB, 6) for n in "fb1o")
        mv_f, mv_b, mv_1, mv_o = (sb(f"mv_{n}", P, TB, 2) for n in "fb1o")
        ve_f, ms_f, rs_f, r2_f = (sb(n, P, TB) for n in ("ve_f", "ms_f", "rs_f", "r2_f"))
        nm_f, nm_b, nm_1, nm_o = (sb(f"nm_{n}", P, TB) for n in "fb1o")
        r_x0 = [sb(f"r_x0{i}", P, TB) for i in range(2)]
        r_keep = sb("r_keep", P, TB)
        ve_b, rs_b, ve_1, rs_1, ve_o, rs_o = (sb(n, P, TB) for n in ("ve_b", "rs_b", "ve_1", "rs_1", "ve_o", "rs_o"))
        logits = sb("logits", P, TB, 2, KE)
        top = sb("top", P, TB * 2)
        total = sb("total", P, TB * 2)
        gate = sb("gate", P, TB, 2 * KE)
        gateT = sb("gateT", 2 * KE, T)

        B_dram = nc.dram_tensor("B_scratch", [2, NS, T], FP32).ap()

        decay = [psum(f"decay{i}") for i in range(2)]
        stateT = [psum(f"stateT{i}") for i in range(2)]
        bank = [psum(f"bank{i}") for i in range(4)]

        f_pe = Steps(sem("f_pe"), steps_of("pe", "F", {"hT": ["hT{}"], "xs": ["xs{}"], "res": ["res{}"], "proj": ["proj"],
                                                       "Ct": ["Ct"], "dt": ["dt{}"]}))
        f_act = Steps(sem("f_act"), steps_of("act", "F", {"h": numbered("h"), "hT": ["hT{}"], "xs": ["cv{}"], "res": ["res{}"], "silu": ["silux", "silur"],
                                                          "proj": ["proj"], "Ct": ["Ct"], "dt": ["ab{}", "rl{}"], "ex": ["ex{}", "ln{}"]}))
        f_dve = Steps(sem("f_dve"), steps_of("dve", "F", {"st": numbered("st"), "ag": numbered("ag"),
                                                          "cvA": ["cvA{}"], "cvB": ["cvB{}"], "cvC": ["cvC{}"], "d1": ["d1{}"], "dx": ["dx{}"]}))
        f_pool = Steps(sem("f_pool"), steps_of("pool", "F", {"rs": ["ve", "r1", "ms", "mr", "me", "r2", "rs", "ng", "nm"], "v": ["v{}"], "w": ["u{}", "w{}"], "w2": ["w2{}"]}))
        s_exp = Steps(sem("s_exp"), [f"{n},{c}" for n in range(NS) for c in range(CT)])
        s_bx = Steps(sem("s_bx"), [f"{n},{c}" for n in range(NS) for c in range(2)])
        s_scan = Steps(sem("s_scan"), [f"{n},{c}" for n in range(NS) for c in range(CT)])
        s_tr = Steps(sem("s_tr"), [f"{n},{c}" for n in range(NS) for c in range(TB)])
        s_acc = Steps(sem("s_acc"), [f"{n},{c}" for n in range(NS) for c in range(TB)])
        b_pe = Steps(sem("b_pe"), steps_of("pe", "B", {"y": ["y{}"], "wo": ["wo{}"], "xnT": ["xnT{}"], "rt": ["rt{}"],
                                                       "logit": ["lg"], "gT": ["gT"]}))
        b_act = Steps(sem("b_act"), steps_of("act", "B", {"t": numbered("t"), "xn": numbered("xn"), "xnT": ["xnT{}"], "rt": ["rt{}"], "gelu": ["gelu"], "ex": ["ex"], "gT": ["gT"]}))
        b_dve = Steps(sem("b_dve"), steps_of("dve", "B", {"keep": ["keep"], "u": ["u{}"], "o": ["o{}"], "r": ["r{}"], "st": numbered("st"),
                                                          "ag": numbered("ag"), "x1": ["x1"], "st1": numbered("s1"), "ag1": numbered("a1"),
                                                          "cum": ["cum{}"], "lb": ["lb"], "mx": ["mx"], "sub": ["sub"], "sm": ["sm"],
                                                          "sn": ["sn"], "rc": ["rc"], "wa": ["wa"]}))
        b_pool = Steps(sem("b_pool"), ["ve", "rb", "ng", "nm", "ve1", "rb1", "ng1", "nm1"])
        l_pe = Steps(sem("l_pe"), steps_of("pe", "L", {"cum": ["cum{}"], "xv": ["xv{}"], "pt": ["pt{}"], "out": ["out{}"]}))
        l_act = Steps(sem("l_act"), steps_of("act", "L", {"cum": ["cum{}"], "pt": ["pt{}"], "out": ["out{}"], "t": numbered("t")}))
        l_dve = Steps(sem("l_dve"), steps_of("dve", "L", {"pr": ["pr{}"], "st": numbered("st"), "ag": numbered("ag"), "x": ["x"]}))
        l_pool = Steps(sem("l_pool"), ["ve", "rs", "ng", "nm"])
        xf_in = sem("xf_in")
        xb_in = [sem(f"xb_in{i}") for i in range(2)]
        stored = [sem(f"stored{i}") for i in range(2)]
        B_out = sem("B_out")
        B_in = [sem(f"B_in{i}") for i in range(BB_RING)]
        w_ld = sem("w_ld")
        w_pe = sem("w_pe")
        w_act = sem("w_act")
        w_dve = sem("w_dve")
        w_pool = sem("w_pool")
        passed = {name: sem(f"passed_{name}") for name in ("sp", "pool", "pe", "act", "dve")}

        def reading_ends(stage, task, k):
            if stage == "F":
                return {"hT": (f_act, f"hT{k}"), "xs": (f_dve, f"cvC{k}"), "res": (f_act, f"res{k}"),
                        "proj": (f_act, "proj"), "Ct": (f_act, "Ct"), "dt": (f_act, f"rl{k}")}[task]
            if stage == "B":
                return {"y": (b_dve, f"u{k}"), "wo": (b_dve, f"r{k + 1}"), "xnT": (b_dve, f"cum{k}"),
                        "rt": (b_act, f"rt{k}"), "logit": (b_dve, "lb"), "gT": (b_act, "gT")}[task]
            return {"cum": (l_act, f"cum{k}"), "xv": (l_dve, f"pr{k}"), "pt": (l_act, f"pt{k}"), "out": (l_act, f"out{k // 2}")}[task]

        numbers, uses_a_period = bank_numbers()

        class Use:

            def __init__(self, tensor, sem, free_at):
                self.bank, self.sem, self.free_at = tensor, sem, free_at

        def bank_of(stage, task, k, batch):
            periods, use = numbers[stage, task, k - k % SHARE_A_BANK.get(task, 1)]
            return (uses_a_period * ((batch.const + 1 + periods) % 2) + use) % 4

        def walk(engine, name, prologue, tasks, scan_part):
            beats = plan(name)
            held = [None] * 4

            def run(stage, task, k, batch):
                use = None
                if name == "pe":
                    at = bank_of(stage, task, k, batch)
                    before = held[at]
                    use = Use(bank[at], before[0].sem, before[0].done(before[1], before[2])) if before else Use(bank[at], w_act, 1)
                    if k % SHARE_A_BANK.get(task, 1) == 0:
                        steps, step = reading_ends(stage, task, k)
                        held[at] = (steps, batch, step)
                elif (stage, task) in FILLED_BY:
                    filler = FILLED_BY[stage, task]
                    use = Use(bank[bank_of(stage, filler, 2 * k if task == "out" else k, batch)], None, None)
                tasks[stage, task](batch, k, use)

            def period(q):
                for at in range(BEATS):
                    scan_part(q, at // 8, at % 8)
                    for periods, stage, task, k in beats[at]:
                        batch = q.shift(1 - periods)
                        if batch.exists:
                            run(stage, task, k, batch)

            prologue()
            for q in (-1, 0, 1):
                period(Batch(q))
            turns = (NB - 4) // 2
            with engine.Fori(0, turns) as turn:
                if name == "pe":
                    held[:] = [(s, Batch(b.const, turn), n) for s, b, n in held]
                start = list(held)
                period(Batch(2, turn))
                period(Batch(3, turn))
                if name == "pe":
                    for (s, b, n), (s2, b2, n2) in zip(start, held):
                        assert s is s2 and n == n2 and b2.const == b.const + 2
            held[:] = [h and (h[0], Batch(h[1].const + 2 * (turns - 1)), h[2]) for h in held]
            for q in range(NB - 2, NB + 3):
                period(Batch(q))

        stage_V = [h[0][:, 0:2, :], h[0][:, 2:4, :]]
        stage_W = [h[1][:, 0:2, :], h[1][:, 2:4, :]]
        stage_U = [bx[0][:, :, :], bx[1][:, :, :]]
        raw = yT[:, :, :].rearrange("p a (b c) -> p (a b) c", b=2)
        wq_raw, wk_raw, winv_raw, wo_raw = (raw[:, 2 * i:2 * i + 2, :] for i in range(4))
        r1_raw = o_rows[:, 0:2, :]
        r2_raw = o_rows[0:KE, 2, :]
        b_raw = o_rows[0:2 * KE, 3, :]
        tr = scratch[:, :, :].rearrange("p a (b c) -> p (a b) c", b=2)
        winvT, r1T, woT, wqiT = (tr[:, 2 * i:2 * i + 2, :] for i in range(4))
        wkiT = cumT[:, 0, :].rearrange("p (a b) -> p a b", a=2)
        bT = cumT[:, 1, 0:2 * 2 * KE].rearrange("p (a b) -> p a b", a=2)
        bias_raw = logits
        block = ctx.enter_context(nc.Block())

        N_WEIGHTS = [0]

        @block.sync
        def _(sp):
            def load(dst, src):
                sp.dma_start(dst, src).then_inc(w_ld, 16)
                N_WEIGHTS[0] += 1

            def rows_of(ap):
                return ap.rearrange("b (j p) d -> b p j d", p=P)

            x_rows, out_rows = rows_of(x), rows_of(out)

            def prologue():
                sp.dma_start(x_front[:, :, :], x_rows[0]).then_inc(xf_in, 16)
                square = "(t p) n -> p t n"
                load(wq_raw, W_Q.rearrange(square, p=P))
                load(wk_raw, W_K.rearrange(square, p=P))
                load(winv_raw, W_inv.rearrange(square, p=P))
                load(wo_raw, W_O.rearrange(square, p=P))
                load(r1_raw, router_w1.rearrange(square, p=P))
                load(r2_raw, router_w2)
                load(o_rows[0:KE, 3, :], b_fwd)
                load(o_rows[KE:2 * KE, 3, :], b_inv)
                for staged, weights in ((stage_V, (V_fwd, W_inv_exp)), (stage_W, (W_fwd, V_inv)), (stage_U, (U_fwd, U_inv))):
                    for br in range(2):
                        for t in range(DT):
                            load(staged[br][:, t, :].rearrange("p (k r) -> p k r", k=KE),
                                 weights[br][:, t * P:(t + 1) * P, :].rearrange("k p r -> p k r"))
                load(w_in_sb[:, :, :], w_in.rearrange(square, p=P))
                load(w_out_sb[:, :, :], w_out.rearrange(square, p=P))
                load(w_xproj_sb[:, :, :], w_xproj.rearrange(square, p=P))
                load(w_dt_sb[:, :], w_dt)
                load(decay_rate[:, :, :], A_log.rearrange(square, p=P))
                for c in range(CT):
                    load(conv_w_sb[:, c, :], conv_w[:, 0, c * P:(c + 1) * P].rearrange("k p -> p k"))
                for dst, src in ((conv_b_sb, conv_b), (skip_sb, D_skip), (b_dt_sb, b_dt), (norm_sb, norm_scale), (b1_sb, router_b1)):
                    load(dst[:, :], src.rearrange("(t p) -> p t", p=P))
                load(alpha_sb[:, :], alpha_bi.partition_broadcast(P))
                load(bias_raw[:, 0, 0, :], router_b2.rearrange("(o k) -> o k", o=1).partition_broadcast(P).rearrange("p o k -> p (o k)"))
                load(bias_raw[:, 0, 1, :], expert_bias.rearrange("(o k) -> o k", o=1).partition_broadcast(P).rearrange("p o k -> p (o k)"))

            def row_of_B(batch, n):
                back = n - BB_RING
                free = batch if back >= 0 else batch.shift(-1)
                if free.exists:
                    sp.wait_ge(s_bx.sem, s_bx.done(free, f"{back % NS},1"))
                if n == 0:
                    sp.sem_inc(passed["sp"], 1)
                    sp.wait_ge(B_out, batch.count(16, 16))
                sp.dma_start(B_rows[:, n % BB_RING, :],
                             B_dram[batch.parity, n:n + 1, :].partition_broadcast(P).rearrange("p o t -> p (o t)")
                             ).then_inc(B_in[n % BB_RING], 16)

            def load_x_front(batch, k, use):
                nxt = batch.shift(1)
                if nxt.turn is None and nxt.const >= NB:
                    return
                sp.wait_ge(f_pe.sem, f_pe.done(batch, "hT1"))
                sp.sem_inc(passed["sp"], 1)
                sp.dma_start(x_front[:, :, :], nxt.dram(x_rows)).then_inc(xf_in, 16)

            def write_B(batch, k, use):
                sp.wait_ge(f_act.sem, f_act.done(batch, "proj"))
                sp.dma_start(B_dram[batch.parity], projT[RANK:RANK + NS, :]).then_inc(B_out, 16)

            def first_rows(batch, k, use):
                row_of_B(batch, k)

            def load_x_back(batch):
                if batch.turn is not None or batch.const >= 2:
                    sp.wait_ge(stored[batch.parity], batch.half_count(16, 0))
                    sp.sem_inc(passed["sp"], 1)
                sp.dma_start(x_back[batch.parity][:, :, :], batch.dram(x_rows)).then_inc(xb_in[batch.parity], 16)

            def store(batch, k, use):
                sp.wait_ge(l_dve.sem, l_dve.done(batch, "x"))
                sp.sem_inc(passed["sp"], 1)
                sp.dma_start(batch.dram(out_rows), x_back[batch.parity][:, :, :]).then_inc(stored[batch.parity], 16)

            def scan_part(q, slot, beat):
                if beat == 0 and q.exists:
                    if slot + BB_RING - 1 < NS:
                        row_of_B(q, slot + BB_RING - 1)
                    if slot == 12:
                        load_x_back(q)

            walk(sp, "sp", prologue, {("F", "x"): load_x_front,
                                ("F", "B"): write_B, ("F", "row"): first_rows, ("L", "store"): store}, scan_part)
            for i in range(2):
                sp.wait_ge(stored[i], NB // 2 * 16)

        @block.gpsimd
        def _(pool):
            def prologue():
                chain = [0]

                def link(ins):
                    chain[0] += 1
                    ins.then_inc(w_pool, 1)
                    pool.wait_ge(w_pool, chain[0])

                link(pool.memset(ident[:, :], 0.0))
                link(pool.affine_select(out=ident[:, :], in_=ident[:, :], compare_op=ALU.not_equal, fill=1.0,
                                        base=0, pattern=[[-1, P]], channel_multiplier=1))
                link(pool.memset(minus_half[:, :], -0.5))
                link(pool.memset(minus_one[:, :], -1.0))
                link(pool.memset(one[:, :], 1.0))
                link(pool.iota(n_valid[:, :, :], pattern=[[P, TB], [0, 2]], base=1, channel_multiplier=1,
                               allow_small_or_imprecise_dtypes=True))

            def rstd(steps, batch, mv, ve, rs, nm, names):
                pool.tensor_scalar(ve[:, :], mv[:, :, 1], EPS, None, ALU.add).then_inc(steps.step(names[0]), 1)
                pool.wait_ge(steps.sem, steps.done(batch, names[0]))
                pool.tensor_tensor(rs[:, :], ve[:, :], minus_half[:, :], ALU.pow).then_inc(steps.step(names[1]), 1)
                if nm is not None:
                    pool.tensor_tensor(nm[:, :], mv[:, :, 0], minus_one[:, :], ALU.mult).then_inc(steps.step(names[2]), 1)
                    pool.wait_ge(steps.sem, steps.done(batch, names[2]))
                    pool.tensor_tensor(nm[:, :], nm[:, :], rs[:, :], ALU.mult).then_inc(steps.step(names[3]), 1)

            def front_rstd(b, k, use):
                pool.wait_ge(f_dve.sem, f_dve.done(b, "ag3"))
                pool.sem_inc(passed["pool"], 1)
                r = r_x0[b.parity]
                rstd(f_pool, b, mv_f, ve_f, r, None, ("ve", "r1"))
                pool.wait_ge(f_pool.sem, f_pool.done(b, "r1"))
                pool.tensor_tensor(ms_f[:, :], mv_f[:, :, 1], r[:, :], ALU.mult).then_inc(f_pool.step("ms"), 1)
                pool.wait_ge(f_pool.sem, f_pool.done(b, "ms"))
                pool.tensor_tensor(ms_f[:, :], ms_f[:, :], r[:, :], ALU.mult).then_inc(f_pool.step("mr"), 1)
                pool.wait_ge(f_pool.sem, f_pool.done(b, "mr"))
                pool.sem_inc(passed["pool"], 1)
                pool.tensor_scalar(ms_f[:, :], ms_f[:, :], EPS, None, ALU.add).then_inc(f_pool.step("me"), 1)
                pool.wait_ge(f_pool.sem, f_pool.done(b, "me"))
                pool.tensor_tensor(r2_f[:, :], ms_f[:, :], minus_half[:, :], ALU.pow).then_inc(f_pool.step("r2"), 1)
                pool.wait_ge(f_pool.sem, f_pool.done(b, "r2"))
                pool.tensor_tensor(rs_f[:, :], r2_f[:, :], r[:, :], ALU.mult).then_inc(f_pool.step("rs"), 1)
                pool.tensor_tensor(nm_f[:, :], mv_f[:, :, 0], minus_one[:, :], ALU.mult).then_inc(f_pool.step("ng"), 1)
                pool.wait_ge(f_pool.sem, f_pool.done(b, "ng"))
                pool.tensor_tensor(nm_f[:, :], nm_f[:, :], rs_f[:, :], ALU.mult).then_inc(f_pool.step("nm"), 1)

            def v_task(b, c, use):
                e, v = scratch[:, c % 2, :], scratch[:, 2 + c % 2, :]
                if c >= 2:
                    pool.wait_ge(f_dve.sem, f_dve.done(b, f"d1{c - 2}"))
                pool.wait_ge(f_act.sem, f_act.done(b, f"ex{c}"))
                pool.sem_inc(passed["pool"], 1)
                pool.tensor_scalar(v, e, 1.0, None, ALU.add).then_inc(f_pool.step(f"v{c}"), 1)

            def w_task(b, c, use):
                e, v = scratch[:, c % 2, :], scratch[:, 2 + c % 2, :]
                pool.wait_ge(f_pool.sem, f_pool.done(b, f"v{c}"))
                pool.sem_inc(passed["pool"], 1)
                pool.tensor_scalar(v, v, -1.0, None, ALU.add).then_inc(f_pool.step(f"u{c}"), 1)
                pool.wait_ge(f_pool.sem, f_pool.done(b, f"u{c}"))
                pool.tensor_tensor(v, e, v, ALU.subtract).then_inc(f_pool.step(f"w{c}"), 1)

            def w2_task(b, c, use):
                v = scratch[:, 2 + c % 2, :]
                pool.wait_ge(f_pool.sem, f_pool.done(b, f"w{c}"))
                pool.tensor_tensor(v, v, dx[b.parity][:, c, :], ALU.add).then_inc(f_pool.step(f"w2{c}"), 1)

            def back_rstd(b, k, use):
                pool.wait_ge(b_dve.sem, b_dve.done(b, "ag3"))
                pool.sem_inc(passed["pool"], 1)
                rstd(b_pool, b, mv_b, ve_b, rs_b, nm_b, ("ve", "rb", "ng", "nm"))

            def x1_rstd(b, k, use):
                pool.wait_ge(b_dve.sem, b_dve.done(b, "a13"))
                pool.sem_inc(passed["pool"], 1)
                rstd(b_pool, b, mv_1, ve_1, rs_1, nm_1, ("ve1", "rb1", "ng1", "nm1"))

            def out_rstd(b, k, use):
                pool.wait_ge(l_dve.sem, l_dve.done(b, "ag3"))
                pool.sem_inc(passed["pool"], 1)
                rstd(l_pool, b, mv_o, ve_o, rs_o, nm_o, ("ve", "rs", "ng", "nm"))

            def scan_part(q, n, beat):
                if not q.exists or beat % 4:
                    return
                half = beat // 4
                if n == 0 and half == 0:
                    pool.wait_ge(f_dve.sem, f_dve.done(q, "dx3"))
                if half == 0:
                    pool.wait_ge(B_in[n % BB_RING], q.count(16 * NS // BB_RING, 16 * (n // BB_RING + 1)))
                free = q if n else q.shift(-1)
                if free.exists:
                    pool.wait_ge(s_scan.sem, s_scan.done(free, f"{(n - 1) % NS},{2 * half + 1}"))
                row = B_rows[:, n % BB_RING, :].rearrange("p (o t) -> p o t", o=1).broadcast_to([P, CT // 2, T])
                pool.tensor_tensor(bx[half][:, :, :], dx[q.parity][:, 2 * half:2 * half + 2, :], row, ALU.mult).then_inc(s_bx.step(f"{n},{half}"), 1)

            walk(pool, "pool", prologue, {("F", "rs"): front_rstd, ("F", "v"): v_task, ("F", "w"): w_task, ("F", "w2"): w2_task, ("B", "rb"): back_rstd,
                                  ("B", "rb1"): x1_rstd, ("L", "rs"): out_rstd}, scan_part)

        def square_T(raw_w):
            return [(a * D + f * P, a * D + (f + 1) * P, raw_w[:, f, a * P:(a + 1) * P], None) for a in range(DT) for f in range(DT)]

        def product(lhs, rhs):
            return [(m * D, (m + 1) * D, lhs[:, t, m * P:(m + 1) * P], rhs[:, t, :], t == 0, t == DT - 1)
                    for m in range(DT) for t in range(DT)]

        jobs = []

        def job(mms, dst, width, depends, scaled=None, parts=P):
            jobs.append((mms, dst, width, depends, scaled, parts))
            return len(jobs) - 1

        flat = lambda ap: ap.rearrange("p a b -> p (a b)")
        j_winvT = job(square_T(winv_raw), flat(winvT), 2 * D, -1)
        j_r1T = job(square_T(r1_raw), flat(r1T), 2 * D, -1)
        j_woT = job(square_T(wo_raw), flat(woT), 2 * D, -1)
        job([(t * KE, (t + 1) * KE, r2_raw[:, t * P:(t + 1) * P], None) for t in range(DT)], flat(w2T), 2 * KE, -1)
        j_bT = job([(t * 2 * KE, (t + 1) * 2 * KE, b_raw[:, t * P:(t + 1) * P], None) for t in range(DT)], bT, 4 * KE, -1, "b")
        j_wqiT = job(product(winvT, wq_raw), flat(wqiT), 2 * D, j_winvT)
        j_wkiT = job(product(winvT, wk_raw), flat(wkiT), 2 * D, j_winvT)
        for br in range(2):
            for lhs, rhs, dst, dep in ((wq_raw if br == 0 else wqiT, stage_V[br], q_to_expert[br], j_wqiT),
                                       (wk_raw if br == 0 else wkiT, stage_W[br], k_to_expert[br], j_wkiT)):
                for m in range(DT):
                    job([(0, KR, lhs[:, t, m * P:(m + 1) * P], rhs[:, t, :], t == 0, t == DT - 1) for t in range(DT)],
                        dst[:, m, :], KR, dep)
            job(product(wq_raw if br == 0 else wqiT, r1T), flat(q_to_router[br]), 2 * D, j_wkiT)
        for br in range(2):
            for pair in range(2):
                mms = []
                for i in range(2):
                    kt = 2 * pair + i
                    mms += [(i * D, (i + 1) * D, stage_U[br][:, t, kt * P:(kt + 1) * P], woT[:, t, :], t == 0, t == DT - 1) for t in range(DT)]
                k0 = 4 * br + 2 * pair
                job(mms, flat(expert_to_out[:, k0:k0 + 2, :]), 2 * D, j_woT, "all" if br else None)
        job([(0, D, bT[:, t, :], woT[:, t, :], t == 0, t == DT - 1) for t in range(DT)], bias_to_out[:, :], D, j_bT, None, 2 * KE)
        N_ACT = [0]

        @block.tensor
        def _(pe):
            def prologue():
                pe.wait_ge(w_ld, 16 * N_WEIGHTS[0])
                pe.wait_ge(w_pool, 2)
                for i, (mms, dst, width, depends, scaled, parts) in enumerate(jobs):
                    if max(i - 3, depends + 1) > 0:
                        pe.wait_ge(w_act, max(i - 3, depends + 1))
                    for mm in mms:
                        if mm[3] is None:
                            src = mm[2]
                            k = src.shape[0]
                            last = pe.transpose(bank[i % 4][:, mm[0]:mm[1]], src, ident[0:k, 0:k])
                        else:
                            last = pe.matmul(bank[i % 4][0:parts, mm[0]:mm[1]], mm[2], mm[3], start=mm[4], stop=mm[5])
                    last.then_inc(w_pe, 1)
                pe.wait_ge(w_act, len(jobs))

            def matmuls(out_ap, pairs):
                for i, (lhsT, rhs) in enumerate(pairs):
                    last = pe.matmul(out_ap, lhsT, rhs, start=(i == 0), stop=(i == len(pairs) - 1))
                return last

            def rows_T(b, t, use, src, steps, name):
                pe.wait_ge(use.sem, use.free_at)
                for j in range(TB):
                    last = pe.transpose(use.bank[:, j * P:(j + 1) * P], src[:, j, t * P:(t + 1) * P], ident[:, :])
                last.then_inc(steps.step(name), 1)

            def hT_task(b, t, use):
                pe.wait_ge(f_act.sem, f_act.done(b, "h3"))
                rows_T(b, t, use, x_front, f_pe, f"hT{t}")

            def xs_task(b, c, use):
                if c == 0:
                    pe.wait_ge(f_act.sem, f_act.done(b, "hT1"))
                pe.wait_ge(use.sem, use.free_at)
                matmuls(use.bank[:, :], [(w_in_sb[:, t, c * P:(c + 1) * P], hT[:, t, :]) for t in range(DT)]).then_inc(f_pe.step(f"xs{c}"), 1)

            def res_task(b, c, use):
                pe.wait_ge(use.sem, use.free_at)
                matmuls(use.bank[:, :], [(w_in_sb[:, t, DI + c * P:DI + (c + 1) * P], hT[:, t, :]) for t in range(DT)]).then_inc(f_pe.step(f"res{c}"), 1)

            def proj_task(b, k, use):
                pe.wait_ge(f_act.sem, f_act.done(b, "silux"))
                pe.wait_ge(use.sem, use.free_at)
                matmuls(use.bank[0:NPROJ, :], [(w_xproj_sb[:, c, :], xs[b.parity][:, c, :]) for c in range(CT)]).then_inc(f_pe.step("proj"), 1)

            def Ct_task(b, k, use):
                pe.wait_ge(use.sem, use.free_at)
                pe.wait_ge(f_act.sem, f_act.done(b, "proj"))
                pe.sem_inc(passed["pe"], 1)
                for j in range(TB):
                    last = pe.transpose(use.bank[:, j * NPROJ:(j + 1) * NPROJ], projT[:, j * P:(j + 1) * P], ident[0:NPROJ, 0:NPROJ])
                last.then_inc(f_pe.step("Ct"), 1)

            def dt_task(b, c, use):
                if c == 0:
                    pe.wait_ge(f_act.sem, f_act.done(b, "proj"))
                pe.wait_ge(use.sem, use.free_at)
                matmuls(use.bank[:, :], [(w_dt_sb[:, c * P:(c + 1) * P], projT[0:RANK, :])]).then_inc(f_pe.step(f"dt{c}"), 1)

            def y_task(b, c, use):
                if c == 0:
                    pe.wait_ge(s_acc.sem, s_acc.done(b, f"{NS - 1},{TB - 1}"))
                pe.wait_ge(use.sem, use.free_at)
                for j in range(TB):
                    last = pe.transpose(use.bank[:, j * P:(j + 1) * P], yT[:, j, c * P:(c + 1) * P], ident[:, :])
                last.then_inc(b_pe.step(f"y{c}"), 1)

            def wo_task(b, k, use):
                if k == 0:
                    pe.wait_ge(b_dve.sem, b_dve.done(b, "o3"))
                if k % 2 == 0:
                    pe.wait_ge(use.sem, use.free_at)
                matmuls(use.bank[:, k % 2 * D:(k % 2 + 1) * D],
                        [(res[b.parity][:, c, k * P:(k + 1) * P], w_out_sb[:, c, :]) for c in range(CT)]).then_inc(b_pe.step(f"wo{k}"), 1)

            def xnT_task(b, t, use):
                pe.wait_ge(b_act.sem, b_act.done(b, "xn3"))
                rows_T(b, t, use, rows, b_pe, f"xnT{t}")

            def rt_task(b, k, use):
                br, m = k // 2, k % 2
                if k == 0:
                    pe.wait_ge(b_act.sem, b_act.done(b, "xnT1"))
                pe.wait_ge(use.sem, use.free_at)
                matmuls(use.bank[:, :], [(q_to_router[br][:, t, m * P:(m + 1) * P], xnT[:, t, :]) for t in range(DT)]).then_inc(b_pe.step(f"rt{k}"), 1)

            def logit_task(b, k, use):
                pe.wait_ge(b_act.sem, b_act.done(b, "gelu"))
                pe.wait_ge(use.sem, use.free_at)
                for j in range(TB):
                    for br in range(2):
                        at = (j * 2 + br) * KE
                        last = matmuls(use.bank[:, at:at + KE],
                                       [(scratch[:, 2 * br + m, j * P:(j + 1) * P], w2T[:, m, :]) for m in range(DT)])
                last.then_inc(b_pe.step("lg"), 1)

            def gateT_task(b, k, use):
                pe.wait_ge(b_dve.sem, b_dve.done(b, "wa"))
                pe.wait_ge(use.sem, use.free_at)
                for j in range(TB):
                    last = pe.transpose(use.bank[0:2 * KE, j * P:(j + 1) * P], gate[:, j, :], ident[:, :])
                last.then_inc(b_pe.step("gT"), 1)

            def cum_task(b, u, use):
                j, br = u // 2, u % 2
                if u == 0:
                    pe.wait_ge(b_dve.sem, b_dve.done(b, "cum1"))
                pe.wait_ge(use.sem, use.free_at)
                matmuls(use.bank[:, :], [(cumT[:, t, j * P:(j + 1) * P], k_to_expert[br][:, t, :]) for t in range(DT)]).then_inc(l_pe.step(f"cum{u}"), 1)

            def xv_task(b, u, use):
                j, br = u // 2, u % 2
                pe.wait_ge(use.sem, use.free_at)
                matmuls(use.bank[:, :], [(xnT[:, t, j * P:(j + 1) * P], q_to_expert[br][:, t, :]) for t in range(DT)]).then_inc(l_pe.step(f"xv{u}"), 1)

            def pt_task(b, u, use):
                pe.wait_ge(l_dve.sem, l_dve.done(b, f"pr{u}"))
                pe.wait_ge(use.sem, use.free_at)
                for i in range(KR // P):
                    last = pe.transpose(use.bank[:, i * P:(i + 1) * P], prod[u % 2][:, i * P:(i + 1) * P], ident[:, :])
                last.then_inc(l_pe.step(f"pt{u}"), 1)

            def out_task(b, u, use):
                j, br = u // 2, u % 2
                pe.wait_ge(l_act.sem, l_act.done(b, f"pt{u}"))
                if br == 0:
                    pe.wait_ge(use.sem, use.free_at)
                if u == 1:
                    pe.wait_ge(b_act.sem, b_act.done(b, "gT"))
                for i in range(4):
                    last = pe.matmul(use.bank[:, 0:D], prodT[:, 4 * br + i, :], expert_to_out[:, 4 * br + i, :], start=(br == 0 and i == 0), stop=False)
                if br:
                    last = pe.matmul(use.bank[:, 0:D], gateT[:, j * P:(j + 1) * P], bias_to_out[:, :], start=False, stop=True)
                last.then_inc(l_pe.step(f"out{u}"), 1)

            def scan_part(q, slot, beat):
                if beat % 2:
                    return
                j = beat // 2
                batch, n = (q, slot - 1) if slot else (q.shift(-1), NS - 1)
                if not batch.exists:
                    return
                if j == 0:
                    pe.wait_ge(s_scan.sem, s_scan.done(batch, f"{n},{CT - 1}"))
                back = n * TB + j - 2
                free = batch if back >= 0 else batch.shift(-1)
                if free.exists:
                    pe.wait_ge(s_acc.sem, s_acc.done(free, f"{back % (NS * TB) // TB},{back % TB}"))
                for c in range(CT):
                    last = pe.transpose(stateT[j % 2][:, c * P:(c + 1) * P], h[n % 2][:, c, j * P:(j + 1) * P], ident[:, :])
                last.then_inc(s_tr.step(f"{n},{j}"), 1)

            walk(pe, "pe", prologue, {("F", "hT"): hT_task, ("F", "xs"): xs_task, ("F", "res"): res_task, ("F", "proj"): proj_task,
                                ("F", "Ct"): Ct_task, ("F", "dt"): dt_task, ("B", "y"): y_task, ("B", "wo"): wo_task, ("B", "xnT"): xnT_task,
                                ("B", "rt"): rt_task, ("B", "logit"): logit_task, ("B", "gT"): gateT_task,
                                ("L", "cum"): cum_task, ("L", "xv"): xv_task, ("L", "pt"): pt_task, ("L", "out"): out_task}, scan_part)

        @block.scalar
        def _(act):
            def prologue():
                act.preload_act_table_set(EXP_SET)
                act.wait_ge(w_ld, 16 * N_WEIGHTS[0])
                for i, (mms, dst, width, depends, scaled, parts) in enumerate(jobs):
                    act.wait_ge(w_pe, i + 1)
                    src = bank[i % 4][0:parts, 0:width]
                    if scaled == "b":
                        both = src.rearrange("p (a b) -> p a b", a=2)
                        act.activation(dst[:, :, 0:KE], both[:, :, 0:KE], ACT.Copy)
                        act.activation(dst[:, :, KE:2 * KE], both[:, :, KE:2 * KE], ACT.Copy, scale=alpha_sb[:, 0:1]).then_inc(w_act, 1)
                    elif scaled == "all":
                        act.activation(dst, src, ACT.Copy, scale=alpha_sb[:, 0:1]).then_inc(w_act, 1)
                    else:
                        act.activation(dst, src, ACT.Copy).then_inc(w_act, 1)
                act.activation(decay_rate[:, :, :], decay_rate[:, :, :], ACT.Exp).then_inc(w_act, 1)
                act.wait_ge(w_dve, 2)

            def centre(steps, b, dst, src, rs, nm, name):
                for j in range(TB):
                    act.activation(dst[:, j, :], src[:, j, :], ACT.Identity, scale=rs[:, j:j + 1], bias=nm[:, j:j + 1]).then_inc(steps.step(f"{name}{j}"), 1)

            def h_task(b, k, use):
                act.wait_ge(f_pool.sem, f_pool.done(b, "nm"))
                centre(f_act, b, x_front, x_front, rs_f, nm_f, "h")

            def t_task(b, k, use):
                act.wait_ge(b_pool.sem, b_pool.done(b, "nm"))
                centre(b_act, b, rows, rows, rs_b, nm_b, "t")

            def xn_task(b, k, use):
                act.wait_ge(b_pool.sem, b_pool.done(b, "nm1"))
                centre(b_act, b, rows, x_back[b.parity], rs_1, nm_1, "xn")

            def out_centre(b, k, use):
                act.wait_ge(l_pool.sem, l_pool.done(b, "nm"))
                centre(l_act, b, o_rows, o_rows, rs_o, nm_o, "t")

            def hT_task(b, t, use):
                act.wait_ge(f_pe.sem, f_pe.done(b, f"hT{t}"))
                act.activation(hT[:, t, :], use.bank[:, :], ACT.Copy, scale=norm_sb[:, t:t + 1]).then_inc(f_act.step(f"hT{t}"), 1)

            def xs_task(b, c, use):
                if c == 0:
                    if b.shift(-2).exists:
                        act.wait_ge(b_dve.sem, b_dve.done(b.shift(-2), "o3"))
                act.wait_ge(f_pe.sem, f_pe.done(b, f"xs{c}"))
                act.activation(xs[b.parity][:, c, :], use.bank[:, :], ACT.Identity,
                                          scale=conv_w_sb[:, c, TAPS - 1:TAPS], bias=conv_b_sb[:, c:c + 1]).then_inc(f_act.step(f"cv{c}"), 1)

            def res_task(b, c, use):
                if c == 0:
                    if b.shift(-2).exists:
                        act.wait_ge(b_pe.sem, b_pe.done(b.shift(-2), "wo3"))
                act.wait_ge(f_pe.sem, f_pe.done(b, f"res{c}"))
                act.activation(res[b.parity][:, c, :], use.bank[:, :], ACT.Copy).then_inc(f_act.step(f"res{c}"), 1)

            def silu_task(b, k, use):
                act.wait_ge(f_dve.sem, f_dve.done(b, "cvC3"))
                act.sem_inc(passed["act"], 1)
                act.preload_act_table_set("silu_and_others")
                act.activation(xs[b.parity][:, :, :], xs[b.parity][:, :, :], ACT.Silu).then_inc(f_act.step("silux"), 1)
                act.wait_ge(f_act.sem, f_act.done(b, "res3"))
                act.activation(res[b.parity][:, :, :], res[b.parity][:, :, :], ACT.Silu).then_inc(f_act.step("silur"), 1)
                act.preload_act_table_set(EXP_SET)

            def proj_task(b, k, use):
                act.wait_ge(f_pe.sem, f_pe.done(b, "proj"))
                if b.turn is not None or b.const > 0:
                    act.wait_ge(B_out, b.count(16, 0))
                act.activation(projT[:, :], use.bank[0:NPROJ, :], ACT.Copy).then_inc(f_act.step("proj"), 1)

            def Ct_task(b, k, use):
                act.wait_ge(f_pe.sem, f_pe.done(b, "Ct"))
                if b.shift(-2).exists:
                    act.wait_ge(s_acc.sem, s_acc.done(b.shift(-2), f"{NS - 1},{TB - 1}"))
                both = use.bank[:, 0:TB * NPROJ].rearrange("p (j n) -> p j n", j=TB)
                act.activation(C_tok[b.parity][:, :, :], both[:, :, RANK + NS:NPROJ], ACT.Copy).then_inc(f_act.step("Ct"), 1)

            def dt_task(b, c, use):
                e = scratch[:, c % 2, :]
                act.wait_ge(f_pe.sem, f_pe.done(b, f"dt{c}"))
                if c >= 2:
                    act.wait_ge(f_pool.sem, f_pool.done(b, f"w{c - 2}"))
                elif c == 0:
                    if b.shift(-2).exists:
                        act.wait_ge(b_pe.sem, b_pe.done(b.shift(-2), "lg"))
                    if b.shift(-2).exists:
                        act.wait_ge(s_bx.sem, s_bx.done(b.shift(-2), f"{NS - 1},1"))
                    if b.shift(-1).exists:
                        act.wait_ge(f_pool.sem, f_pool.done(b.shift(-1), "w3"))
                act.activation(e, use.bank[:, :], ACT.Abs, bias=b_dt_sb[:, c:c + 1]).then_inc(f_act.step(f"ab{c}"), 1)
                act.activation(dx[b.parity][:, c, :], use.bank[:, :], ACT.Relu, bias=b_dt_sb[:, c:c + 1]).then_inc(f_act.step(f"rl{c}"), 1)

            def ex_task(b, c, use):
                e = scratch[:, c % 2, :]
                act.wait_ge(f_act.sem, f_act.done(b, f"ab{c}"))
                act.activation(e, e, ACT.Exp, scale=-1.0).then_inc(f_act.step(f"ex{c}"), 1)
                act.wait_ge(f_act.sem, f_act.done(b, f"ex{c}"))
                act.activation(delta[b.parity][:, c, :], e, ACT.Ln, bias=one[:, 0:1]).then_inc(f_act.step(f"ln{c}"), 1)

            def xnT_task(b, t, use):
                act.wait_ge(b_pe.sem, b_pe.done(b, f"xnT{t}"))
                act.activation(xnT[:, t, :], use.bank[:, :], ACT.Copy).then_inc(b_act.step(f"xnT{t}"), 1)

            def rt_task(b, k, use):
                if k == 0:
                    if b.shift(1).exists:
                        act.wait_ge(f_dve.sem, f_dve.done(b.shift(1), "d13"))
                act.wait_ge(b_pe.sem, b_pe.done(b, f"rt{k}"))
                act.activation(scratch[:, k, :], use.bank[:, :], ACT.Identity, bias=b1_sb[:, k % 2:k % 2 + 1]).then_inc(b_act.step(f"rt{k}"), 1)

            def gelu_task(b, k, use):
                act.wait_ge(b_act.sem, b_act.done(b, "rt3"))
                act.sem_inc(passed["act"], 1)
                act.preload_act_table_set("gelu_and_others")
                act.activation(scratch[:, :, :], scratch[:, :, :], ACT.Gelu).then_inc(b_act.step("gelu"), 1)
                act.preload_act_table_set(EXP_SET)

            def soft_exp(b, k, use):
                act.wait_ge(b_dve.sem, b_dve.done(b, "sub"))
                act.activation(logits[:, :, :, :], logits[:, :, :, :], ACT.Exp).then_inc(b_act.step("ex"), 1)

            def gateT_task(b, k, use):
                act.wait_ge(b_pe.sem, b_pe.done(b, "gT"))
                act.activation(gateT[:, :], use.bank[0:2 * KE, :], ACT.Copy).then_inc(b_act.step("gT"), 1)

            def cum_task(b, u, use):
                j, br = u // 2, u % 2
                act.wait_ge(l_pe.sem, l_pe.done(b, f"cum{u}"))
                if u >= 2:
                    act.wait_ge(l_dve.sem, l_dve.done(b, f"pr{u - 2}"))
                elif u == 0:
                    if b.shift(-1).exists:
                        act.wait_ge(l_dve.sem, l_dve.done(b.shift(-1), "pr7"))
                    act.wait_ge(b_dve.sem, b_dve.done(b, "wa"))
                for k in range(KE):
                    last = act.activation(cum_sb[u % 2][:, k * RK:(k + 1) * RK], use.bank[:, k * RK:(k + 1) * RK], ACT.Copy,
                                          scale=gate[:, j, br * KE + k:br * KE + k + 1])
                last.then_inc(l_act.step(f"cum{u}"), 1)

            def pt_task(b, u, use):
                br, j = u % 2, u // 2
                free = b if j else b.shift(-1)
                if free.exists:
                    act.wait_ge(l_pe.sem, l_pe.done(free, f"out{(u - 2) % 8}"))
                act.wait_ge(l_pe.sem, l_pe.done(b, f"pt{u}"))
                act.activation(flat(prodT[:, 4 * br:4 * br + 4, :]), use.bank[:, :], ACT.Copy).then_inc(l_act.step(f"pt{u}"), 1)

            def out_task(b, j, use):
                if j == 0:
                    if b.shift(-1).exists:
                        act.wait_ge(l_dve.sem, l_dve.done(b.shift(-1), "x"))
                act.wait_ge(l_pe.sem, l_pe.done(b, f"out{2 * j + 1}"))
                act.activation(o_rows[:, j, :], use.bank[:, 0:D], ACT.Copy).then_inc(l_act.step(f"out{j}"), 1)

            def scan_part(q, n, beat):
                if not q.exists or beat % 2:
                    return
                c = beat // 2
                if n == 0:
                    act.wait_ge(f_dve.sem, f_dve.done(q, f"d1{c}"))
                back = n * CT + c - 2
                free = q if back >= 0 else q.shift(-1)
                if free.exists:
                    act.wait_ge(s_scan.sem, s_scan.done(free, f"{back % (NS * CT) // CT},{back % CT}"))
                act.activation(decay[c % 2][:, :], delta[q.parity][:, c, :], ACT.Exp, scale=decay_rate[:, c, n:n + 1]).then_inc(s_exp.step(f"{n},{c}"), 1)

            walk(act, "act", prologue, {("F", "h"): h_task, ("B", "t"): t_task, ("B", "xn"): xn_task, ("L", "t"): out_centre, ("F", "hT"): hT_task, ("F", "xs"): xs_task, ("F", "res"): res_task, ("F", "silu"): silu_task,
                                 ("F", "proj"): proj_task, ("F", "Ct"): Ct_task, ("F", "dt"): dt_task, ("F", "ex"): ex_task, ("B", "xnT"): xnT_task, ("B", "rt"): rt_task,
                                 ("B", "gelu"): gelu_task, ("B", "ex"): soft_exp, ("B", "gT"): gateT_task,
                                 ("L", "cum"): cum_task, ("L", "pt"): pt_task, ("L", "out"): out_task}, scan_part)

        @block.vector
        def _(dve):
            def prologue():
                dve.wait_ge(w_act, len(jobs) + 1)
                dve.tensor_scalar(decay_rate[:, :, :], decay_rate[:, :, :], -1.0, None, ALU.mult).then_inc(w_dve, 1)
                both = top[:, 0:KE]
                dve.tensor_tensor(both, bias_raw[:, 0, 0, :], bias_raw[:, 0, 1, :], ALU.add).then_inc(w_dve, 1)
                dve.wait_ge(w_dve, 2)
                dve.tensor_copy(logit_bias[:, :, :, :].rearrange("p a b k -> p (a b) k"),
                                both.rearrange("p (o k) -> p o k", o=1).broadcast_to([P, TB * 2, KE])).then_inc(w_dve, 1)
                dve.wait_ge(w_dve, 3)
                dve.wait_ge(w_pool, 6)

            def stats(steps, src, st, name):
                for j in range(TB):
                    dve.bn_stats(st[:, j, :], src[:, j, :]).then_inc(steps.step(f"{name}{j}"), 1)

            def aggregate(steps, b, st, mv, stat, name):
                dve.wait_ge(steps.sem, steps.done(b, f"{stat}{TB - 1}"))
                dve.sem_inc(passed["dve"], 1)
                for j in range(TB):
                    dve.bn_aggr(mv[:, j, :], st[:, j, :]).then_inc(steps.step(f"{name}{j}"), 1)

            def front_stats(b, k, use):
                dve.wait_ge(xf_in, b.count(16, 16))
                stats(f_dve, x_front, st_f, "st")

            def front_aggregate(b, k, use):
                aggregate(f_dve, b, st_f, mv_f, "st", "ag")

            def tap(back, name, before):
                def task(b, c, use):
                    x_c = xs[b.parity][:, c, :]
                    dve.wait_ge(before[0].sem, before[0].done(b, f"{before[1]}{c}"))
                    dve.scalar_tensor_tensor(out=x_c[:, back:], in0=use.bank[:, 0:T - back], scalar=conv_w_sb[:, c, TAPS - 1 - back:TAPS - back],
                                             in1=x_c[:, back:], op0=ALU.mult, op1=ALU.add).then_inc(f_dve.step(f"{name}{c}"), 1)
                return task

            def d1_task(b, c, use):
                dve.wait_ge(f_pool.sem, f_pool.done(b, f"w2{c}"))
                dve.wait_ge(f_act.sem, f_act.done(b, f"ln{c}"))
                dve.tensor_tensor(delta[b.parity][:, c, :], delta[b.parity][:, c, :], scratch[:, 2 + c % 2, :], ALU.add).then_inc(f_dve.step(f"d1{c}"), 1)

            def dx_task(b, c, use):
                dve.wait_ge(f_dve.sem, f_dve.done(b, f"d1{c}"))
                dve.tensor_tensor(dx[b.parity][:, c, :], delta[b.parity][:, c, :], xs[b.parity][:, c, :], ALU.mult).then_inc(f_dve.step(f"dx{c}"), 1)

            def keep_task(b, k, use):
                dve.tensor_copy(r_keep[:, :], r_x0[b.parity][:, :]).then_inc(b_dve.step("keep"), 1)

            def u_task(b, c, use):
                r = b.parity
                dve.wait_ge(b_pe.sem, b_pe.done(b, f"y{c}"))
                dve.scalar_tensor_tensor(out=xs[r][:, c, :], in0=xs[r][:, c, :], scalar=skip_sb[:, c:c + 1],
                                         in1=use.bank[:, :], op0=ALU.mult, op1=ALU.add).then_inc(b_dve.step(f"u{c}"), 1)

            def o_task(b, c, use):
                r = b.parity
                dve.wait_ge(b_dve.sem, b_dve.done(b, f"u{c}"))
                dve.tensor_tensor(res[r][:, c, :], xs[r][:, c, :], res[r][:, c, :], ALU.mult).then_inc(b_dve.step(f"o{c}"), 1)

            def r_task(b, j, use):
                if j == 0:
                    dve.wait_ge(xb_in[b.parity], b.half_count(16, 16))
                    dve.wait_ge(b_dve.sem, b_dve.done(b, "keep"))
                    if b.shift(-1).exists:
                        dve.wait_ge(b_pe.sem, b_pe.done(b.shift(-1), "xnT1"))
                if j % 2 == 0:
                    dve.wait_ge(b_pe.sem, b_pe.done(b, f"wo{j + 1}"))
                dve.scalar_tensor_tensor(out=rows[:, j, :], in0=x_back[b.parity][:, j, :], scalar=r_keep[:, j:j + 1],
                                         in1=use.bank[:, j % 2 * D:(j % 2 + 1) * D], op0=ALU.mult, op1=ALU.add).then_inc(b_dve.step(f"r{j}"), 1)

            def st_task(b, k, use):
                dve.wait_ge(b_dve.sem, b_dve.done(b, "r3"))
                stats(b_dve, rows, st_b, "st")

            def ag_task(b, k, use):
                aggregate(b_dve, b, st_b, mv_b, "st", "ag")

            def x1_task(b, k, use):
                dve.wait_ge(b_act.sem, b_act.done(b, "t3"))
                dve.tensor_tensor(x_back[b.parity][:, :, :], x_back[b.parity][:, :, :], rows[:, :, :], ALU.add).then_inc(b_dve.step("x1"), 1)

            def st1_task(b, k, use):
                dve.wait_ge(b_dve.sem, b_dve.done(b, "x1"))
                stats(b_dve, x_back[b.parity], st_1, "s1")

            def ag1_task(b, k, use):
                aggregate(b_dve, b, st_1, mv_1, "s1", "a1")

            def cum_task(b, t, use):
                dve.wait_ge(b_act.sem, b_act.done(b, f"xnT{t}"))
                dve.tensor_tensor_scan(cumT[:, t, :], one[:, 0:1].broadcast_to([P, T]), use.bank[:, :], 0.0,
                                       ALU.mult, ALU.add).then_inc(b_dve.step(f"cum{t}"), 1)

            flat_l = logits[:, :, :, :].rearrange("p a b k -> p (a b) k")

            def lb_task(b, k, use):
                dve.wait_ge(b_pe.sem, b_pe.done(b, "lg"))
                dve.tensor_tensor(flat_l, use.bank[:, 0:TB * 2 * KE].rearrange("p (a k) -> p a k", k=KE),
                                  logit_bias[:, :, :, :].rearrange("p a b k -> p (a b) k"), ALU.add).then_inc(b_dve.step("lb"), 1)

            def mx_task(b, k, use):
                dve.wait_ge(b_dve.sem, b_dve.done(b, "lb"))
                dve.tensor_reduce(top[:, :], flat_l, AX.X, ALU.max).then_inc(b_dve.step("mx"), 1)

            def sub_task(b, k, use):
                dve.wait_ge(b_dve.sem, b_dve.done(b, "mx"))
                dve.tensor_tensor(flat_l, flat_l, top[:, :].rearrange("p (a o) -> p a o", o=1).broadcast_to([P, TB * 2, KE]),
                                  ALU.subtract).then_inc(b_dve.step("sub"), 1)

            def sm_task(b, k, use):
                dve.wait_ge(b_act.sem, b_act.done(b, "ex"))
                dve.tensor_reduce(total[:, :], flat_l, AX.X, ALU.add).then_inc(b_dve.step("sm"), 1)

            def sn_task(b, k, use):
                dve.wait_ge(b_dve.sem, b_dve.done(b, "sm"))
                dve.tensor_tensor(total[:, :], total[:, :], n_valid[:, :, :].rearrange("p a b -> p (a b)"), ALU.mult).then_inc(b_dve.step("sn"), 1)

            def rc_task(b, k, use):
                dve.wait_ge(b_dve.sem, b_dve.done(b, "sn"))
                dve.reciprocal(total[:, :], total[:, :]).then_inc(b_dve.step("rc"), 1)

            def wa_task(b, k, use):
                dve.wait_ge(b_dve.sem, b_dve.done(b, "rc"))
                if b.shift(-1).exists:
                    dve.wait_ge(l_act.sem, l_act.done(b.shift(-1), "cum7"))
                dve.tensor_tensor(gate[:, :, :].rearrange("p a (b k) -> p (a b) k", k=KE), flat_l,
                                  total[:, :].rearrange("p (a o) -> p a o", o=1).broadcast_to([P, TB * 2, KE]), ALU.mult).then_inc(b_dve.step("wa"), 1)

            def pr_task(b, u, use):
                dve.wait_ge(l_act.sem, l_act.done(b, f"cum{u}"))
                dve.wait_ge(l_pe.sem, l_pe.done(b, f"xv{u}"))
                assert u < 2 or l_pe.index[f"xv{u}"] > l_pe.index[f"pt{u - 2}"]
                dve.tensor_tensor(prod[u % 2][:, :], use.bank[:, :], cum_sb[u % 2][:, :], ALU.mult).then_inc(l_dve.step(f"pr{u}"), 1)

            def out_stats(b, k, use):
                dve.wait_ge(l_act.sem, l_act.done(b, "out3"))
                stats(l_dve, o_rows, st_o, "st")

            def out_aggregate(b, k, use):
                aggregate(l_dve, b, st_o, mv_o, "st", "ag")

            def x_task(b, k, use):
                dve.wait_ge(l_act.sem, l_act.done(b, "t3"))
                dve.tensor_tensor(x_back[b.parity][:, :, :], x_back[b.parity][:, :, :], o_rows[:, :, :], ALU.add).then_inc(l_dve.step("x"), 1)

            def scan_part(q, slot, beat):
                k = beat // 2
                if beat % 2 == 0:
                    if not q.exists:
                        return
                    n, c = slot, k
                    dve.wait_ge(s_exp.sem, s_exp.done(q, f"{n},{c}"))
                    if c % 2 == 0:
                        dve.wait_ge(s_bx.sem, s_bx.done(q, f"{n},{c // 2}"))
                    if c == 0:
                        free = q if n >= 2 else q.shift(-1)
                        if free.exists:
                            dve.wait_ge(s_tr.sem, s_tr.done(free, f"{(n - 2) % NS},{TB - 1}"))
                    dve.tensor_tensor_scan(h[n % 2][:, c, :], decay[c % 2][:, :], bx[c // 2][:, c % 2, :], 0.0,
                                           ALU.mult, ALU.add).then_inc(s_scan.step(f"{n},{c}"), 1)
                    return
                batch, n = (q, slot - 1) if slot else (q.shift(-1), NS - 1)
                if not batch.exists:
                    return
                dve.wait_ge(s_tr.sem, s_tr.done(batch, f"{n},{k}"))
                if n == 0:
                    if k == 0:
                        dve.wait_ge(f_act.sem, f_act.done(batch, "Ct"))
                        if batch.shift(-1).exists:
                            dve.wait_ge(b_pe.sem, b_pe.done(batch.shift(-1), "y3"))
                    ins = dve.tensor_scalar(yT[:, k, :], stateT[k % 2][:, :], C_tok[batch.parity][:, k, n:n + 1], None, ALU.mult)
                else:
                    dve.wait_ge(s_acc.sem, s_acc.done(batch, f"{n - 1},{k}"))
                    ins = dve.scalar_tensor_tensor(out=yT[:, k, :], in0=stateT[k % 2][:, :], scalar=C_tok[batch.parity][:, k, n:n + 1],
                                                   in1=yT[:, k, :], op0=ALU.mult, op1=ALU.add)
                ins.then_inc(s_acc.step(f"{n},{k}"), 1)

            walk(dve, "dve", prologue,
                 {("F", "st"): front_stats, ("F", "ag"): front_aggregate, ("F", "cvA"): tap(1, "cvA", (f_act, "cv")),
                  ("F", "cvB"): tap(2, "cvB", (f_dve, "cvA")), ("F", "cvC"): tap(3, "cvC", (f_dve, "cvB")), ("F", "d1"): d1_task, ("F", "dx"): dx_task,
                  ("B", "keep"): keep_task, ("B", "u"): u_task, ("B", "o"): o_task, ("B", "r"): r_task, ("B", "st"): st_task, ("B", "ag"): ag_task,
                  ("B", "x1"): x1_task, ("B", "st1"): st1_task, ("B", "ag1"): ag1_task, ("B", "cum"): cum_task, ("B", "lb"): lb_task, ("B", "mx"): mx_task,
                  ("B", "sub"): sub_task, ("B", "sm"): sm_task, ("B", "sn"): sn_task, ("B", "rc"): rc_task, ("B", "wa"): wa_task,
                  ("L", "pr"): pr_task, ("L", "st"): out_stats, ("L", "ag"): out_aggregate, ("L", "x"): x_task}, scan_part)


INPUTS = ["L0_attn_x", "L0_attn_norm_scale", "L0_attn_w_in", "L0_attn_conv_w", "L0_attn_conv_b", "L0_attn_A_log", "L0_attn_D",
          "L0_attn_w_xproj", "L0_attn_w_dt", "L0_attn_b_dt", "L0_attn_w_out", "L0_ffn_W_Q", "L0_ffn_W_K", "L0_ffn_W_O",
          "L0_ffn_W_inv", "L0_ffn_V_fwd", "L0_ffn_W_fwd", "L0_ffn_U_fwd", "L0_ffn_b_fwd", "L0_ffn_V_inv", "L0_ffn_W_inv_exp",
          "L0_ffn_U_inv", "L0_ffn_b_inv", "L0_ffn_router_w1", "L0_ffn_router_b1", "L0_ffn_router_w2", "L0_ffn_router_b2",
          "L0_ffn_alpha_bi", "L0_ffn_expert_bias"]


def kernel(**inputs):
    import numpy as np
    import concourse.bacc as bacc
    from concourse.bass_utils import run_bass_kernel_spmd

    nc = bacc.Bacc("TRN2", target_bir_lowering=False, num_devices=1)
    arrays, args = {}, []
    for name in INPUTS:
        a = np.ascontiguousarray(inputs[name])
        if a.ndim == 0:
            a = a.reshape(1)
        arrays[f"in_{name}"] = a
        args.append(nc.dram_tensor(f"in_{name}", a.shape, mybir.dt.from_np(a.dtype), kind="ExternalInput").ap())
    args.append(nc.dram_tensor("out_0", (NB, T, D), FP32, kind="ExternalOutput").ap())
    program(nc, *args)
    result = run_bass_kernel_spmd(nc, [arrays], core_ids=[0])
    return result.results[0]["out_0"]
```

```python
import concourse.bass as bass
from concourse import mybir
from contextlib import ExitStack

FP32 = mybir.dt.float32
ALU = mybir.AluOpType
ACT = mybir.ActivationFunctionType
AX = mybir.AxisListType

P = 128
NB, T, D = 16, 512, 256
DI, NS, RANK = 512, 16, 16
TAPS = 4
KE, RK = 8, 64
KR = KE * RK
TB, CT, DT = T // P, DI // P, D // P
NPROJ = RANK + 2 * NS
EPS = 1e-5
SLOTS = NS
BB_RING = 4
BX_RING = 3
EXP_SET = "natural_log_exp_and_others"


class Batch:

    def __init__(self, const, turn=None):
        self.const, self.turn = const, turn
        self.parity = const % 2

    def shift(self, k):
        return Batch(self.const + k, self.turn)

    @property
    def exists(self):
        return self.turn is not None or 0 <= self.const < NB

    def count(self, per_batch, more):
        if self.turn is None:
            return self.const * per_batch + more
        return self.turn * (2 * per_batch) + (self.const * per_batch + more)

    def half_count(self, per_pair, more):
        if self.turn is None:
            return self.const // 2 * per_pair + more
        return self.turn * per_pair + (self.const // 2 * per_pair + more)

    def dram(self, ap):
        if self.turn is None:
            return ap[self.const]
        return ap[bass.ds(self.turn * 2 + self.const, 1)].rearrange("o p j d -> (o p) j d")


class Steps:

    def __init__(self, sem, names):
        self.sem, self.names = sem, names
        self.index = {n: i for i, n in enumerate(names)}
        self.next = 0

    def done(self, batch, name):
        return batch.count(len(self.names), self.index[name] + 1)

    def step(self, name):
        assert self.names[self.next] == name, (self.names[self.next], name)
        self.next = (self.next + 1) % len(self.names)
        return self.sem


BEATS = 8 * SLOTS
JOBS_FROM, JOBS_EVERY = 60, 3
TIMETABLE = {
    ("B", "keep", "dve"): (255,),
    ("F", "st", "dve"): (7,),
    ("F", "ag", "dve"): (8,),
    ("F", "rs", "pool"): (15,),
    ("F", "h", "act"): (17,),
    ("F", "hT", "pe"): (17, 26),
    ("F", "hT", "act"): (28, 31),
    ("F", "x", "sp"): (86,),
    ("F", "xs", "pe"): (32, 35, 37, 40),
    ("F", "xs", "act"): (34, 36, 40, 43),
    ("F", "cvA", "dve"): (35, 37, 38, 42),
    ("F", "cvB", "dve"): (37, 37, 39, 42),
    ("F", "cvC", "dve"): (37, 37, 39, 44),
    ("F", "res", "pe"): (36, 38, 41, 65),
    ("F", "res", "act"): (36, 43, 47, 68),
    ("F", "silu", "act"): (70,),
    ("F", "proj", "pe"): (75,),
    ("F", "proj", "act"): (79,),
    ("F", "B", "sp"): (72,),
    ("F", "Ct", "pe"): (94,),
    ("F", "Ct", "act"): (102,),
    ("F", "dt", "pe"): (82, 89, 100, 108),
    ("F", "dt", "act"): (89, 93, 107, 111),
    ("F", "ex", "act"): (91, 94, 107, 119),
    ("F", "ln", "act"): (92, 96, 107, 119),
    ("F", "w", "pool"): (101, 105, 117, 126),
    ("F", "w2", "pool"): (101, 109, 121, 126),
    ("F", "d1", "dve"): (94, 104, 119, 122),
    ("F", "row", "sp"): (102, 123, 126),
    ("B", "y", "pe"): (263, 263, 264, 264),
    ("B", "u", "dve"): (263, 264, 264, 268),
    ("B", "o", "dve"): (268, 270, 271, 271),
    ("B", "wo", "pe"): (274, 278, 282, 287),
    ("B", "r", "dve"): (283, 283, 287, 289),
    ("B", "st", "dve"): (293,),
    ("B", "ag", "dve"): (295,),
    ("B", "rb", "pool"): (300,),
    ("B", "t", "act"): (302,),
    ("B", "x1", "dve"): (301,),
    ("B", "st1", "dve"): (302,),
    ("B", "ag1", "dve"): (304,),
    ("B", "rb1", "pool"): (309,),
    ("B", "xn", "act"): (310,),
    ("B", "xnT", "pe"): (317, 319),
    ("B", "xnT", "act"): (320, 320),
    ("B", "cum", "dve"): (322, 324),
    ("B", "rt", "pe"): (324, 327, 329, 333),
    ("B", "rt", "act"): (331, 332, 332, 338),
    ("B", "gelu", "act"): (338,),
    ("B", "logit", "pe"): (342,),
    ("B", "logit", "act"): (346,),
    ("B", "logit_rows", "pe"): (346,),
    ("B", "lb", "dve"): (346,),
    ("B", "mx", "dve"): (347,),
    ("B", "sub", "dve"): (347,),
    ("B", "ex", "act"): (348,),
    ("B", "sm", "dve"): (349,),
    ("B", "sn", "dve"): (351,),
    ("B", "rc", "dve"): (352,),
    ("B", "wa", "dve"): (353,),
    ("B", "gT", "pe"): (371,),
    ("B", "gT", "act"): (376,),
    ("L", "cum", "pe"): (348, 354, 363, 374, 386, 390, 398, 428),
    ("L", "xv", "pe"): (351, 358, 367, 378, 394, 423, 426, 431),
    ("L", "cum", "act"): (357, 360, 368, 379, 391, 392, 408, 432),
    ("L", "pr", "dve"): (357, 360, 372, 379, 396, 424, 428, 435),
    ("L", "pt", "pe"): (364, 371, 383, 385, 399, 430, 433, 439),
    ("L", "pt", "act"): (370, 376, 384, 386, 406, 434, 436, 438),
    ("L", "out", "pe"): (373, 381, 393, 398, 431, 434, 439, 443),
    ("L", "out", "act"): (382, 401, 440, 445),
    ("L", "st", "dve"): (454,),
    ("L", "ag", "dve"): (462,),
    ("L", "rs", "pool"): (473,),
    ("L", "t", "act"): (468,),
    ("F", "dx", "pool"): (105, 113, 126, 127),
    ("L", "x", "pool"): (477, 477),
    ("L", "store", "sp"): (466,),
}

FILLED_BY = {("F", "hT"): "hT", ("F", "xs"): "xs", ("F", "cvA"): "xs", ("F", "cvB"): "xs", ("F", "cvC"): "xs", ("F", "res"): "res",
             ("F", "proj"): "proj", ("F", "Ct"): "Ct", ("F", "dt"): "dt", ("B", "u"): "y", ("B", "r"): "wo", ("B", "xnT"): "xnT",
             ("B", "cum"): "xnT", ("B", "rt"): "rt", ("B", "logit"): "logit", ("B", "lb"): "logit_rows", ("B", "gT"): "gT",
             ("L", "cum"): "cum", ("L", "pr"): "xv", ("L", "pt"): "pt", ("L", "out"): "out"}
SHARE_A_BANK = {"wo": 2, "out": 2}


def rows_of_plan(engine):
    return sorted((beat, i, stage, task, k) for i, ((stage, task, who), beats) in enumerate(TIMETABLE.items()) if who == engine
                  for k, beat in enumerate(beats))


def plan(engine):
    beats = [[] for _ in range(BEATS)]
    for beat, _, stage, task, k in rows_of_plan(engine):
        beats[beat % BEATS].append((beat // BEATS, stage, task, k))
    return beats


def bank_numbers():
    numbers, n = {}, 0
    for tasks in plan("pe"):
        for periods, stage, task, k in tasks:
            if k % SHARE_A_BANK.get(task, 1) == 0:
                numbers[stage, task, k] = (periods, n)
                n += 1
    return numbers, n + n % 2


def steps_of(engine, stage, tasks):
    return [name.format(k) for _, _, of, task, k in rows_of_plan(engine) if of == stage for name in tasks.get(task, [])]


def user_before(batch, n, uses, ring):
    if n >= ring:
        return batch, n - ring
    return batch.shift(-1), max(m for m in range(uses) if m % ring == n)


def numbered(*names):
    return [f"{n}{i}" for n in names for i in range(TB)]


def program(nc, x, norm_scale, w_in, conv_w, conv_b, A_log, D_skip, w_xproj, w_dt, b_dt, w_out,
            W_Q, W_K, W_O, W_inv, V_fwd, W_fwd, U_fwd, b_fwd, V_inv, W_inv_exp, U_inv, b_inv,
            router_w1, router_b1, router_w2, router_b2, alpha_bi, expert_bias, out):
    ctx = ExitStack()
    with ctx:
        ctx.enter_context(nc.allow_non_contiguous_dma(reason="small weights, loaded once"))

        def sb(name, *shape):
            return ctx.enter_context(nc.sbuf_tensor(name, list(shape), FP32))

        def psum(name):
            return ctx.enter_context(nc.psum_tensor(name, [P, T], FP32))

        def sem(name):
            return ctx.enter_context(nc.semaphore(name))

        w_in_sb = sb("w_in_sb", P, DT, 2 * DI)
        w_out_sb = sb("w_out_sb", P, CT, D)
        w_xproj_sb = sb("w_xproj_sb", P, CT, NPROJ)
        rank_and_gate = sb("rank_and_gate", 3 * KE * 2, DI)
        w_dt_sb = rank_and_gate[0:RANK, :]
        decay_rate = sb("decay_rate", P, CT, NS)
        conv_w_sb = sb("conv_w_sb", P, CT, TAPS)
        conv_b_sb = sb("conv_b_sb", P, CT)
        skip_sb = sb("skip_sb", P, CT)
        b_dt_sb = sb("b_dt_sb", P, CT)
        norm_sb = sb("norm_sb", P, DT)
        b1_sb = sb("b1_sb", P, DT)
        q_to_expert = [sb(f"q_to_expert{br}", P, DT, KR) for br in range(2)]
        k_to_expert = [sb(f"k_to_expert{br}", P, DT, KR) for br in range(2)]
        q_to_router = [sb(f"q_to_router{br}", P, DT, D) for br in range(2)]
        expert_to_out = sb("expert_to_out", P, 8, D)
        w2_padded = sb("w2_padded", P, DT, 3 * KE)
        bias_to_out = sb("bias_rows", 6 * KE, D)[4 * KE:6 * KE, :]
        logit_bias = sb("logit_bias", P, TB, 2, KE)
        n_valid = sb("n_valid", P, TB, 2)
        alpha_sb = sb("alpha_sb", P, 1)
        minus_half = sb("minus_half", P, TB)
        minus_one = sb("minus_one", P, TB)
        one = sb("one", P, 1)
        ident = sb("ident", P, P)

        x_front = sb("x_front", P, TB, D)
        x_back = [sb(f"x_back{i}", P, TB, D) for i in range(2)]
        hT = sb("hT", P, DT, T)
        xs = [sb(f"xs{i}", P, CT, T) for i in range(2)]
        res = [sb(f"res{i}", P, CT, T) for i in range(2)]
        delta = [sb(f"delta{i}", P, CT, T) for i in range(2)]
        dx = [sb(f"dx{i}", P, CT, T) for i in range(2)]
        scratch = sb("scratch", P, 4, T)
        B_rows = sb("B_rows", P, BB_RING, T)
        bx = [sb(f"bx{i}", P, CT // 2, T) for i in range(BX_RING)]
        h = [sb(f"h{i}", P, CT, T) for i in range(2)]
        yT = sb("yT", P, TB, DI)
        rows = sb("rows", P, TB, D)
        xnT = sb("xnT", P, DT, T)
        cumT = sb("cumT", P, DT, T)
        cum_sb = [sb(f"cum_sb{i}", P, KR) for i in range(2)]
        prod = [sb(f"prod{i}", P, KR) for i in range(2)]
        prodT = sb("prodT", P, 8, P)
        o_rows = sb("o_rows", P, TB, D)
        projT = hT[0:NPROJ, 0, :]
        C_tok = [sb(f"C_tok{i}", P, TB, NS) for i in range(2)]
        st_f, st_b, st_1, st_o = (sb(f"st_{n}", P, TB, 6) for n in "fb1o")
        mv_f, mv_b, mv_1, mv_o = (sb(f"mv_{n}", P, TB, 2) for n in "fb1o")
        ve_f, ms_f, rs_f, r2_f = (sb(n, P, TB) for n in ("ve_f", "ms_f", "rs_f", "r2_f"))
        nm_f, nm_b, nm_1, nm_o = (sb(f"nm_{n}", P, TB) for n in "fb1o")
        r_x0 = [sb(f"r_x0{i}", P, TB) for i in range(2)]
        r_keep = sb("r_keep", P, TB)
        ve_b, rs_b, ve_1, rs_1, ve_o, rs_o = (sb(n, P, TB) for n in ("ve_b", "rs_b", "ve_1", "rs_1", "ve_o", "rs_o"))
        logits = sb("logits", P, TB, 2, KE)
        top = sb("top", P, TB * 2)
        total = sb("total", P, TB * 2)
        gate = sb("gate", P, TB, 2 * KE)
        logitT = rank_and_gate[4 * KE:6 * KE, :]
        gateT = rank_and_gate[4 * KE:6 * KE, :]

        B_dram = nc.dram_tensor("B_scratch", [2, NS, T], FP32).ap()

        decay = [psum(f"decay{i}") for i in range(2)]
        stateT = [psum(f"stateT{i}") for i in range(2)]
        bank = [psum(f"bank{i}") for i in range(4)]

        f_pe = Steps(sem("f_pe"), steps_of("pe", "F", {"hT": ["hT{}"], "xs": ["xs{}"], "res": ["res{}"], "proj": ["proj"],
                                                       "Ct": ["Ct"], "dt": ["dt{}"]}))
        f_act = Steps(sem("f_act"), steps_of("act", "F", {"h": numbered("h"), "hT": ["hT{}"], "xs": ["cv{}"], "res": ["res{}"], "silu": ["silux", "silur"],
                                                          "proj": ["proj"], "Ct": ["Ct"], "dt": ["ab{}", "rl{}"], "ex": ["ex{}", "v{}"], "ln": ["ln{}", "u{}"]}))
        f_dve = Steps(sem("f_dve"), steps_of("dve", "F", {"st": numbered("st"), "ag": numbered("ag"),
                                                          "cvA": ["cvA{}"], "cvB": ["cvB{}"], "cvC": ["cvC{}"], "d1": ["d1{}"]}))
        f_pool = Steps(sem("f_pool"), steps_of("pool", "F", {"rs": ["ve", "r1", "ms", "mr", "me", "r2", "rs", "ng", "nm"], "w": ["w{}"], "w2": ["w2{}"], "dx": ["dx{}"]}))
        s_exp = Steps(sem("s_exp"), [f"{n},{c}" for n in range(NS) for c in range(CT)])
        s_bx = Steps(sem("s_bx"), [f"{n},{c}" for n in range(NS) for c in range(2)])
        s_scan = Steps(sem("s_scan"), [f"{n},{c}" for n in range(NS) for c in range(CT)])
        s_tr = Steps(sem("s_tr"), [f"{n},{c}" for n in range(NS) for c in range(TB)])
        s_acc = Steps(sem("s_acc"), [f"{n},{c}" for n in range(NS) for c in range(TB)])
        b_pe = Steps(sem("b_pe"), steps_of("pe", "B", {"y": ["y{}"], "wo": ["wo{}"], "xnT": ["xnT{}"], "rt": ["rt{}"],
                                                       "logit": ["lg"], "logit_rows": ["lt"], "gT": ["gT"]}))
        b_act = Steps(sem("b_act"), steps_of("act", "B", {"t": numbered("t"), "xn": numbered("xn"), "xnT": ["xnT{}"], "rt": ["rt{}"], "gelu": ["gelu"], "logit": ["lc"], "ex": ["ex"], "gT": ["gT"]}))
        b_dve = Steps(sem("b_dve"), steps_of("dve", "B", {"keep": ["keep"], "u": ["u{}"], "o": ["o{}"], "r": ["r{}"], "st": numbered("st"),
                                                          "ag": numbered("ag"), "x1": ["x1"], "st1": numbered("s1"), "ag1": numbered("a1"),
                                                          "cum": ["cum{}"], "lb": ["lb"], "mx": ["mx"], "sub": ["sub"], "sm": ["sm"],
                                                          "sn": ["sn"], "rc": ["rc"], "wa": ["wa"]}))
        b_pool = Steps(sem("b_pool"), ["ve", "rb", "ng", "nm", "ve1", "rb1", "ng1", "nm1"])
        l_pe = Steps(sem("l_pe"), steps_of("pe", "L", {"cum": ["cum{}"], "xv": ["xv{}"], "pt": ["pt{}"], "out": ["out{}"]}))
        l_act = Steps(sem("l_act"), steps_of("act", "L", {"cum": ["cum{}"], "pt": ["pt{}"], "out": ["out{}"], "t": numbered("t")}))
        l_dve = Steps(sem("l_dve"), steps_of("dve", "L", {"pr": ["pr{}"], "st": numbered("st"), "ag": numbered("ag")}))
        l_pool = Steps(sem("l_pool"), ["ve", "rs", "ng", "nm", "x0", "x1"])
        xf_in = sem("xf_in")
        xb_in = [sem(f"xb_in{i}") for i in range(2)]
        stored = [sem(f"stored{i}") for i in range(2)]
        B_out = sem("B_out")
        B_in = [sem(f"B_in{i}") for i in range(BB_RING)]
        w_ld = sem("w_ld")
        e_ld = sem("e_ld")
        w_rate = sem("w_rate")
        w_pe = sem("w_pe")
        w_act = sem("w_act")
        w_dve = sem("w_dve")
        w_pool = sem("w_pool")
        passed = {name: sem(f"passed_{name}") for name in ("sp", "pool", "pe", "act", "dve")}

        def reading_ends(stage, task, k):
            if stage == "F":
                return {"hT": (f_act, f"hT{k}"), "xs": (f_dve, f"cvC{k}"), "res": (f_act, f"res{k}"),
                        "proj": (f_act, "proj"), "Ct": (f_act, "Ct"), "dt": (f_act, f"rl{k}")}[task]
            if stage == "B":
                return {"y": (b_dve, f"u{k}"), "wo": (b_dve, f"r{k + 1}"), "xnT": (b_dve, f"cum{k}"),
                        "rt": (b_act, f"rt{k}"), "logit": (b_act, "lc"), "logit_rows": (b_dve, "lb"), "gT": (b_act, "gT")}[task]
            return {"cum": (l_act, f"cum{k}"), "xv": (l_dve, f"pr{k}"), "pt": (l_act, f"pt{k}"), "out": (l_act, f"out{k // 2}")}[task]

        numbers, uses_a_period = bank_numbers()

        class Use:

            def __init__(self, tensor, sem, free_at):
                self.bank, self.sem, self.free_at = tensor, sem, free_at

        def bank_of(stage, task, k, batch):
            periods, use = numbers[stage, task, k - k % SHARE_A_BANK.get(task, 1)]
            return (uses_a_period * ((batch.const + 1 + periods) % 2) + use) % 4

        def walk(engine, name, prologue, tasks, scan_part):
            beats = plan(name)
            held = [None] * 4

            def run(stage, task, k, batch):
                use = None
                if name == "pe":
                    at = bank_of(stage, task, k, batch)
                    before = held[at]
                    use = Use(bank[at], before[0].sem, before[0].done(before[1], before[2])) if before else Use(bank[at], w_pool, 2)
                    if k % SHARE_A_BANK.get(task, 1) == 0:
                        steps, step = reading_ends(stage, task, k)
                        held[at] = (steps, batch, step)
                elif (stage, task) in FILLED_BY:
                    filler = FILLED_BY[stage, task]
                    use = Use(bank[bank_of(stage, filler, 2 * k if task == "out" else k, batch)], None, None)
                tasks[stage, task](batch, k, use)

            def period(q):
                for at in range(BEATS):
                    scan_part(q, at // 8, at % 8)
                    for periods, stage, task, k in beats[at]:
                        batch = q.shift(1 - periods)
                        if batch.exists:
                            run(stage, task, k, batch)

            prologue()
            for q in (-1, 0, 1):
                period(Batch(q))
            turns = (NB - 4) // 2
            with engine.Fori(0, turns) as turn:
                if name == "pe":
                    held[:] = [(s, Batch(b.const, turn), n) for s, b, n in held]
                start = list(held)
                period(Batch(2, turn))
                period(Batch(3, turn))
                if name == "pe":
                    for (s, b, n), (s2, b2, n2) in zip(start, held):
                        assert s is s2 and n == n2 and b2.const == b.const + 2
            held[:] = [h and (h[0], Batch(h[1].const + 2 * (turns - 1)), h[2]) for h in held]
            for q in range(NB - 2, NB + 3):
                period(Batch(q))

        stage_V = [h[0][:, 0:2, :], h[0][:, 2:4, :]]
        stage_W = [h[1][:, 0:2, :], h[1][:, 2:4, :]]
        stage_U = [bx[0][:, :, :], bx[1][:, :, :]]
        raw = yT[:, :, :].rearrange("p a (b c) -> p (a b) c", b=2)
        wq_raw, wk_raw, winv_raw, wo_raw = (raw[:, 2 * i:2 * i + 2, :] for i in range(4))
        r1_raw = o_rows[:, 0:2, :]
        r2_raw = o_rows[0:KE, 2, :]
        b_raw = o_rows[0:2 * KE, 3, :]
        tr = dx[1][:, :, :].rearrange("p a (b c) -> p (a b) c", b=2)
        winvT, r1T, woT, wqiT = (tr[:, 2 * i:2 * i + 2, :] for i in range(4))
        wkiT = cumT[:, 0, :].rearrange("p (a b) -> p a b", a=2)
        bT = cumT[:, 1, 0:2 * 2 * KE].rearrange("p (a b) -> p a b", a=2)
        bias_raw = logits
        def square_T(raw_w):
            return [(a * D + f * P, a * D + (f + 1) * P, raw_w[:, f, a * P:(a + 1) * P], None) for a in range(DT) for f in range(DT)]

        def product(lhs, rhs):
            return [(m * D, (m + 1) * D, lhs[:, t, m * P:(m + 1) * P], rhs[:, t, :], t == 0, t == DT - 1)
                    for m in range(DT) for t in range(DT)]

        jobs = []

        def job(mms, dst, width, depends, scaled=None, parts=P):
            jobs.append((mms, dst, width, depends, scaled, parts))
            return len(jobs) - 1

        flat = lambda ap: ap.rearrange("p a b -> p (a b)")
        j_winvT = job(square_T(winv_raw), flat(winvT), 2 * D, -1)
        j_r1T = job(square_T(r1_raw), flat(r1T), 2 * D, -1)
        j_woT = job(square_T(wo_raw), flat(woT), 2 * D, -1)
        job([(t * KE, (t + 1) * KE, r2_raw[:, t * P:(t + 1) * P], None) for t in range(DT)], w2_padded[:, :, KE:2 * KE], 2 * KE, -1, "w2")
        j_bT = job([(t * 2 * KE, (t + 1) * 2 * KE, b_raw[:, t * P:(t + 1) * P], None) for t in range(DT)], bT, 4 * KE, -1, "b")
        j_wqiT = job(product(winvT, wq_raw), flat(wqiT), 2 * D, j_winvT)
        j_wkiT = job(product(winvT, wk_raw), flat(wkiT), 2 * D, j_winvT)
        for br in range(2):
            for lhs, rhs, dst, dep in ((wq_raw if br == 0 else wqiT, stage_V[br], q_to_expert[br], j_wqiT),
                                       (wk_raw if br == 0 else wkiT, stage_W[br], k_to_expert[br], j_wkiT)):
                for m in range(DT):
                    job([(0, KR, lhs[:, t, m * P:(m + 1) * P], rhs[:, t, :], t == 0, t == DT - 1) for t in range(DT)],
                        dst[:, m, :], KR, dep)
            job(product(wq_raw if br == 0 else wqiT, r1T), flat(q_to_router[br]), 2 * D, j_wkiT)
        for br in range(2):
            for pair in range(2):
                mms = []
                for i in range(2):
                    kt = 2 * pair + i
                    mms += [(i * D, (i + 1) * D, stage_U[br][:, t, kt * P:(kt + 1) * P], woT[:, t, :], t == 0, t == DT - 1) for t in range(DT)]
                k0 = 4 * br + 2 * pair
                job(mms, flat(expert_to_out[:, k0:k0 + 2, :]), 2 * D, j_woT, "all" if br else None)
        job([(0, D, bT[:, t, :], woT[:, t, :], t == 0, t == DT - 1) for t in range(DT)], bias_to_out[:, :], D, j_bT, None, 2 * KE)
        job_bank = decay + stateT
        job_beats = [JOBS_FROM + JOBS_EVERY * i for i in range(len(jobs))]
        assert job_beats[-1] < BEATS

        block = ctx.enter_context(nc.Block())

        N_WEIGHTS, N_EXPERT = [0], [0]

        @block.sync
        def _(sp):
            def load(dst, src):
                sp.dma_start(dst, src).then_inc(w_ld, 16)
                N_WEIGHTS[0] += 1

            def load_expert(dst, src):
                sp.dma_start(dst, src).then_inc(e_ld, 16)
                N_EXPERT[0] += 1

            def rows_of(ap):
                return ap.rearrange("b (j p) d -> b p j d", p=P)

            x_rows, out_rows = rows_of(x), rows_of(out)

            def prologue():
                sp.dma_start(x_front[:, :, :], x_rows[0]).then_inc(xf_in, 16)
                square = "(t p) n -> p t n"
                load(w_in_sb[:, :, :], w_in.rearrange(square, p=P))
                for dst, src in ((norm_sb, norm_scale), (conv_b_sb, conv_b), (skip_sb, D_skip), (b_dt_sb, b_dt), (b1_sb, router_b1)):
                    load(dst[:, :], src.rearrange("(t p) -> p t", p=P))
                for c in range(CT):
                    load(conv_w_sb[:, c, :], conv_w[:, 0, c * P:(c + 1) * P].rearrange("k p -> p k"))
                load(w_xproj_sb[:, :, :], w_xproj.rearrange(square, p=P))
                load(w_dt_sb[:, :], w_dt)
                load(decay_rate[:, :, :], A_log.rearrange(square, p=P))
                load(alpha_sb[:, :], alpha_bi.partition_broadcast(P))
                load(bias_raw[:, 0, 0, :], router_b2.rearrange("(o k) -> o k", o=1).partition_broadcast(P).rearrange("p o k -> p (o k)"))
                load(bias_raw[:, 0, 1, :], expert_bias.rearrange("(o k) -> o k", o=1).partition_broadcast(P).rearrange("p o k -> p (o k)"))
                load_expert(wq_raw, W_Q.rearrange(square, p=P))
                load_expert(wk_raw, W_K.rearrange(square, p=P))
                load_expert(winv_raw, W_inv.rearrange(square, p=P))
                load_expert(wo_raw, W_O.rearrange(square, p=P))
                load_expert(r1_raw, router_w1.rearrange(square, p=P))
                load_expert(r2_raw, router_w2)
                load_expert(o_rows[0:KE, 3, :], b_fwd)
                load_expert(o_rows[KE:2 * KE, 3, :], b_inv)
                for staged, weights in ((stage_V, (V_fwd, W_inv_exp)), (stage_W, (W_fwd, V_inv)), (stage_U, (U_fwd, U_inv))):
                    for br in range(2):
                        for t in range(DT):
                            load_expert(staged[br][:, t, :].rearrange("p (k r) -> p k r", k=KE),
                                        weights[br][:, t * P:(t + 1) * P, :].rearrange("k p r -> p k r"))
                load_expert(w_out_sb[:, :, :], w_out.rearrange(square, p=P))

            def row_of_B(batch, n):
                free, back = user_before(batch, n, NS, BB_RING)
                if free.exists:
                    sp.wait_ge(s_bx.sem, s_bx.done(free, f"{back},1"))
                if n == 0:
                    sp.sem_inc(passed["sp"], 1)
                    sp.wait_ge(B_out, batch.count(16, 16))
                sp.dma_start(B_rows[:, n % BB_RING, :],
                             B_dram[batch.parity, n:n + 1, :].partition_broadcast(P).rearrange("p o t -> p (o t)")
                             ).then_inc(B_in[n % BB_RING], 16)

            def load_x_front(batch, k, use):
                nxt = batch.shift(1)
                if nxt.turn is None and nxt.const >= NB:
                    return
                sp.wait_ge(f_pe.sem, f_pe.done(batch, "hT1"))
                sp.sem_inc(passed["sp"], 1)
                sp.dma_start(x_front[:, :, :], nxt.dram(x_rows)).then_inc(xf_in, 16)

            def write_B(batch, k, use):
                sp.wait_ge(f_act.sem, f_act.done(batch, "proj"))
                sp.dma_start(B_dram[batch.parity], projT[RANK:RANK + NS, :]).then_inc(B_out, 16)

            def first_rows(batch, k, use):
                row_of_B(batch, k)

            def load_x_back(batch):
                if batch.turn is not None or batch.const >= 2:
                    sp.wait_ge(stored[batch.parity], batch.half_count(16, 0))
                    sp.sem_inc(passed["sp"], 1)
                sp.dma_start(x_back[batch.parity][:, :, :], batch.dram(x_rows)).then_inc(xb_in[batch.parity], 16)

            def store(batch, k, use):
                sp.wait_ge(l_pool.sem, l_pool.done(batch, "x1"))
                sp.sem_inc(passed["sp"], 1)
                sp.dma_start(batch.dram(out_rows), x_back[batch.parity][:, :, :]).then_inc(stored[batch.parity], 16)

            def scan_part(q, slot, beat):
                if beat == 0 and q.exists:
                    if slot + BB_RING - 1 < NS:
                        row_of_B(q, slot + BB_RING - 1)
                    if slot == 12:
                        load_x_back(q)

            walk(sp, "sp", prologue, {("F", "x"): load_x_front,
                                ("F", "B"): write_B, ("F", "row"): first_rows, ("L", "store"): store}, scan_part)
            for i in range(2):
                sp.wait_ge(stored[i], NB // 2 * 16)

        @block.gpsimd
        def _(pool):
            def prologue():
                chain = [0]

                def link(ins):
                    chain[0] += 1
                    ins.then_inc(w_pool, 1)
                    pool.wait_ge(w_pool, chain[0])

                link(pool.memset(ident[:, :], 0.0))
                link(pool.affine_select(out=ident[:, :], in_=ident[:, :], compare_op=ALU.not_equal, fill=1.0,
                                        base=0, pattern=[[-1, P]], channel_multiplier=1))
                link(pool.memset(minus_half[:, :], -0.5))
                link(pool.memset(minus_one[:, :], -1.0))
                link(pool.memset(w2_padded[:, :, :], 0.0))
                link(pool.memset(one[:, :], 1.0))
                link(pool.iota(n_valid[:, :, :], pattern=[[P, TB], [0, 2]], base=1, channel_multiplier=1,
                               allow_small_or_imprecise_dtypes=True))

            def rstd(steps, batch, mv, ve, rs, nm, names):
                pool.tensor_scalar(ve[:, :], mv[:, :, 1], EPS, None, ALU.add).then_inc(steps.step(names[0]), 1)
                pool.wait_ge(steps.sem, steps.done(batch, names[0]))
                pool.tensor_tensor(rs[:, :], ve[:, :], minus_half[:, :], ALU.pow).then_inc(steps.step(names[1]), 1)
                if nm is not None:
                    pool.tensor_tensor(nm[:, :], mv[:, :, 0], minus_one[:, :], ALU.mult).then_inc(steps.step(names[2]), 1)
                    pool.wait_ge(steps.sem, steps.done(batch, names[2]))
                    pool.tensor_tensor(nm[:, :], nm[:, :], rs[:, :], ALU.mult).then_inc(steps.step(names[3]), 1)

            def front_rstd(b, k, use):
                pool.wait_ge(f_dve.sem, f_dve.done(b, "ag3"))
                pool.sem_inc(passed["pool"], 1)
                r = r_x0[b.parity]
                rstd(f_pool, b, mv_f, ve_f, r, None, ("ve", "r1"))
                pool.wait_ge(f_pool.sem, f_pool.done(b, "r1"))
                pool.tensor_tensor(ms_f[:, :], mv_f[:, :, 1], r[:, :], ALU.mult).then_inc(f_pool.step("ms"), 1)
                pool.wait_ge(f_pool.sem, f_pool.done(b, "ms"))
                pool.tensor_tensor(ms_f[:, :], ms_f[:, :], r[:, :], ALU.mult).then_inc(f_pool.step("mr"), 1)
                pool.wait_ge(f_pool.sem, f_pool.done(b, "mr"))
                pool.sem_inc(passed["pool"], 1)
                pool.tensor_scalar(ms_f[:, :], ms_f[:, :], EPS, None, ALU.add).then_inc(f_pool.step("me"), 1)
                pool.wait_ge(f_pool.sem, f_pool.done(b, "me"))
                pool.tensor_tensor(r2_f[:, :], ms_f[:, :], minus_half[:, :], ALU.pow).then_inc(f_pool.step("r2"), 1)
                pool.wait_ge(f_pool.sem, f_pool.done(b, "r2"))
                pool.tensor_tensor(rs_f[:, :], r2_f[:, :], r[:, :], ALU.mult).then_inc(f_pool.step("rs"), 1)
                pool.tensor_tensor(nm_f[:, :], mv_f[:, :, 0], minus_one[:, :], ALU.mult).then_inc(f_pool.step("ng"), 1)
                pool.wait_ge(f_pool.sem, f_pool.done(b, "ng"))
                pool.tensor_tensor(nm_f[:, :], nm_f[:, :], rs_f[:, :], ALU.mult).then_inc(f_pool.step("nm"), 1)

            def w_task(b, c, use):
                e, v = scratch[:, c % 2, :], scratch[:, 2 + c % 2, :]
                pool.wait_ge(f_act.sem, f_act.done(b, f"u{c}"))
                pool.tensor_tensor(v, e, v, ALU.subtract).then_inc(f_pool.step(f"w{c}"), 1)

            def w2_task(b, c, use):
                v = scratch[:, 2 + c % 2, :]
                pool.wait_ge(f_pool.sem, f_pool.done(b, f"w{c}"))
                pool.tensor_tensor(v, v, dx[b.parity][:, c, :], ALU.add).then_inc(f_pool.step(f"w2{c}"), 1)

            def dx_task(b, c, use):
                pool.wait_ge(f_dve.sem, f_dve.done(b, f"d1{c}"))
                pool.tensor_tensor(dx[b.parity][:, c, :], delta[b.parity][:, c, :], xs[b.parity][:, c, :], ALU.mult).then_inc(f_pool.step(f"dx{c}"), 1)

            def x_task(b, k, use):
                half = slice(2 * k, 2 * k + 2)
                pool.wait_ge(l_act.sem, l_act.done(b, f"t{2 * k + 1}"))
                pool.tensor_tensor(x_back[b.parity][:, half, :], x_back[b.parity][:, half, :], o_rows[:, half, :], ALU.add).then_inc(l_pool.step(f"x{k}"), 1)

            def back_rstd(b, k, use):
                pool.wait_ge(b_dve.sem, b_dve.done(b, "ag3"))
                pool.sem_inc(passed["pool"], 1)
                rstd(b_pool, b, mv_b, ve_b, rs_b, nm_b, ("ve", "rb", "ng", "nm"))

            def x1_rstd(b, k, use):
                pool.wait_ge(b_dve.sem, b_dve.done(b, "a13"))
                pool.sem_inc(passed["pool"], 1)
                rstd(b_pool, b, mv_1, ve_1, rs_1, nm_1, ("ve1", "rb1", "ng1", "nm1"))

            def out_rstd(b, k, use):
                pool.wait_ge(l_dve.sem, l_dve.done(b, "ag3"))
                pool.sem_inc(passed["pool"], 1)
                rstd(l_pool, b, mv_o, ve_o, rs_o, nm_o, ("ve", "rs", "ng", "nm"))

            def scan_part(q, n, beat):
                if not q.exists or beat % 4:
                    return
                half = beat // 4
                if q.turn is None and q.const == 0 and n == 0 and half == 0:
                    pool.wait_ge(w_act, len(jobs))
                if n == 0 and half == 0:
                    pool.wait_ge(f_pool.sem, f_pool.done(q, "dx3"))
                if half == 0:
                    rows_of_place = len(range(n % BB_RING, NS, BB_RING))
                    pool.wait_ge(B_in[n % BB_RING], q.count(16 * rows_of_place, 16 * (n // BB_RING + 1)))
                use = 2 * n + half
                free, back = user_before(q, use, 2 * NS, BX_RING)
                if free.exists:
                    pool.wait_ge(s_scan.sem, s_scan.done(free, f"{back // 2},{back % 2 * 2 + 1}"))
                row = B_rows[:, n % BB_RING, :].rearrange("p (o t) -> p o t", o=1).broadcast_to([P, CT // 2, T])
                pool.tensor_tensor(bx[use % BX_RING][:, :, :], dx[q.parity][:, 2 * half:2 * half + 2, :], row, ALU.mult).then_inc(s_bx.step(f"{n},{half}"), 1)

            walk(pool, "pool", prologue, {("F", "rs"): front_rstd, ("F", "w"): w_task, ("F", "w2"): w2_task, ("F", "dx"): dx_task, ("L", "x"): x_task, ("B", "rb"): back_rstd,
                                  ("B", "rb1"): x1_rstd, ("L", "rs"): out_rstd}, scan_part)

        @block.tensor
        def _(pe):
            def prologue():
                pe.wait_ge(w_ld, 16 * N_WEIGHTS[0])
                pe.wait_ge(w_pool, 2)

            def combine_weights(i):
                mms, dst, width, depends, scaled, parts = jobs[i]
                if i == 0:
                    pe.wait_ge(e_ld, 16 * N_EXPERT[0])
                if max(i - 3, depends + 1) > 0:
                    pe.wait_ge(w_act, max(i - 3, depends + 1))
                for mm in mms:
                    if mm[3] is None:
                        src = mm[2]
                        k = src.shape[0]
                        last = pe.transpose(job_bank[i % 4][:, mm[0]:mm[1]], src, ident[0:k, 0:k])
                    else:
                        last = pe.matmul(job_bank[i % 4][0:parts, mm[0]:mm[1]], mm[2], mm[3], start=mm[4], stop=mm[5])
                last.then_inc(w_pe, 1)

            def matmuls(out_ap, pairs):
                for i, (lhsT, rhs) in enumerate(pairs):
                    last = pe.matmul(out_ap, lhsT, rhs, start=(i == 0), stop=(i == len(pairs) - 1))
                return last

            def rows_T(b, t, use, src, steps, name):
                pe.wait_ge(use.sem, use.free_at)
                for j in range(TB):
                    last = pe.transpose(use.bank[:, j * P:(j + 1) * P], src[:, j, t * P:(t + 1) * P], ident[:, :])
                last.then_inc(steps.step(name), 1)

            def hT_task(b, t, use):
                pe.wait_ge(f_act.sem, f_act.done(b, "h3"))
                rows_T(b, t, use, x_front, f_pe, f"hT{t}")

            def xs_task(b, c, use):
                if c == 0:
                    pe.wait_ge(f_act.sem, f_act.done(b, "hT1"))
                if use.sem is f_act.sem:
                    pe.sem_inc(passed["pe"], 1)
                pe.wait_ge(use.sem, use.free_at)
                matmuls(use.bank[:, :], [(w_in_sb[:, t, c * P:(c + 1) * P], hT[:, t, :]) for t in range(DT)]).then_inc(f_pe.step(f"xs{c}"), 1)

            def res_task(b, c, use):
                pe.wait_ge(use.sem, use.free_at)
                matmuls(use.bank[:, :], [(w_in_sb[:, t, DI + c * P:DI + (c + 1) * P], hT[:, t, :]) for t in range(DT)]).then_inc(f_pe.step(f"res{c}"), 1)

            def proj_task(b, k, use):
                pe.wait_ge(f_act.sem, f_act.done(b, "silux"))
                if use.sem is f_act.sem:
                    pe.sem_inc(passed["pe"], 1)
                pe.wait_ge(use.sem, use.free_at)
                matmuls(use.bank[0:NPROJ, :], [(w_xproj_sb[:, c, :], xs[b.parity][:, c, :]) for c in range(CT)]).then_inc(f_pe.step("proj"), 1)

            def Ct_task(b, k, use):
                pe.wait_ge(use.sem, use.free_at)
                if use.sem is f_act.sem:
                    pe.sem_inc(passed["pe"], 1)
                pe.wait_ge(f_act.sem, f_act.done(b, "proj"))
                pe.sem_inc(passed["pe"], 1)
                for j in range(TB):
                    last = pe.transpose(use.bank[:, j * NPROJ:(j + 1) * NPROJ], projT[:, j * P:(j + 1) * P], ident[0:NPROJ, 0:NPROJ])
                last.then_inc(f_pe.step("Ct"), 1)

            def dt_task(b, c, use):
                if c == 0:
                    pe.wait_ge(f_act.sem, f_act.done(b, "proj"))
                if use.sem is f_act.sem:
                    pe.sem_inc(passed["pe"], 1)
                pe.wait_ge(use.sem, use.free_at)
                matmuls(use.bank[:, :], [(w_dt_sb[:, c * P:(c + 1) * P], projT[0:RANK, :])]).then_inc(f_pe.step(f"dt{c}"), 1)

            def y_task(b, c, use):
                if c == 0:
                    pe.wait_ge(s_acc.sem, s_acc.done(b, f"{NS - 1},{TB - 1}"))
                pe.wait_ge(use.sem, use.free_at)
                for j in range(TB):
                    last = pe.transpose(use.bank[:, j * P:(j + 1) * P], yT[:, j, c * P:(c + 1) * P], ident[:, :])
                last.then_inc(b_pe.step(f"y{c}"), 1)

            def wo_task(b, k, use):
                if k == 0:
                    pe.wait_ge(b_dve.sem, b_dve.done(b, "o3"))
                if k % 2 == 0:
                    if use.sem is b_dve.sem:
                        pe.sem_inc(passed["pe"], 1)
                    pe.wait_ge(use.sem, use.free_at)
                matmuls(use.bank[:, k % 2 * D:(k % 2 + 1) * D],
                        [(res[b.parity][:, c, k * P:(k + 1) * P], w_out_sb[:, c, :]) for c in range(CT)]).then_inc(b_pe.step(f"wo{k}"), 1)

            def xnT_task(b, t, use):
                pe.wait_ge(b_act.sem, b_act.done(b, "xn3"))
                rows_T(b, t, use, rows, b_pe, f"xnT{t}")

            def rt_task(b, k, use):
                br, m = k // 2, k % 2
                if k == 0:
                    pe.wait_ge(b_act.sem, b_act.done(b, "xnT1"))
                if use.sem is b_act.sem:
                    pe.sem_inc(passed["pe"], 1)
                pe.wait_ge(use.sem, use.free_at)
                matmuls(use.bank[:, :], [(q_to_router[br][:, t, m * P:(m + 1) * P], xnT[:, t, :]) for t in range(DT)]).then_inc(b_pe.step(f"rt{k}"), 1)

            def logit_task(b, k, use):
                pe.wait_ge(b_act.sem, b_act.done(b, "gelu"))
                if use.sem is b_act.sem:
                    pe.sem_inc(passed["pe"], 1)
                pe.wait_ge(use.sem, use.free_at)
                matmuls(use.bank[0:2 * KE, :], [(w2_padded[:, m, (1 - br) * KE:(3 - br) * KE], scratch[:, 2 * br + m, :])
                                                for br in range(2) for m in range(DT)]).then_inc(b_pe.step("lg"), 1)

            def logit_rows_task(b, k, use):
                pe.wait_ge(use.sem, use.free_at)
                if use.sem is b_act.sem:
                    pe.sem_inc(passed["pe"], 1)
                pe.wait_ge(b_act.sem, b_act.done(b, "lc"))
                pe.sem_inc(passed["pe"], 1)
                for j in range(TB):
                    last = pe.transpose(use.bank[:, j * 2 * KE:(j + 1) * 2 * KE], logitT[:, j * P:(j + 1) * P], ident[4 * KE:6 * KE, 4 * KE:6 * KE])
                last.then_inc(b_pe.step("lt"), 1)

            def gateT_task(b, k, use):
                pe.wait_ge(b_dve.sem, b_dve.done(b, "wa"))
                if use.sem is b_dve.sem:
                    pe.sem_inc(passed["pe"], 1)
                pe.wait_ge(use.sem, use.free_at)
                for j in range(TB):
                    last = pe.transpose(use.bank[0:2 * KE, j * P:(j + 1) * P], gate[:, j, :], ident[:, :])
                last.then_inc(b_pe.step("gT"), 1)

            def cum_task(b, u, use):
                j, br = u // 2, u % 2
                if u == 0:
                    pe.wait_ge(b_dve.sem, b_dve.done(b, "cum1"))
                if use.sem is b_dve.sem:
                    pe.sem_inc(passed["pe"], 1)
                pe.wait_ge(use.sem, use.free_at)
                matmuls(use.bank[:, :], [(cumT[:, t, j * P:(j + 1) * P], k_to_expert[br][:, t, :]) for t in range(DT)]).then_inc(l_pe.step(f"cum{u}"), 1)

            def xv_task(b, u, use):
                j, br = u // 2, u % 2
                pe.wait_ge(use.sem, use.free_at)
                matmuls(use.bank[:, :], [(xnT[:, t, j * P:(j + 1) * P], q_to_expert[br][:, t, :]) for t in range(DT)]).then_inc(l_pe.step(f"xv{u}"), 1)

            def pt_task(b, u, use):
                pe.wait_ge(l_dve.sem, l_dve.done(b, f"pr{u}"))
                if use.sem is l_dve.sem:
                    pe.sem_inc(passed["pe"], 1)
                pe.wait_ge(use.sem, use.free_at)
                for i in range(KR // P):
                    last = pe.transpose(use.bank[:, i * P:(i + 1) * P], prod[u % 2][:, i * P:(i + 1) * P], ident[:, :])
                last.then_inc(l_pe.step(f"pt{u}"), 1)

            def out_task(b, u, use):
                j, br = u // 2, u % 2
                pe.wait_ge(l_act.sem, l_act.done(b, f"pt{u}"))
                if br == 0:
                    if use.sem is l_act.sem:
                        pe.sem_inc(passed["pe"], 1)
                    pe.wait_ge(use.sem, use.free_at)
                if u == 1:
                    pe.wait_ge(b_act.sem, b_act.done(b, "gT"))
                for i in range(4):
                    last = pe.matmul(use.bank[:, 0:D], prodT[:, 4 * br + i, :], expert_to_out[:, 4 * br + i, :], start=(br == 0 and i == 0), stop=False)
                if br:
                    last = pe.matmul(use.bank[:, 0:D], gateT[:, j * P:(j + 1) * P], bias_to_out[:, :], start=False, stop=True)
                last.then_inc(l_pe.step(f"out{u}"), 1)

            def scan_part(q, slot, beat):
                if q.turn is None and q.const == -1 and 8 * slot + beat in job_beats:
                    combine_weights(job_beats.index(8 * slot + beat))
                if beat % 2:
                    return
                j = beat // 2
                batch, n = (q, slot - 1) if slot else (q.shift(-1), NS - 1)
                if not batch.exists:
                    return
                if j == 0 and n == 0 and batch.turn is None and batch.const == 0:
                    pe.wait_ge(w_act, len(jobs))
                if j == 0:
                    pe.wait_ge(s_scan.sem, s_scan.done(batch, f"{n},{CT - 1}"))
                back = n * TB + j - 2
                free = batch if back >= 0 else batch.shift(-1)
                if free.exists:
                    pe.wait_ge(s_acc.sem, s_acc.done(free, f"{back % (NS * TB) // TB},{back % TB}"))
                for c in range(CT):
                    last = pe.transpose(stateT[j % 2][:, c * P:(c + 1) * P], h[n % 2][:, c, j * P:(j + 1) * P], ident[:, :])
                last.then_inc(s_tr.step(f"{n},{j}"), 1)

            walk(pe, "pe", prologue, {("F", "hT"): hT_task, ("F", "xs"): xs_task, ("F", "res"): res_task, ("F", "proj"): proj_task,
                                ("F", "Ct"): Ct_task, ("F", "dt"): dt_task, ("B", "y"): y_task, ("B", "wo"): wo_task, ("B", "xnT"): xnT_task,
                                ("B", "rt"): rt_task, ("B", "logit"): logit_task, ("B", "logit_rows"): logit_rows_task, ("B", "gT"): gateT_task,
                                ("L", "cum"): cum_task, ("L", "xv"): xv_task, ("L", "pt"): pt_task, ("L", "out"): out_task}, scan_part)

        @block.scalar
        def _(act):
            def prologue():
                act.preload_act_table_set(EXP_SET)
                act.wait_ge(w_ld, 16 * N_WEIGHTS[0])
                act.activation(decay_rate[:, :, :], decay_rate[:, :, :], ACT.Exp).then_inc(w_rate, 1)

            def keep_combined(i):
                mms, dst, width, depends, scaled, parts = jobs[i]
                act.wait_ge(w_pe, i + 1)
                src = job_bank[i % 4][0:parts, 0:width]
                if scaled == "b":
                    both = src.rearrange("p (a b) -> p a b", a=2)
                    act.activation(dst[:, :, 0:KE], both[:, :, 0:KE], ACT.Copy)
                    act.activation(dst[:, :, KE:2 * KE], both[:, :, KE:2 * KE], ACT.Copy, scale=alpha_sb[:, 0:1]).then_inc(w_act, 1)
                elif scaled == "w2":
                    act.wait_ge(w_pool, 7)
                    act.activation(dst, src.rearrange("p (a b) -> p a b", a=DT), ACT.Copy).then_inc(w_act, 1)
                elif scaled == "all":
                    act.activation(dst, src, ACT.Copy, scale=alpha_sb[:, 0:1]).then_inc(w_act, 1)
                else:
                    act.activation(dst, src, ACT.Copy).then_inc(w_act, 1)

            def centre(steps, b, dst, src, rs, nm, name):
                for j in range(TB):
                    act.activation(dst[:, j, :], src[:, j, :], ACT.Identity, scale=rs[:, j:j + 1], bias=nm[:, j:j + 1]).then_inc(steps.step(f"{name}{j}"), 1)

            def h_task(b, k, use):
                act.wait_ge(f_pool.sem, f_pool.done(b, "nm"))
                centre(f_act, b, x_front, x_front, rs_f, nm_f, "h")

            def t_task(b, k, use):
                act.wait_ge(b_pool.sem, b_pool.done(b, "nm"))
                centre(b_act, b, rows, rows, rs_b, nm_b, "t")

            def xn_task(b, k, use):
                act.wait_ge(b_pool.sem, b_pool.done(b, "nm1"))
                centre(b_act, b, rows, x_back[b.parity], rs_1, nm_1, "xn")

            def out_centre(b, k, use):
                act.wait_ge(l_pool.sem, l_pool.done(b, "nm"))
                centre(l_act, b, o_rows, o_rows, rs_o, nm_o, "t")

            def hT_task(b, t, use):
                act.wait_ge(f_pe.sem, f_pe.done(b, f"hT{t}"))
                if t == 0 and (b.turn is not None or b.const > 0):
                    act.wait_ge(B_out, b.count(16, 0))
                act.activation(hT[:, t, :], use.bank[:, :], ACT.Copy, scale=norm_sb[:, t:t + 1]).then_inc(f_act.step(f"hT{t}"), 1)

            def xs_task(b, c, use):
                if c == 0:
                    if b.shift(-2).exists:
                        act.wait_ge(b_dve.sem, b_dve.done(b.shift(-2), "o3"))
                act.wait_ge(f_pe.sem, f_pe.done(b, f"xs{c}"))
                act.activation(xs[b.parity][:, c, :], use.bank[:, :], ACT.Identity,
                                          scale=conv_w_sb[:, c, TAPS - 1:TAPS], bias=conv_b_sb[:, c:c + 1]).then_inc(f_act.step(f"cv{c}"), 1)

            def res_task(b, c, use):
                if c == 0:
                    if b.shift(-2).exists:
                        act.wait_ge(b_pe.sem, b_pe.done(b.shift(-2), "wo3"))
                act.wait_ge(f_pe.sem, f_pe.done(b, f"res{c}"))
                act.activation(res[b.parity][:, c, :], use.bank[:, :], ACT.Copy).then_inc(f_act.step(f"res{c}"), 1)

            def silu_task(b, k, use):
                act.wait_ge(f_dve.sem, f_dve.done(b, "cvC3"))
                act.sem_inc(passed["act"], 1)
                act.preload_act_table_set("silu_and_others")
                act.activation(xs[b.parity][:, :, :], xs[b.parity][:, :, :], ACT.Silu).then_inc(f_act.step("silux"), 1)
                act.wait_ge(f_act.sem, f_act.done(b, "res3"))
                act.activation(res[b.parity][:, :, :], res[b.parity][:, :, :], ACT.Silu).then_inc(f_act.step("silur"), 1)
                act.preload_act_table_set(EXP_SET)

            def proj_task(b, k, use):
                act.wait_ge(f_pe.sem, f_pe.done(b, "proj"))
                act.activation(projT[:, :], use.bank[0:NPROJ, :], ACT.Copy).then_inc(f_act.step("proj"), 1)

            def Ct_task(b, k, use):
                act.wait_ge(f_pe.sem, f_pe.done(b, "Ct"))
                if b.shift(-2).exists:
                    act.wait_ge(s_acc.sem, s_acc.done(b.shift(-2), f"{NS - 1},{TB - 1}"))
                both = use.bank[:, 0:TB * NPROJ].rearrange("p (j n) -> p j n", j=TB)
                act.activation(C_tok[b.parity][:, :, :], both[:, :, RANK + NS:NPROJ], ACT.Copy).then_inc(f_act.step("Ct"), 1)

            def dt_task(b, c, use):
                e = scratch[:, c % 2, :]
                act.wait_ge(f_pe.sem, f_pe.done(b, f"dt{c}"))
                if c >= 2:
                    act.wait_ge(f_pool.sem, f_pool.done(b, f"w{c - 2}"))
                elif c == 0:
                    if b.shift(-2).exists:
                        act.wait_ge(b_pe.sem, b_pe.done(b.shift(-2), "lg"))
                    if b.shift(-2).exists:
                        act.wait_ge(s_bx.sem, s_bx.done(b.shift(-2), f"{NS - 1},1"))
                    if b.shift(-1).exists:
                        act.wait_ge(f_pool.sem, f_pool.done(b.shift(-1), "w3"))
                act.activation(e, use.bank[:, :], ACT.Abs, bias=b_dt_sb[:, c:c + 1]).then_inc(f_act.step(f"ab{c}"), 1)
                act.activation(dx[b.parity][:, c, :], use.bank[:, :], ACT.Relu, bias=b_dt_sb[:, c:c + 1]).then_inc(f_act.step(f"rl{c}"), 1)

            def ex_task(b, c, use):
                e, v = scratch[:, c % 2, :], scratch[:, 2 + c % 2, :]
                act.wait_ge(f_act.sem, f_act.done(b, f"ab{c}"))
                act.activation(e, e, ACT.Exp, scale=-1.0).then_inc(f_act.step(f"ex{c}"), 1)
                act.wait_ge(f_act.sem, f_act.done(b, f"ex{c}"))
                if c >= 2:
                    act.wait_ge(f_dve.sem, f_dve.done(b, f"d1{c - 2}"))
                act.activation(v, e, ACT.Identity, bias=one[:, 0:1]).then_inc(f_act.step(f"v{c}"), 1)

            def ln_task(b, c, use):
                e, v = scratch[:, c % 2, :], scratch[:, 2 + c % 2, :]
                act.activation(delta[b.parity][:, c, :], e, ACT.Ln, bias=one[:, 0:1]).then_inc(f_act.step(f"ln{c}"), 1)
                act.wait_ge(f_act.sem, f_act.done(b, f"v{c}"))
                act.activation(v, v, ACT.Identity, bias=minus_one[:, 0:1]).then_inc(f_act.step(f"u{c}"), 1)

            def xnT_task(b, t, use):
                act.wait_ge(b_pe.sem, b_pe.done(b, f"xnT{t}"))
                act.activation(xnT[:, t, :], use.bank[:, :], ACT.Copy).then_inc(b_act.step(f"xnT{t}"), 1)

            def rt_task(b, k, use):
                if k == 0:
                    if b.shift(1).exists:
                        act.wait_ge(f_dve.sem, f_dve.done(b.shift(1), "d13"))
                act.wait_ge(b_pe.sem, b_pe.done(b, f"rt{k}"))
                act.activation(scratch[:, k, :], use.bank[:, :], ACT.Identity, bias=b1_sb[:, k % 2:k % 2 + 1]).then_inc(b_act.step(f"rt{k}"), 1)

            def gelu_task(b, k, use):
                act.wait_ge(b_act.sem, b_act.done(b, "rt3"))
                act.sem_inc(passed["act"], 1)
                act.preload_act_table_set("gelu_and_others")
                act.activation(scratch[:, :, :], scratch[:, :, :], ACT.Gelu).then_inc(b_act.step("gelu"), 1)
                act.preload_act_table_set(EXP_SET)

            def logit_task(b, k, use):
                act.wait_ge(b_pe.sem, b_pe.done(b, "lg"))
                if b.shift(-1).exists:
                    act.wait_ge(l_pe.sem, l_pe.done(b.shift(-1), "out7"))
                act.activation(logitT[:, :], use.bank[0:2 * KE, :], ACT.Copy).then_inc(b_act.step("lc"), 1)

            def soft_exp(b, k, use):
                act.wait_ge(b_dve.sem, b_dve.done(b, "sub"))
                act.activation(logits[:, :, :, :], logits[:, :, :, :], ACT.Exp).then_inc(b_act.step("ex"), 1)

            def gateT_task(b, k, use):
                act.wait_ge(b_pe.sem, b_pe.done(b, "gT"))
                act.activation(gateT[:, :], use.bank[0:2 * KE, :], ACT.Copy).then_inc(b_act.step("gT"), 1)

            def cum_task(b, u, use):
                j, br = u // 2, u % 2
                act.wait_ge(l_pe.sem, l_pe.done(b, f"cum{u}"))
                if u >= 2:
                    act.wait_ge(l_dve.sem, l_dve.done(b, f"pr{u - 2}"))
                elif u == 0:
                    if b.shift(-1).exists:
                        act.wait_ge(l_dve.sem, l_dve.done(b.shift(-1), "pr7"))
                    act.wait_ge(b_dve.sem, b_dve.done(b, "wa"))
                for k in range(KE):
                    last = act.activation(cum_sb[u % 2][:, k * RK:(k + 1) * RK], use.bank[:, k * RK:(k + 1) * RK], ACT.Copy,
                                          scale=gate[:, j, br * KE + k:br * KE + k + 1])
                last.then_inc(l_act.step(f"cum{u}"), 1)

            def pt_task(b, u, use):
                br, j = u % 2, u // 2
                free = b if j else b.shift(-1)
                if free.exists:
                    act.wait_ge(l_pe.sem, l_pe.done(free, f"out{(u - 2) % 8}"))
                act.wait_ge(l_pe.sem, l_pe.done(b, f"pt{u}"))
                act.activation(flat(prodT[:, 4 * br:4 * br + 4, :]), use.bank[:, :], ACT.Copy).then_inc(l_act.step(f"pt{u}"), 1)

            def out_task(b, j, use):
                if j == 0:
                    if b.shift(-1).exists:
                        act.wait_ge(l_pool.sem, l_pool.done(b.shift(-1), "x1"))
                act.wait_ge(l_pe.sem, l_pe.done(b, f"out{2 * j + 1}"))
                act.activation(o_rows[:, j, :], use.bank[:, 0:D], ACT.Copy).then_inc(l_act.step(f"out{j}"), 1)

            def scan_part(q, n, beat):
                if q.turn is None and q.const == -1 and 8 * n + beat in job_beats:
                    keep_combined(job_beats.index(8 * n + beat))
                if not q.exists or beat % 2:
                    return
                c = beat // 2
                if q.turn is None and q.const == 0 and n == 0 and c == 0:
                    act.wait_ge(w_act, len(jobs))
                    act.wait_ge(w_dve, 1)
                if n == 0:
                    act.wait_ge(f_dve.sem, f_dve.done(q, f"d1{c}"))
                back = n * CT + c - 2
                free = q if back >= 0 else q.shift(-1)
                if free.exists:
                    act.wait_ge(s_scan.sem, s_scan.done(free, f"{back % (NS * CT) // CT},{back % CT}"))
                act.activation(decay[c % 2][:, :], delta[q.parity][:, c, :], ACT.Exp, scale=decay_rate[:, c, n:n + 1]).then_inc(s_exp.step(f"{n},{c}"), 1)

            walk(act, "act", prologue, {("F", "h"): h_task, ("B", "t"): t_task, ("B", "xn"): xn_task, ("L", "t"): out_centre, ("F", "hT"): hT_task, ("F", "xs"): xs_task, ("F", "res"): res_task, ("F", "silu"): silu_task,
                                 ("F", "proj"): proj_task, ("F", "Ct"): Ct_task, ("F", "dt"): dt_task, ("F", "ex"): ex_task, ("F", "ln"): ln_task, ("B", "xnT"): xnT_task, ("B", "rt"): rt_task,
                                 ("B", "gelu"): gelu_task, ("B", "logit"): logit_task, ("B", "ex"): soft_exp, ("B", "gT"): gateT_task,
                                 ("L", "cum"): cum_task, ("L", "pt"): pt_task, ("L", "out"): out_task}, scan_part)

        @block.vector
        def _(dve):
            def prologue():
                dve.wait_ge(w_rate, 1)
                dve.tensor_scalar(decay_rate[:, :, :], decay_rate[:, :, :], -1.0, None, ALU.mult).then_inc(w_dve, 1)
                both = top[:, 0:KE]
                dve.tensor_tensor(both, bias_raw[:, 0, 0, :], bias_raw[:, 0, 1, :], ALU.add).then_inc(w_dve, 1)
                dve.wait_ge(w_dve, 2)
                dve.tensor_copy(logit_bias[:, :, :, :].rearrange("p a b k -> p (a b) k"),
                                both.rearrange("p (o k) -> p o k", o=1).broadcast_to([P, TB * 2, KE])).then_inc(w_dve, 1)
                dve.wait_ge(w_dve, 3)
                dve.wait_ge(w_pool, 7)

            def stats(steps, src, st, name):
                for j in range(TB):
                    dve.bn_stats(st[:, j, :], src[:, j, :]).then_inc(steps.step(f"{name}{j}"), 1)

            def aggregate(steps, b, st, mv, stat, name):
                dve.wait_ge(steps.sem, steps.done(b, f"{stat}{TB - 1}"))
                dve.sem_inc(passed["dve"], 1)
                for j in range(TB):
                    dve.bn_aggr(mv[:, j, :], st[:, j, :]).then_inc(steps.step(f"{name}{j}"), 1)

            def front_stats(b, k, use):
                dve.wait_ge(xf_in, b.count(16, 16))
                stats(f_dve, x_front, st_f, "st")

            def front_aggregate(b, k, use):
                aggregate(f_dve, b, st_f, mv_f, "st", "ag")

            def tap(back, name, before):
                def task(b, c, use):
                    x_c = xs[b.parity][:, c, :]
                    dve.wait_ge(before[0].sem, before[0].done(b, f"{before[1]}{c}"))
                    dve.scalar_tensor_tensor(out=x_c[:, back:], in0=use.bank[:, 0:T - back], scalar=conv_w_sb[:, c, TAPS - 1 - back:TAPS - back],
                                             in1=x_c[:, back:], op0=ALU.mult, op1=ALU.add).then_inc(f_dve.step(f"{name}{c}"), 1)
                return task

            def d1_task(b, c, use):
                dve.wait_ge(f_pool.sem, f_pool.done(b, f"w2{c}"))
                dve.wait_ge(f_act.sem, f_act.done(b, f"ln{c}"))
                dve.tensor_tensor(delta[b.parity][:, c, :], delta[b.parity][:, c, :], scratch[:, 2 + c % 2, :], ALU.add).then_inc(f_dve.step(f"d1{c}"), 1)

            def keep_task(b, k, use):
                dve.tensor_copy(r_keep[:, :], r_x0[b.parity][:, :]).then_inc(b_dve.step("keep"), 1)

            def u_task(b, c, use):
                r = b.parity
                dve.wait_ge(b_pe.sem, b_pe.done(b, f"y{c}"))
                dve.scalar_tensor_tensor(out=xs[r][:, c, :], in0=xs[r][:, c, :], scalar=skip_sb[:, c:c + 1],
                                         in1=use.bank[:, :], op0=ALU.mult, op1=ALU.add).then_inc(b_dve.step(f"u{c}"), 1)

            def o_task(b, c, use):
                r = b.parity
                dve.wait_ge(b_dve.sem, b_dve.done(b, f"u{c}"))
                dve.tensor_tensor(res[r][:, c, :], xs[r][:, c, :], res[r][:, c, :], ALU.mult).then_inc(b_dve.step(f"o{c}"), 1)

            def r_task(b, j, use):
                if j == 0:
                    dve.wait_ge(xb_in[b.parity], b.half_count(16, 16))
                    dve.wait_ge(b_dve.sem, b_dve.done(b, "keep"))
                    if b.shift(-1).exists:
                        dve.wait_ge(b_pe.sem, b_pe.done(b.shift(-1), "xnT1"))
                if j % 2 == 0:
                    dve.wait_ge(b_pe.sem, b_pe.done(b, f"wo{j + 1}"))
                dve.scalar_tensor_tensor(out=rows[:, j, :], in0=x_back[b.parity][:, j, :], scalar=r_keep[:, j:j + 1],
                                         in1=use.bank[:, j % 2 * D:(j % 2 + 1) * D], op0=ALU.mult, op1=ALU.add).then_inc(b_dve.step(f"r{j}"), 1)

            def st_task(b, k, use):
                dve.wait_ge(b_dve.sem, b_dve.done(b, "r3"))
                stats(b_dve, rows, st_b, "st")

            def ag_task(b, k, use):
                aggregate(b_dve, b, st_b, mv_b, "st", "ag")

            def x1_task(b, k, use):
                dve.wait_ge(b_act.sem, b_act.done(b, "t3"))
                dve.tensor_tensor(x_back[b.parity][:, :, :], x_back[b.parity][:, :, :], rows[:, :, :], ALU.add).then_inc(b_dve.step("x1"), 1)

            def st1_task(b, k, use):
                dve.wait_ge(b_dve.sem, b_dve.done(b, "x1"))
                stats(b_dve, x_back[b.parity], st_1, "s1")

            def ag1_task(b, k, use):
                aggregate(b_dve, b, st_1, mv_1, "s1", "a1")

            def cum_task(b, t, use):
                dve.wait_ge(b_act.sem, b_act.done(b, f"xnT{t}"))
                dve.tensor_tensor_scan(cumT[:, t, :], one[:, 0:1].broadcast_to([P, T]), use.bank[:, :], 0.0,
                                       ALU.mult, ALU.add).then_inc(b_dve.step(f"cum{t}"), 1)

            flat_l = logits[:, :, :, :].rearrange("p a b k -> p (a b) k")

            def lb_task(b, k, use):
                dve.wait_ge(b_pe.sem, b_pe.done(b, "lt"))
                dve.tensor_tensor(flat_l, use.bank[:, 0:TB * 2 * KE].rearrange("p (a k) -> p a k", k=KE),
                                  logit_bias[:, :, :, :].rearrange("p a b k -> p (a b) k"), ALU.add).then_inc(b_dve.step("lb"), 1)

            def mx_task(b, k, use):
                dve.wait_ge(b_dve.sem, b_dve.done(b, "lb"))
                dve.tensor_reduce(top[:, :], flat_l, AX.X, ALU.max).then_inc(b_dve.step("mx"), 1)

            def sub_task(b, k, use):
                dve.wait_ge(b_dve.sem, b_dve.done(b, "mx"))
                dve.tensor_tensor(flat_l, flat_l, top[:, :].rearrange("p (a o) -> p a o", o=1).broadcast_to([P, TB * 2, KE]),
                                  ALU.subtract).then_inc(b_dve.step("sub"), 1)

            def sm_task(b, k, use):
                dve.wait_ge(b_act.sem, b_act.done(b, "ex"))
                dve.tensor_reduce(total[:, :], flat_l, AX.X, ALU.add).then_inc(b_dve.step("sm"), 1)

            def sn_task(b, k, use):
                dve.wait_ge(b_dve.sem, b_dve.done(b, "sm"))
                dve.tensor_tensor(total[:, :], total[:, :], n_valid[:, :, :].rearrange("p a b -> p (a b)"), ALU.mult).then_inc(b_dve.step("sn"), 1)

            def rc_task(b, k, use):
                dve.wait_ge(b_dve.sem, b_dve.done(b, "sn"))
                dve.reciprocal(total[:, :], total[:, :]).then_inc(b_dve.step("rc"), 1)

            def wa_task(b, k, use):
                dve.wait_ge(b_dve.sem, b_dve.done(b, "rc"))
                if b.shift(-1).exists:
                    dve.wait_ge(l_act.sem, l_act.done(b.shift(-1), "cum7"))
                dve.tensor_tensor(gate[:, :, :].rearrange("p a (b k) -> p (a b) k", k=KE), flat_l,
                                  total[:, :].rearrange("p (a o) -> p a o", o=1).broadcast_to([P, TB * 2, KE]), ALU.mult).then_inc(b_dve.step("wa"), 1)

            def pr_task(b, u, use):
                dve.wait_ge(l_act.sem, l_act.done(b, f"cum{u}"))
                dve.wait_ge(l_pe.sem, l_pe.done(b, f"xv{u}"))
                assert u < 2 or l_pe.index[f"xv{u}"] > l_pe.index[f"pt{u - 2}"]
                dve.tensor_tensor(prod[u % 2][:, :], use.bank[:, :], cum_sb[u % 2][:, :], ALU.mult).then_inc(l_dve.step(f"pr{u}"), 1)

            def out_stats(b, k, use):
                dve.wait_ge(l_act.sem, l_act.done(b, "out3"))
                stats(l_dve, o_rows, st_o, "st")

            def out_aggregate(b, k, use):
                aggregate(l_dve, b, st_o, mv_o, "st", "ag")

            def scan_part(q, slot, beat):
                k = beat // 2
                if beat % 2 == 0:
                    if not q.exists:
                        return
                    n, c = slot, k
                    if q.turn is None and q.const == 0 and n == 0 and c == 0:
                        dve.wait_ge(w_act, len(jobs))
                    dve.wait_ge(s_exp.sem, s_exp.done(q, f"{n},{c}"))
                    if c % 2 == 0:
                        dve.wait_ge(s_bx.sem, s_bx.done(q, f"{n},{c // 2}"))
                    if c == 0:
                        free = q if n >= 2 else q.shift(-1)
                        if free.exists:
                            dve.wait_ge(s_tr.sem, s_tr.done(free, f"{(n - 2) % NS},{TB - 1}"))
                    dve.tensor_tensor_scan(h[n % 2][:, c, :], decay[c % 2][:, :], bx[(2 * n + c // 2) % BX_RING][:, c % 2, :], 0.0,
                                           ALU.mult, ALU.add).then_inc(s_scan.step(f"{n},{c}"), 1)
                    return
                batch, n = (q, slot - 1) if slot else (q.shift(-1), NS - 1)
                if not batch.exists:
                    return
                dve.wait_ge(s_tr.sem, s_tr.done(batch, f"{n},{k}"))
                if n == 0:
                    if k == 0:
                        dve.wait_ge(f_act.sem, f_act.done(batch, "Ct"))
                        if batch.shift(-1).exists:
                            dve.wait_ge(b_pe.sem, b_pe.done(batch.shift(-1), "y3"))
                    ins = dve.tensor_scalar(yT[:, k, :], stateT[k % 2][:, :], C_tok[batch.parity][:, k, n:n + 1], None, ALU.mult)
                else:
                    dve.wait_ge(s_acc.sem, s_acc.done(batch, f"{n - 1},{k}"))
                    ins = dve.scalar_tensor_tensor(out=yT[:, k, :], in0=stateT[k % 2][:, :], scalar=C_tok[batch.parity][:, k, n:n + 1],
                                                   in1=yT[:, k, :], op0=ALU.mult, op1=ALU.add)
                ins.then_inc(s_acc.step(f"{n},{k}"), 1)

            walk(dve, "dve", prologue,
                 {("F", "st"): front_stats, ("F", "ag"): front_aggregate, ("F", "cvA"): tap(1, "cvA", (f_act, "cv")),
                  ("F", "cvB"): tap(2, "cvB", (f_dve, "cvA")), ("F", "cvC"): tap(3, "cvC", (f_dve, "cvB")), ("F", "d1"): d1_task,
                  ("B", "keep"): keep_task, ("B", "u"): u_task, ("B", "o"): o_task, ("B", "r"): r_task, ("B", "st"): st_task, ("B", "ag"): ag_task,
                  ("B", "x1"): x1_task, ("B", "st1"): st1_task, ("B", "ag1"): ag1_task, ("B", "cum"): cum_task, ("B", "lb"): lb_task, ("B", "mx"): mx_task,
                  ("B", "sub"): sub_task, ("B", "sm"): sm_task, ("B", "sn"): sn_task, ("B", "rc"): rc_task, ("B", "wa"): wa_task,
                  ("L", "pr"): pr_task, ("L", "st"): out_stats, ("L", "ag"): out_aggregate}, scan_part)


INPUTS = ["L0_attn_x", "L0_attn_norm_scale", "L0_attn_w_in", "L0_attn_conv_w", "L0_attn_conv_b", "L0_attn_A_log", "L0_attn_D",
          "L0_attn_w_xproj", "L0_attn_w_dt", "L0_attn_b_dt", "L0_attn_w_out", "L0_ffn_W_Q", "L0_ffn_W_K", "L0_ffn_W_O",
          "L0_ffn_W_inv", "L0_ffn_V_fwd", "L0_ffn_W_fwd", "L0_ffn_U_fwd", "L0_ffn_b_fwd", "L0_ffn_V_inv", "L0_ffn_W_inv_exp",
          "L0_ffn_U_inv", "L0_ffn_b_inv", "L0_ffn_router_w1", "L0_ffn_router_b1", "L0_ffn_router_w2", "L0_ffn_router_b2",
          "L0_ffn_alpha_bi", "L0_ffn_expert_bias"]


def kernel(**inputs):
    import numpy as np
    import concourse.bacc as bacc
    from concourse.bass_utils import run_bass_kernel_spmd

    nc = bacc.Bacc("TRN2", target_bir_lowering=False, num_devices=1)
    arrays, args = {}, []
    for name in INPUTS:
        a = np.ascontiguousarray(inputs[name])
        if a.ndim == 0:
            a = a.reshape(1)
        arrays[f"in_{name}"] = a
        args.append(nc.dram_tensor(f"in_{name}", a.shape, mybir.dt.from_np(a.dtype), kind="ExternalInput").ap())
    args.append(nc.dram_tensor("out_0", (NB, T, D), FP32, kind="ExternalOutput").ap())
    program(nc, *args)
    result = run_bass_kernel_spmd(nc, [arrays], core_ids=[0])
    return result.results[0]["out_0"]
```
